# Optimizing a Trainium2 kernel written in Bass

```python
import numpy as np
import jax
import jax.numpy as jnp

def _softmax(x, axis=-1):
    return jax.nn.softmax(x, axis=axis)

def _gelu(x):
    return jax.nn.gelu(x, approximate=True)

def _silu(x):
    return jax.nn.silu(x)

def _sigmoid(x):
    return jax.nn.sigmoid(x)

def _layernorm(x, axis=-1, eps=1e-05):
    m = jnp.mean(x, axis=axis, keepdims=True)
    v = jnp.var(x, axis=axis, keepdims=True)
    return (x - m) / jnp.sqrt(v + eps)

def _scatter_add(tgt, idx, src, axis=0):
    return tgt.at[idx].add(src)

def _segment_sum(src, seg, n):
    return jax.ops.segment_sum(src, seg, n)
kernel_name = 'mk_xattn_ffn_d2_seqx_r4_9eacf6'

def setup_inputs(seed: int=0):
    np.random.seed(seed)
    _w = jnp.asarray

    def _rec_inputs():
        import jax
        import jax.numpy as jnp
        _rk = jax.random.key(seed)
        x = 7.22e-05 + 1 * jax.random.normal(jax.random.fold_in(_rk, 1), (8, 100, 256), jnp.float32)
        _lenS = 100 - jax.random.randint(jax.random.fold_in(_rk, 7), (8,), 0, max(1, 100 // 4) + 1, jnp.int32)
        _lenS2 = 361 - jax.random.randint(jax.random.fold_in(_rk, 8), (8,), 0, max(1, 361 // 4) + 1, jnp.int32)
        _ctx_768P = jax.random.normal(jax.random.fold_in(_rk, 11), (8, 16, 192), jnp.float32)
        _ctx_768c = jax.random.dirichlet(jax.random.fold_in(_rk, 511), 0.3 * jnp.ones((16,), jnp.float32), (8, 361))
        _ctx_768t = jnp.einsum('bsk,bkd->bsd', _ctx_768c, _ctx_768P)
        _ctx_768t = _ctx_768t * jax.lax.rsqrt(jnp.mean(jnp.square(_ctx_768t)) + 1e-12) * 0.953939
        ctx_768 = -0.000191848 + 0.999787 * (_ctx_768t + 0.3 * jax.random.normal(jax.random.fold_in(_rk, 611), (8, 361, 192), jnp.float32))
        _validS = jnp.arange(100)[None, :] < _lenS[:, None]
        _validS2 = jnp.arange(361)[None, :] < _lenS2[:, None]
        _causal = jnp.tril(jnp.ones((100, 100), dtype=bool))
        mask_BxS2_bf1 = jnp.ones((8, 361), dtype=bool)
        return (x, ctx_768, mask_BxS2_bf1)
    x, ctx_768, mask_BxS2_bf1 = _rec_inputs()

    def _L0_xattn_setup():
        import jax, jax.numpy as jnp
        import numpy as np
        NUM_HEADS = 16
        CLAMP = 10000.0
        key = jax.random.key(seed)
        ks = jax.random.split(key, 8)
        B, Nq, Nkv, Cq, Ckv = (4, 512, 512, 256, 192)
        s_q = 1.0 / np.sqrt(Cq)
        s_kv = 1.0 / np.sqrt(Ckv)
        return {'query': jax.random.normal(ks[0], (B, Nq, Cq), jnp.float32), 'key_value': jax.random.normal(ks[1], (B, Nkv, Ckv), jnp.float32), 'Wq': jax.random.normal(ks[2], (Cq, Cq), jnp.float32) * s_q, 'bq': jnp.zeros((Cq,), jnp.float32), 'Wk': jax.random.normal(ks[3], (Ckv, Cq), jnp.float32) * s_kv, 'bk': jnp.zeros((Cq,), jnp.float32), 'Wv': jax.random.normal(ks[4], (Ckv, Cq), jnp.float32) * s_kv, 'bv': jnp.zeros((Cq,), jnp.float32), 'Wo': jax.random.normal(ks[5], (Cq, Cq), jnp.float32) * s_q, 'bo': jnp.zeros((Cq,), jnp.float32)}
    _L0_xattn_all = _L0_xattn_setup()
    _L0_xattn_in = {k: v for k, v in _L0_xattn_all.items() if k in ('Wq', 'bq', 'Wk', 'bk', 'Wv', 'bv', 'Wo', 'bo')}
    del _L0_xattn_all

    def _L0_ffn_setup():
        import jax, jax.numpy as jnp
        import numpy as np
        D_MODEL = 256
        D_HIDDEN = 1024
        NUM_EXPERTS = 8
        B, T = (2, 512)
        key = jax.random.key(seed)
        ks = jax.random.split(key, 8)
        s = 0.02
        x = jax.random.normal(ks[0], (B, T, D_MODEL), dtype=jnp.float32)
        Wg = jax.random.normal(ks[1], (D_MODEL, NUM_EXPERTS), dtype=jnp.float32) * s
        bg = jnp.zeros((NUM_EXPERTS,), dtype=jnp.float32)
        W1 = jax.random.normal(ks[2], (NUM_EXPERTS, D_MODEL, D_HIDDEN), dtype=jnp.float32) * s
        b1 = jnp.zeros((NUM_EXPERTS, D_HIDDEN), dtype=jnp.float32)
        W2 = jax.random.normal(ks[3], (NUM_EXPERTS, D_HIDDEN, D_MODEL), dtype=jnp.float32) * s
        b2 = jnp.zeros((NUM_EXPERTS, D_MODEL), dtype=jnp.float32)
        return {'x': x, 'Wg': Wg, 'bg': bg, 'W1': W1, 'b1': b1, 'W2': W2, 'b2': b2}
    _L0_ffn_all = _L0_ffn_setup()
    _L0_ffn_in = {k: v for k, v in _L0_ffn_all.items() if k in ('Wg', 'bg', 'W1', 'b1', 'W2', 'b2')}
    del _L0_ffn_all

    def _L1_xattn_setup():
        import jax, jax.numpy as jnp
        import numpy as np
        DIM = 256
        CTX_DIM = 192
        HEADS = 8
        DIM_HEAD = 64
        INNER = HEADS * DIM_HEAD
        SCALE = 8.0
        EPS = 1e-05

        def stable_layernorm(x, g):
            x = x / jax.lax.stop_gradient(jnp.max(x, axis=-1, keepdims=True))
            mean = jnp.mean(x, axis=-1, keepdims=True)
            var = jnp.var(x, axis=-1, keepdims=True)
            return (x - mean) * jax.lax.rsqrt(var + EPS) * g

        def l2norm(t):
            n = jnp.sqrt(jnp.sum(t * t, axis=-1, keepdims=True))
            return t / jnp.maximum(n, 1e-12)
        key = jax.random.key(seed)
        ks = jax.random.split(key, 10)
        b, n, m = (4, 512, 256)
        inp = {'x': jax.random.normal(ks[0], (b, n, DIM), jnp.float32), 'context': jax.random.normal(ks[1], (b, m, CTX_DIM), jnp.float32), 'mask': jnp.ones((b, m), dtype=bool), 'g_norm': jnp.ones((DIM,), jnp.float32), 'Wq': jax.random.normal(ks[2], (DIM, INNER), jnp.float32) * DIM ** (-0.5), 'Wkv': jax.random.normal(ks[3], (CTX_DIM, 2 * INNER), jnp.float32) * CTX_DIM ** (-0.5), 'null_kv': jax.random.normal(ks[4], (2, DIM_HEAD), jnp.float32), 'q_scale': jnp.ones((DIM_HEAD,), jnp.float32), 'k_scale': jnp.ones((DIM_HEAD,), jnp.float32), 'Wo': jax.random.normal(ks[5], (INNER, DIM), jnp.float32) * INNER ** (-0.5), 'g_out': jnp.ones((DIM,), jnp.float32)}
        return inp
    _L1_xattn_all = _L1_xattn_setup()
    _L1_xattn_in = {k: v for k, v in _L1_xattn_all.items() if k in ('g_norm', 'Wq', 'Wkv', 'null_kv', 'q_scale', 'k_scale', 'Wo', 'g_out')}
    del _L1_xattn_all

    def _L1_ffn_setup():
        import jax, jax.numpy as jnp
        import numpy as np
        H = 256
        I = 128
        E = 64
        G = 8
        TOPK_GROUP = 4
        K = 8
        I_SH = 256
        SCALE = 2.5

        def _route(x, router_w, e_bias):
            T = x.shape[0]
            scores = jax.nn.sigmoid(x.astype(jnp.float32) @ router_w.T.astype(jnp.float32))
            sfc = jax.lax.stop_gradient(scores) + e_bias[None, :]
            group_scores = jax.lax.top_k(sfc.reshape(T, G, E // G), 2)[0].sum(-1)
            _, gidx = jax.lax.top_k(group_scores, TOPK_GROUP)
            gmask = jax.nn.one_hot(gidx, G, dtype=sfc.dtype).sum(1)
            smask = jnp.repeat(gmask, E // G, axis=1)
            masked = jnp.where(smask > 0, sfc, 0.0)
            _, topk_idx = jax.lax.top_k(masked, K)
            w = jnp.take_along_axis(scores, topk_idx, axis=1)
            w = w / (w.sum(-1, keepdims=True) + 1e-20)
            return (topk_idx, w * SCALE)
        key = jax.random.key(seed)
        ks = jax.random.split(key, 9)
        s = 0.02
        return {'hidden_states': jax.random.normal(ks[0], (2, 256, H), jnp.float32), 'router_w': jax.random.normal(ks[1], (E, H), jnp.float32) * s, 'e_bias': jnp.zeros((E,), jnp.float32), 'Wg': jax.random.normal(ks[2], (E, H, I), jnp.float32) * s, 'Wu': jax.random.normal(ks[3], (E, H, I), jnp.float32) * s, 'Wd': jax.random.normal(ks[4], (E, I, H), jnp.float32) * s, 'SWg': jax.random.normal(ks[5], (H, I_SH), jnp.float32) * s, 'SWu': jax.random.normal(ks[6], (H, I_SH), jnp.float32) * s, 'SWd': jax.random.normal(ks[7], (I_SH, H), jnp.float32) * s}
    _L1_ffn_all = _L1_ffn_setup()
    _L1_ffn_in = {k: v for k, v in _L1_ffn_all.items() if k in ('router_w', 'e_bias', 'Wg', 'Wu', 'Wd', 'SWg', 'SWu', 'SWd')}
    del _L1_ffn_all
    return {'x': x, 'ctx_768': ctx_768, 'mask_BxS2_bf1': mask_BxS2_bf1, 'L0_xattn_Wq': _L0_xattn_in['Wq'], 'L0_xattn_bq': _L0_xattn_in['bq'], 'L0_xattn_Wk': _L0_xattn_in['Wk'], 'L0_xattn_bk': _L0_xattn_in['bk'], 'L0_xattn_Wv': _L0_xattn_in['Wv'], 'L0_xattn_bv': _L0_xattn_in['bv'], 'L0_xattn_Wo': _L0_xattn_in['Wo'], 'L0_xattn_bo': _L0_xattn_in['bo'], 'L0_ffn_Wg': _L0_ffn_in['Wg'], 'L0_ffn_bg': _L0_ffn_in['bg'], 'L0_ffn_W1': _L0_ffn_in['W1'], 'L0_ffn_b1': _L0_ffn_in['b1'], 'L0_ffn_W2': _L0_ffn_in['W2'], 'L0_ffn_b2': _L0_ffn_in['b2'], 'L1_xattn_g_norm': _L1_xattn_in['g_norm'], 'L1_xattn_Wq': _L1_xattn_in['Wq'], 'L1_xattn_Wkv': _L1_xattn_in['Wkv'], 'L1_xattn_null_kv': _L1_xattn_in['null_kv'], 'L1_xattn_q_scale': _L1_xattn_in['q_scale'], 'L1_xattn_k_scale': _L1_xattn_in['k_scale'], 'L1_xattn_Wo': _L1_xattn_in['Wo'], 'L1_xattn_g_out': _L1_xattn_in['g_out'], 'L1_ffn_router_w': _L1_ffn_in['router_w'], 'L1_ffn_e_bias': _L1_ffn_in['e_bias'], 'L1_ffn_Wg': _L1_ffn_in['Wg'], 'L1_ffn_Wu': _L1_ffn_in['Wu'], 'L1_ffn_Wd': _L1_ffn_in['Wd'], 'L1_ffn_SWg': _L1_ffn_in['SWg'], 'L1_ffn_SWu': _L1_ffn_in['SWu'], 'L1_ffn_SWd': _L1_ffn_in['SWd']}

def reference(x, ctx_768, mask_BxS2_bf1, L0_xattn_Wq, L0_xattn_bq, L0_xattn_Wk, L0_xattn_bk, L0_xattn_Wv, L0_xattn_bv, L0_xattn_Wo, L0_xattn_bo, L0_ffn_Wg, L0_ffn_bg, L0_ffn_W1, L0_ffn_b1, L0_ffn_W2, L0_ffn_b2, L1_xattn_g_norm, L1_xattn_Wq, L1_xattn_Wkv, L1_xattn_null_kv, L1_xattn_q_scale, L1_xattn_k_scale, L1_xattn_Wo, L1_xattn_g_out, L1_ffn_router_w, L1_ffn_e_bias, L1_ffn_Wg, L1_ffn_Wu, L1_ffn_Wd, L1_ffn_SWg, L1_ffn_SWu, L1_ffn_SWd):
    import jax
    import jax.numpy as jnp

    def _L0_xattn_ref(query, key_value, Wq, bq, Wk, bk, Wv, bv, Wo, bo):
        import jax, jax.numpy as jnp
        import numpy as np
        NUM_HEADS = 16
        CLAMP = 10000.0
        B, Nq, Cq = query.shape
        Nkv = key_value.shape[1]
        H = NUM_HEADS
        D = Cq // H
        scale = D ** (-0.5)
        q = (query @ Wq + bq).reshape(B, Nq, H, D).transpose(0, 2, 1, 3)
        k = (key_value @ Wk + bk).reshape(B, Nkv, H, D).transpose(0, 2, 1, 3)
        v = (key_value @ Wv + bv).reshape(B, Nkv, H, D).transpose(0, 2, 1, 3)
        attn = jnp.einsum('bhqd,bhkd->bhqk', q, k) * scale
        attn = jnp.clip(attn, -CLAMP, CLAMP)
        attn = jax.nn.softmax(attn, axis=-1)
        attn = jnp.where(jnp.any(jnp.isnan(attn)), jnp.asarray(1.0 / Nkv, attn.dtype), attn)
        x = jnp.einsum('bhqk,bhkd->bqhd', attn, v).reshape(B, Nq, Cq)
        return x @ Wo + bo

    def _L0_ffn_ref(x, Wg, bg, W1, b1, W2, b2):
        import jax, jax.numpy as jnp
        import numpy as np
        D_MODEL = 256
        D_HIDDEN = 1024
        NUM_EXPERTS = 8
        B, T = (2, 512)
        gate_logits = jnp.einsum('btd,de->bte', x, Wg) + bg
        gate_scores = jax.nn.softmax(gate_logits, axis=-1)
        top1_idx = jnp.argmax(gate_scores, axis=-1)
        top1_mask = jax.nn.one_hot(top1_idx, NUM_EXPERTS, dtype=x.dtype)
        top1_weight = jnp.sum(gate_scores * top1_mask, axis=-1, keepdims=True)
        h = jax.nn.silu(jnp.einsum('btd,edh->bteh', x, W1) + b1)
        o = jnp.einsum('bteh,ehd->bted', h, W2) + b2
        y = jnp.sum(o * top1_mask[..., None], axis=2) * top1_weight
        return y

    def _L1_xattn_ref(x, context, mask, g_norm, Wq, Wkv, null_kv, q_scale, k_scale, Wo, g_out):
        import jax, jax.numpy as jnp
        import numpy as np
        DIM = 256
        CTX_DIM = 192
        HEADS = 8
        DIM_HEAD = 64
        INNER = HEADS * DIM_HEAD
        SCALE = 8.0
        EPS = 1e-05

        def stable_layernorm(x, g):
            x = x / jax.lax.stop_gradient(jnp.max(x, axis=-1, keepdims=True))
            mean = jnp.mean(x, axis=-1, keepdims=True)
            var = jnp.var(x, axis=-1, keepdims=True)
            return (x - mean) * jax.lax.rsqrt(var + EPS) * g

        def l2norm(t):
            n = jnp.sqrt(jnp.sum(t * t, axis=-1, keepdims=True))
            return t / jnp.maximum(n, 1e-12)
        b, n, _ = x.shape
        x = stable_layernorm(x, g_norm)
        q = jnp.einsum('bnd,de->bne', x, Wq)
        kv = jnp.einsum('bmd,de->bme', context, Wkv)
        k, v = jnp.split(kv, 2, axis=-1)

        def split_heads(t):
            return t.reshape(t.shape[0], t.shape[1], HEADS, DIM_HEAD).transpose(0, 2, 1, 3)
        q, k, v = map(split_heads, (q, k, v))
        nk = jnp.broadcast_to(null_kv[0], (b, HEADS, 1, DIM_HEAD))
        nv = jnp.broadcast_to(null_kv[1], (b, HEADS, 1, DIM_HEAD))
        k = jnp.concatenate([nk, k], axis=2)
        v = jnp.concatenate([nv, v], axis=2)
        q = l2norm(q) * q_scale
        k = l2norm(k) * k_scale
        sim = jnp.einsum('bhid,bhjd->bhij', q, k) * SCALE
        max_neg = -jnp.finfo(sim.dtype).max
        m = jnp.pad(mask, ((0, 0), (1, 0)), constant_values=True)[:, None, None, :]
        sim = jnp.where(m, sim, max_neg)
        attn = jax.nn.softmax(sim.astype(jnp.float32), axis=-1).astype(sim.dtype)
        out = jnp.einsum('bhij,bhjd->bhid', attn, v)
        out = out.transpose(0, 2, 1, 3).reshape(b, n, INNER)
        out = jnp.einsum('bne,ed->bnd', out, Wo)
        return stable_layernorm(out, g_out)

    def _L1_ffn_ref(hidden_states, router_w, e_bias, Wg, Wu, Wd, SWg, SWu, SWd):
        import jax, jax.numpy as jnp
        import numpy as np
        H = 256
        I = 128
        E = 64
        G = 8
        TOPK_GROUP = 4
        K = 8
        I_SH = 256
        SCALE = 2.5

        def _route(x, router_w, e_bias):
            T = x.shape[0]
            scores = jax.nn.sigmoid(x.astype(jnp.float32) @ router_w.T.astype(jnp.float32))
            sfc = jax.lax.stop_gradient(scores) + e_bias[None, :]
            group_scores = jax.lax.top_k(sfc.reshape(T, G, E // G), 2)[0].sum(-1)
            _, gidx = jax.lax.top_k(group_scores, TOPK_GROUP)
            gmask = jax.nn.one_hot(gidx, G, dtype=sfc.dtype).sum(1)
            smask = jnp.repeat(gmask, E // G, axis=1)
            masked = jnp.where(smask > 0, sfc, 0.0)
            _, topk_idx = jax.lax.top_k(masked, K)
            w = jnp.take_along_axis(scores, topk_idx, axis=1)
            w = w / (w.sum(-1, keepdims=True) + 1e-20)
            return (topk_idx, w * SCALE)
        orig_shape = hidden_states.shape
        x = hidden_states.reshape(-1, orig_shape[-1])
        T = x.shape[0]
        topk_idx, topk_w = _route(x, router_w, e_bias)
        coef = jnp.zeros((T, E), topk_w.dtype).at[jnp.arange(T)[:, None], topk_idx].add(topk_w)
        g = jnp.einsum('th,ehi->tei', x, Wg)
        u = jnp.einsum('th,ehi->tei', x, Wu)
        h = jax.nn.silu(g) * u * coef[:, :, None]
        moe_out = jnp.einsum('tei,eih->th', h, Wd)
        shared = jax.nn.silu(x @ SWg) * (x @ SWu) @ SWd
        return (moe_out + shared).reshape(orig_shape)
    x = x + _L0_xattn_ref(_layernorm(x, axis=-1), ctx_768, L0_xattn_Wq, L0_xattn_bq, L0_xattn_Wk, L0_xattn_bk, L0_xattn_Wv, L0_xattn_bv, L0_xattn_Wo, L0_xattn_bo)
    x = x + _L0_ffn_ref(_layernorm(x, axis=-1), L0_ffn_Wg, L0_ffn_bg, L0_ffn_W1, L0_ffn_b1, L0_ffn_W2, L0_ffn_b2)
    x = x + _L1_xattn_ref(_layernorm(x, axis=-1), ctx_768, mask_BxS2_bf1, L1_xattn_g_norm, L1_xattn_Wq, L1_xattn_Wkv, L1_xattn_null_kv, L1_xattn_q_scale, L1_xattn_k_scale, L1_xattn_Wo, L1_xattn_g_out)
    x = x + _L1_ffn_ref(_layernorm(x, axis=-1), L1_ffn_router_w, L1_ffn_e_bias, L1_ffn_Wg, L1_ffn_Wu, L1_ffn_Wd, L1_ffn_SWg, L1_ffn_SWu, L1_ffn_SWd)
    return x

_drawn_inputs = setup_inputs


def setup_inputs(seed=0):
    import zlib

    import numpy as np

    out = dict(_drawn_inputs(seed))
    spreads = {'L0_xattn_bq': (0.0, 0.512),
     'L0_xattn_bk': (0.0, 0.8),
     'L0_xattn_bv': (0.0, 0.1),
     'L0_xattn_bo': (0.0, 0.1),
     'L0_ffn_bg': (0.0, 0.673),
     'L0_ffn_b1': (0.0, 0.8),
     'L0_ffn_b2': (0.0, 0.564),
     'L1_xattn_g_norm': (1.0, 0.2),
     'L1_xattn_q_scale': (1.0, 0.2),
     'L1_xattn_k_scale': (1.0, 0.2),
     'L1_xattn_g_out': (1.0, 0.2),
     'L1_ffn_e_bias': (0.0, 0.8)}
    factors = {'L0_ffn_Wg': 2.92,
     'L0_ffn_W1': 3.902,
     'L0_ffn_W2': 3.679,
     'L1_xattn_null_kv': 6.309,
     'L1_ffn_router_w': 8.0,
     'L1_ffn_Wg': 8.0,
     'L1_ffn_Wu': 8.0,
     'L1_ffn_Wd': 8.0,
     'L1_ffn_SWg': 5.215,
     'L1_ffn_SWu': 5.115,
     'L1_ffn_SWd': 5.061}
    for name, (base, spread) in spreads.items():
        noise = np.random.default_rng([zlib.crc32(name.encode()), seed]).standard_normal(out[name].shape)
        drawn = base * np.exp(spread * noise) if base else spread * noise
        out[name] = jnp.asarray(drawn.astype(out[name].dtype))
    for name, factor in factors.items():
        out[name] = (out[name] * factor).astype(out[name].dtype)
    return out
```

```python
import numpy as np
import concourse.bass as bass
from concourse import mybir

F32 = mybir.dt.float32
F32R = mybir.dt.float32r
I32 = mybir.dt.int32
U32 = mybir.dt.uint32
U8 = mybir.dt.uint8
ACT = mybir.ActivationFunctionType
ALU = mybir.AluOpType
AX = mybir.AxisListType

P = 128
B, NQ, D = 8, 100, 256
NKV, DC = 361, 192
DCC = DC // 2
FULL, TAIL = 2, NKV - 2 * P
EPS = 1e-5
CLAMP = 10000.0
SCALE0 = 16 ** -0.5
LOOK = 3
AHEAD = 2
NPB = 4
SLOT_V = 3 * 512


def build(nc, a):
    sb = nc.alloc_sbuf_tensor
    sem = nc.alloc_semaphore

    psum = nc.alloc_psum_tensor("psum", [P, 8, 512], F32)
    x = sb("x", [NQ, B + 1, D], F32)
    ident = sb("ident", [P, P], F32)
    ones_row = sb("ones_row", [1, P], F32)
    eps_col = sb("eps_col", [P, 1], F32)
    stats = sb("stats", [NQ, B + 1, 6], F32)
    mv = sb("mv", [NQ, B, 2], F32)
    rstd = sb("rstd", [NQ, B], F32)
    std = sb("std", [NQ, B], F32)
    keys_at = nc.sbuf_base
    kT_all = sb("kT_all", [P, 4 * (B + 1) * (NKV + 1)], F32)
    vals_at = nc.sbuf_base
    v_all = sb("v_all", [P, B, 3, 512], F32)
    qT_all = sb("qT_all", [P, 4 * (B + 1) * NQ], F32)
    qm = [sb(f"qm{p}", [P, 16, NQ], F32) for p in range(2)]
    vs = [sb(f"vs{p}", [P, 3, 512], F32) for p in range(2)]
    probs = sb("probs", [NQ, NPB, 2, NKV + 1], F32)
    negmax = sb("negmax", [NQ, NPB, 2], F32)
    sums = sb("sums", [NQ, 2, 16], F32)
    inv_sums = sb("inv_sums", [NQ, 16], F32)
    probsT = [sb(f"probsT{p}", [P, 3, 2 * NQ], F32) for p in range(2)]
    oT = sb("oT", [P, 4, NQ], F32)
    o_tok = sb("o_tok", [NQ, 512], F32)
    o_tokT = sb("o_tokT", [P, 4, NQ], F32)

    ctx_nat = [sb(f"ctx_nat{p}", [P, 3, DC], F32) for p in range(2)]
    ctxT = sb("ctxT", [DCC + 1, 2, NKV], F32)
    xn = sb("xn", [NQ, D], F32)
    xnT = sb("xnT", [P, 2, NQ], F32)

    headmask = sb("headmask", [P, 8], F32)
    early = sb("early", [P, (B + 1) * D], F32)
    wq0, wk0, wv0, wo0 = (early[:, k * 2 * D:(k + 1) * 2 * D].rearrange("p (c n) -> p c n", c=2) for k in range(4))
    wk0 = wk0[0:DCC]
    wv0 = wv0[0:DCC + 1]
    z_all = early[0:NQ, :].rearrange("q (b d) -> q b d", d=D)
    bq0 = sb("bq0", [P, 2], F32)
    bq0s = sb("bq0s", [P, 2], F32)
    bk0 = sb("bk0", [P, 2], F32)
    bo0 = sb("bo0", [1, D], F32)

    E0, H0 = 8, 1024
    HC = H0 // P
    NBLK = (B * NQ + E0 * (P - 1)) // P
    keys_arena = kT_all[:, :]
    vals_arena = v_all[:, :, :, :].rearrange("p b t n -> p (b t n)")

    def carve(arena, at, shape):
        n = int(np.prod(shape))
        view = arena[:, at[0]:at[0] + n]
        at[0] += n
        names = " ".join("abc"[:len(shape)])
        return view.rearrange(f"p ({names}) -> p {names}", **{k: v for k, v in zip("abc", shape)})

    def carve_r(name, base, at, shape):
        n = int(np.prod(shape))
        view = nc.alloc_sbuf_tensor_at(name, [P, n], F32R, offset=base + 4 * at[0])[:, :]
        at[0] += n
        names = " ".join("abc"[:len(shape)])
        return view.rearrange(f"p ({names}) -> p {names}", **{k: v for k, v in zip("abc", shape)})
    at_k, at_v = [0], [0]
    w1_e = [carve(vals_arena, at_v, (2, H0)) for _ in range(2)]
    w2_e = [carve(vals_arena, at_v, (HC, D)) for _ in range(2)]
    xn_all = carve(keys_arena, at_k, (B, D))[0:NQ]
    y_tok = carve(keys_arena, at_k, (B, D))[0:NQ]
    xs_rows = [carve(keys_arena, at_k, (D,)) for _ in range(2)]
    xsT = [carve(keys_arena, at_k, (2, P)) for _ in range(2)]
    hT = [carve(keys_arena, at_k, (HC, P)) for _ in range(2)]
    ys_rows = [carve(keys_arena, at_k, (D,)) for _ in range(2)]
    b1_rows = [sb(f"b1_rows{p}", [HC, P], F32) for p in range(2)]
    b1_col = [sb(f"b1_col{p}", [P, HC], F32) for p in range(2)]
    b2_row = [sb(f"b2_row{p}", [1, D], F32) for p in range(2)]
    wg0 = sb("wg0", [P, 2, E0], F32)
    bg0 = sb("bg0", [1, E0], F32)
    earlier = sb("earlier", [NQ, NQ], F32)
    ones_sq = sb("ones_sq", [NQ, P], F32)
    below8 = sb("below8", [P, 8, 8], F32)
    iota16 = sb("iota16", [P, 16], F32)
    logits = sb("logits", [NQ, B, E0], F32)
    top_logit = sb("top_logit", [NQ, B], F32)
    top_weight = sb("top_weight", [NQ, B], F32)
    choice = sb("choice", [NQ, B, E0], F32)
    route_a = sb("route_a", [P, B * E0 * 8], F32)
    route_b = sb("route_b", [P, B, E0], F32)
    counts = sb("counts", [P, B, E0], F32)
    per_expert = sb("per_expert", [P, 4, E0], F32)
    block_expert = sb("block_expert", [P, NBLK], F32)
    block_expert_i = sb("block_expert_i", [P, NBLK], I32)
    slot_f = sb("slot_f", [NQ, B], F32)
    slot = sb("slot", [NQ, B], U32)
    zeros = sb("zeros", [P, D], F32)
    xs_dram = nc.dram_tensor("xs_dram", [NBLK * P, D], F32, kind="Internal").ap()
    ys_dram = nc.dram_tensor("ys_dram", [NBLK * P, D], F32, kind="Internal").ap()

    HD1, SCALE1 = 64, 8.0
    FLT_MAX = float(np.finfo(np.float32).max)
    flat = lambda t: t[:, :, :].rearrange("p a b -> p (a b)")
    two = lambda v: v[:, 0:1024].rearrange("p (c n) -> p c n", c=2)
    wk1, wv1 = (two(flat(vs[p]))[0:DCC] for p in range(2))
    wq1 = two(flat(qm[0]))
    k_tok = flat(qm[1])[:, 0:3 * 512].rearrange("p (t n) -> p t n", t=3)
    y_all = probs[:, :, :, :].rearrange("q a b n -> q (a b n)")[:, 0:B * D].rearrange("q (b d) -> q b d", b=B)
    mask_bias = [flat(ctx_nat[p])[0:NQ, 0:NKV + 1] for p in range(2)]
    wo1 = sb("wo1", [P, 4, D], F32)
    g_norm = sb("g_norm", [NQ, D], F32)
    g_out = sb("g_out", [NQ, D], F32)
    turn = sb("turn", [NQ, NPB], F32)
    flt_max = sb("flt_max", [NQ, 1], F32)
    mask_u8 = sb("mask_u8", [NQ, B + 1, NKV], U8)
    null_row = sb("null_row", [P, HD1], F32)
    null_col = sb("null_col", [P, 1], F32)
    null_ss = sb("null_ss", [P, 1], F32)
    q_scale_col = sb("q_scale_col", [P, 1], F32)
    k_scale_col = sb("k_scale_col", [P, 1], F32)
    halfmask = sb("halfmask", [P, 2], F32)
    key_ss = sb("key_ss", [P, 3, 8], F32)
    q_ss = sb("q_ss", [NQ, 8], F32)
    row_max = sb("row_max", [NQ, B], F32)
    top_out = sb("top_out", [NQ, 1], F32)

    E1, H1, HS = 64, 128, 256
    G1, TOPG, SCALE2 = 8, 4, 2.5
    HT = B * NQ // 2
    PAIRS = 4
    at_k, at_v = [0], [0]
    xnT_all = carve(keys_arena, at_k, (2, B * NQ))
    xT_high = carve_r("xT_high", keys_at, at_k, (2, B * NQ))
    xT_low = carve_r("xT_low", keys_at, at_k, (2, B * NQ))
    g_act = [carve(keys_arena, at_k, (HT,)) for _ in range(2)]
    sh_hT = carve(keys_arena, at_k, (2, B * NQ))
    sh_g = [carve(keys_arena, at_k, (HT,)) for _ in range(2)]
    sh_u = [carve(keys_arena, at_k, (HT,)) for _ in range(2)]
    sh_y = carve(keys_arena, at_k, (B, D))[0:NQ]
    scores1 = carve(keys_arena, at_k, (B, E1))[0:NQ]
    sfc = carve(keys_arena, at_k, (B, E1))[0:NQ]
    picked = carve(keys_arena, at_k, (B, E1))[0:NQ]
    work1 = carve(keys_arena, at_k, (B, E1))[0:NQ]
    swg = carve(vals_arena, at_v, (2, HS))
    swu = carve(vals_arena, at_v, (2, HS))
    swd = carve(vals_arena, at_v, (2, D))
    router_rows = carve(vals_arena, at_v, (D,))[0:E1]
    routerT = carve(vals_arena, at_v, (2, E1))
    WGU, WALL = 4 * H1, 4 * H1 + D
    we = [carve(vals_arena, at_v, (WALL,)) for _ in range(2)]
    we_high = [carve_r(f"we_high{p}", vals_at, at_v, (WALL,)) for p in range(2)]
    we_low = [carve_r(f"we_low{p}", vals_at, at_v, (WALL,)) for p in range(2)]
    h1T = carve(vals_arena, at_v, (B * NQ,))
    h1_high = [carve_r(f"h1_high{p}", vals_at, at_v, (B * NQ,)) for p in range(2)]
    group2 = vals_arena[0:NQ, at_v[0]:at_v[0] + 4 * B * G1 * 4].rearrange("q (k n) -> q k n", k=4)
    h1_low = [carve_r(f"h1_low{p}", vals_at, at_v, (B * NQ,)) for p in range(2)]
    coef = carve(vals_arena, at_v, (B, E1))[0:NQ]
    work2 = carve(vals_arena, at_v, (B, E1))[0:NQ]
    e_bias = carve(vals_arena, at_v, (E1,))[0:NQ]
    iota64 = sb("iota64", [E1, E1], F32)
    e_col = sb("e_col", [E1, 1], F32)
    group_sum = carve(vals_arena, at_v, (B, G1))[0:NQ]
    group_kept = carve(vals_arena, at_v, (B, G1))[0:NQ]
    top8 = carve(vals_arena, at_v, (B, 8))[0:NQ]
    weight_sum = sb("weight_sum", [NQ, B], F32)
    taken = carve(vals_arena, at_v, (E1,))[0:NQ]
    used = sb("used", [E1, 4], F32)
    place = carve(vals_arena, at_v, (E1,))[0:E1]
    expert_list = sb("expert_list", [1, E1], I32)
    n_used = sb("n_used", [1, 1], I32)

    consts_ready = sem("consts_ready")
    x_loaded = sem("x_loaded")
    w0_loaded, wo0_loaded = sem("w0_loaded"), sem("wo0_loaded")
    N_W0 = 6
    dve_step = sem("dve_step")
    ln_stats, ln_std = sem("ln_stats"), sem("ln_std")
    bq_scaled = sem("bq_scaled")

    ctx_loaded = [sem(f"ctx_loaded{p}") for p in range(2)]
    ctxT_in_psum, ctxT_ready = sem("ctxT_in_psum"), sem("ctxT_ready")
    xn_ready, xnT_in_psum, xnT_ready = sem("xn_ready"), sem("xnT_in_psum"), sem("xnT_ready")
    k_in_psum, k_stored = sem("k_in_psum"), sem("k_stored")
    v_in_psum, v_stored = sem("v_in_psum"), sem("v_stored")
    q_in_psum, q_stored = sem("q_in_psum"), sem("q_stored")

    gate_loaded, xs_cleared = sem("gate_loaded"), sem("xs_cleared")
    xn_kept, gate_logits = sem("xn_kept"), sem("gate_logits")
    g_centred, g_exp = sem("g_centred"), sem("g_exp")
    choice_ready, ranks_ready, slots_ready = sem("choice_ready"), sem("ranks_ready"), sem("slots_ready")
    xs_scattered = sem("xs_scattered")
    expert_used = sem("expert_used")
    rows_used = sem("rows_used")
    w1_loaded = [sem(f"w1_loaded{p}") for p in range(2)]
    w2_loaded = [sem(f"w2_loaded{p}") for p in range(2)]
    xs_loaded = [sem(f"xs_loaded{p}") for p in range(2)]
    xsT_ready = sem("xsT_ready")
    hidden_in_psum, hidden_ready = sem("hidden_in_psum"), sem("hidden_ready")
    ys_ready = sem("ys_ready")
    ys_stored = [sem(f"ys_stored{p}") for p in range(2)]
    y_gathered = [sem(f"y_gathered{b}") for b in range(B)]
    x1_stats = sem("x1_stats")

    const1_loaded = sem("const1_loaded")
    w1x_loaded = sem("w1x_loaded")
    null_v_stored = sem("null_v_stored")
    kq1_cleared = sem("kq1_cleared")
    mask_null = sem("mask_null")
    mask_ready = sem("mask_ready")
    null_norm = sem("null_norm")
    null_sq = sem("null_sq")
    null_k_stored = sem("null_k_stored")
    v1_in_psum = sem("v1_in_psum")
    v1_stored = sem("v1_stored")
    q1_in_psum = sem("q1_in_psum")
    k1_squared = sem("k1_squared")
    k1_ss = sem("k1_ss")
    k1_norm = sem("k1_norm")
    k1_inv = sem("k1_inv")
    k1_scaled = sem("k1_scaled")
    q1_squared = sem("q1_squared")
    q1_ss = sem("q1_ss")
    q1_norm = sem("q1_norm")
    q1_inv = sem("q1_inv")
    q1_scaled = sem("q1_scaled")
    kT1_stored = sem("kT1_stored")
    kT1_in_psum = sem("kT1_in_psum")
    k1_in_psum = sem("k1_in_psum")
    qT1_stored = sem("qT1_stored")
    qT1_in_psum = sem("qT1_in_psum")
    take_step = sem("take_step")
    x3_stats = sem("x3_stats")

    sh_loaded = sem("sh_loaded")
    router_loaded = sem("router_loaded")
    r_wT_in_psum = sem("r_wT_in_psum")
    r_wT_ready = sem("r_wT_ready")
    r_scores = sem("r_scores")
    r_taken = sem("r_taken")
    r_counted = sem("r_counted")
    r_used = sem("r_used")
    r_placed = sem("r_placed")
    r_place_ready = sem("r_place_ready")
    r_listed = sem("r_listed")
    list_ready = sem("list_ready")
    sh_in_psum = sem("sh_in_psum")
    sh_g_taken = sem("sh_g_taken")
    sh_u_taken = sem("sh_u_taken")
    sh_h_ready = sem("sh_h_ready")
    sh_y_in_psum = sem("sh_y_in_psum")
    sh_y_taken = sem("sh_y_taken")
    sh_added = sem("sh_added")
    x_high_ready = sem("x_high_ready")
    x_low_ready = sem("x_low_ready")
    we_high_ready = sem("we_high_ready")
    we_split = sem("we_split")
    h1_full = sem("h1_full")
    h1_high_ready = sem("h1_high_ready")
    gu_in_psum = sem("gu_in_psum")
    silu_done = sem("silu_done")
    h1_ready = sem("h1_ready")
    y1_in_psum = sem("y1_in_psum")
    y1_added = sem("y1_added")
    out_stored = sem("out_stored")
    x_final = sem("x_final")
    we_loaded = [sem(f"we_loaded{p}") for p in range(2)]

    class Attn:

        def __init__(s, n, heads, hd, nk, vcols, negated=False):
            s.exp_scale = -1.0 if negated else 1.0
            s.n, s.heads, s.hd, s.nk, s.vcols = n, heads, hd, nk, vcols
            s.ppb = heads // 2
            s.hpc = P // hd
            s.chunks = heads * hd // P
            s.tail = nk - 2 * P
            s.mask_bias = None
            s.kT = kT_all[:, 0:s.chunks * (B + 1) * nk].rearrange("p (c n) -> p c n", c=s.chunks)
            s.qT = qT_all[:, 0:s.chunks * (B + 1) * NQ].rearrange("p (c n) -> p c n", c=s.chunks)
            s.qm_ready = sem(f"L{n}_qm_ready")
            s.scores_ready = sem(f"L{n}_scores_ready")
            s.clipped = sem(f"L{n}_clipped")
            s.max_ready = sem(f"L{n}_max_ready")
            s.exp_done = sem(f"L{n}_exp_done")
            s.transposed = sem(f"L{n}_transposed")
            s.probsT_ready = sem(f"L{n}_probsT_ready")
            s.attended = sem(f"L{n}_attended")
            s.out_taken = sem(f"L{n}_out_taken")
            s.tok_ready = sem(f"L{n}_tok_ready")
            s.inv_ready = sem(f"L{n}_inv_ready")
            s.normalised = sem(f"L{n}_normalised")
            s.tokT_in_psum = sem(f"L{n}_tokT_in_psum")
            s.tokT_ready = sem(f"L{n}_tokT_ready")
            s.projected = sem(f"L{n}_projected")
            s.added = sem(f"L{n}_added")
            s.stats_ready = sem(f"L{n}_stats_ready")
            s.vs_loaded = [sem(f"L{n}_vs_loaded{p}") for p in range(2)]

    A0 = Attn(0, 16, 16, NKV, 32)
    A1 = Attn(1, 8, 64, NKV + 1, 64, negated=True)

    ctxT_ps = psum[0:DCC, 0:2, 0:NKV]
    k_ps = psum[:, 2:4, 0:NKV]
    v_ps = psum[:, 4:6, :].rearrange("p a (t n) -> p (a t) n", t=2)
    xnT_ps = psum[:, 6, 0:2 * NQ].rearrange("p (c n) -> p c n", c=2)
    q_ps = psum[:, 7, 0:2 * NQ].rearrange("p (c n) -> p c n", c=2)
    xnT1_ps = psum[:, 7, 0:2 * NQ].rearrange("p (c n) -> p c n", c=2)
    k1_ps = psum[:, 2:5, :]
    v1_ps = [psum[:, k, :] for k in (5, 6, 5)]
    q1_ps = psum[:, 7, :]
    score_ps = [psum[:, 2 * k:2 * k + 2, :] for k in range(2)]
    pT_ps = psum[:, 4:6, :].rearrange("p a (t n) -> p (a t) n", t=2)[:, 0:3, 0:2 * NQ]
    o_ps = psum[:, 6, 0:4 * NQ].rearrange("p (g n) -> p g n", g=4)
    y_ps = psum[:, 7, :]

    rows = [P, P, TAIL]

    def sp_load0(sp):
        sp.dma_start(x[:, 1:B + 1, :], a["x"].rearrange("b q d -> q b d")).then_inc(x_loaded, 16)
        sp_ctx(sp, 0, 0)
        for dst, src in (
            (wk0[:, :, :], a["L0_xattn_Wk"].rearrange("(c p) n -> p c n", p=DCC)),
            (wv0[0:DCC, :, :], a["L0_xattn_Wv"].rearrange("(c p) n -> p c n", p=DCC)),
            (wv0[DCC:DCC + 1, 1, :], a["L0_xattn_bv"].rearrange("(o n) -> o n", o=1)),
            (bk0[:, :], a["L0_xattn_bk"].rearrange("(c p) -> p c", p=P)),
            (wq0[:, :, :], a["L0_xattn_Wq"].rearrange("(c p) n -> p c n", p=P)),
            (bq0[:, :], a["L0_xattn_bq"].rearrange("(c p) -> p c", p=P)),
        ):
            sp.dma_start(dst, src, allow_slow_non_contiguous=True).then_inc(w0_loaded, 16)
        sp_ctx(sp, 1, 1)
        for dst, src in (
            (wo0[:, :, :], a["L0_xattn_Wo"].rearrange("(c p) n -> p c n", p=P)),
            (bo0[:, :], a["L0_xattn_bo"].rearrange("(o n) -> o n", o=1)),
        ):
            sp.dma_start(dst, src).then_inc(wo0_loaded, 16)

    def sp_ctx(sp, b, p):
        src = a["ctx_768"][b]
        sp.dma_start(ctx_nat[p][:, 0:FULL, :], src[0:FULL * P, :].rearrange("(t p) d -> p t d", p=P)
                     ).then_inc(ctx_loaded[p], 16)
        sp.dma_start(ctx_nat[p][0:TAIL, FULL, :], src[FULL * P:NKV, :]).then_inc(ctx_loaded[p], 16)

    def sp_project0(sp):
        with sp.Fori(1, B // 2) as i:
            for p in range(2):
                sp.wait_ge(ctxT_in_psum, 2 * i + p - 1)
                sp_ctx(sp, 2 * i + p, p)

    def pool_consts(pool):
        nc.gpsimd.memset(ident[:, :], 0.0).then_inc(consts_ready, 1)
        nc.gpsimd.memset(headmask[:, :], 1.0).then_inc(consts_ready, 1)
        nc.gpsimd.memset(eps_col[:, :], EPS).then_inc(consts_ready, 1)
        nc.gpsimd.memset(ones_row[:, :], 1.0).then_inc(consts_ready, 1)
        pool.wait_ge(consts_ready, 4)
        nc.gpsimd.memset(ctxT[DCC:DCC + 1, :, :], 1.0).then_inc(consts_ready, 1)
        pool.wait_ge(consts_ready, 5)
        nc.gpsimd.affine_select(out=ident[:, :], in_=ident[:, :], compare_op=ALU.not_equal, fill=1.0, base=0,
                                pattern=[[-1, P]], channel_multiplier=1).then_inc(consts_ready, 1)
        nc.gpsimd.affine_select(out=headmask[:, :], in_=headmask[:, :], compare_op=ALU.is_ge, fill=0.0, base=0,
                                pattern=[[-16, 8]], channel_multiplier=1).then_inc(consts_ready, 1)
        pool.wait_ge(consts_ready, 7)
        nc.gpsimd.affine_select(out=headmask[:, :], in_=headmask[:, :], compare_op=ALU.is_ge, fill=0.0, base=15,
                                pattern=[[16, 8]], channel_multiplier=-1).then_inc(consts_ready, 1)
        nc.gpsimd.memset(v_all[:, 0:B, :, :].rearrange("p b t (h e) -> p (b t h) e", e=32)[:, :, 16:32], 0.0
                         ).then_inc(consts_ready, 1)
        nc.gpsimd.memset(A0.kT[:, :, B * NKV:(B + 1) * NKV], 0.0).then_inc(consts_ready, 1)
        nc.gpsimd.memset(A0.qT[:, :, B * NQ:(B + 1) * NQ], 0.0).then_inc(consts_ready, 1)
        nc.gpsimd.memset(sums[:, :, :], 1.0).then_inc(consts_ready, 1)
        nc.gpsimd.memset(x[:, 0, :], 0.0).then_inc(consts_ready, 1)
    N_CONSTS = 13

    dve_steps = [0]

    def mark(ins):
        dve_steps[0] += 1
        ins.then_inc(dve_step, 1)

    def marked(dve):
        dve.wait_ge(dve_step, dve_steps[0])

    def step(dve, ins):
        mark(ins)
        marked(dve)

    def dve_ln_finish(dve, k):
        for b in range(B):
            nc.vector.bn_aggr(mv[:, b, :], stats[:, b + 1, :]).then_inc(ln_stats, 1)
        dve.wait_ge(ln_std, k + 1)
        step(dve, nc.vector.reciprocal(rstd[:, :], std[:, :]))

    def act_std(act, k):
        act.wait_ge(ln_stats, B * (k + 1))
        act.wait_ge(consts_ready, N_CONSTS)
        nc.scalar.activation(std[:, :], mv[:, :, 1], ACT.Sqrt, bias=eps_col[0:NQ, :]).then_inc(ln_std, 1)

    def dve_project0(dve):
        dve.wait_ge(x_loaded, 16)
        for b in range(B):
            mark(nc.vector.bn_stats(stats[:, b + 1, :], x[:, b + 1, :]))
        marked(dve)
        dve_ln_finish(dve, 0)
        with dve.Fori(0, B) as b:
            nc.vector.tensor_scalar(xn[:, :], x[:, b + 1, :], mv[:, b, 0:1], rstd[:, bass.ds(b, 1)], ALU.subtract, ALU.mult
                                    ).then_inc(xn_ready, 1)
            dve.wait_ge(xnT_in_psum, b + 1)
            nc.vector.tensor_copy(xnT[:, :, :], xnT_ps).then_inc(xnT_ready, 1)
            dve.wait_ge(v_in_psum, b + 1)
            nc.vector.tensor_copy(
                v_all[:, b, 0:FULL, :].rearrange("p t (h e) -> p (t h) e", e=32)[:, :, 0:16],
                v_ps[:, 0:FULL, :].rearrange("p t (h e) -> p (t h) e", e=16)).then_inc(v_stored, 1)
            nc.vector.tensor_copy(
                v_all[0:TAIL, b, FULL, :].rearrange("p (h e) -> p h e", e=32)[:, :, 0:16],
                v_ps[0:TAIL, FULL, :].rearrange("p (h e) -> p h e", e=16)).then_inc(v_stored, 1)

    def pe_project0(pe):
        pe.wait_ge(consts_ready, N_CONSTS)
        pe.wait_ge(w0_loaded, 16 * N_W0)
        with pe.Fori(0, B // 2) as i:
            for p in range(2):
                b = 2 * i + p
                pe.wait_ge(ctx_loaded[p], 32 * i + 32)
                for c in range(2):
                    for t in range(3):
                        last = nc.tensor.transpose(ctxT_ps[:, c, t * P:t * P + rows[t]],
                                                   ctx_nat[p][0:rows[t], t, c * DCC:(c + 1) * DCC],
                                                   ident[0:rows[t], 0:rows[t]])
                last.then_inc(ctxT_in_psum, 1)
                pe.wait_ge(xn_ready, b + 1)
                for c in range(2):
                    last = nc.tensor.transpose(xnT_ps[:, c, :], xn[:, c * P:(c + 1) * P], ident[0:NQ, 0:NQ])
                last.then_inc(xnT_in_psum, 1)
                pe.wait_ge(ctxT_ready, b + 1)
                for m in range(2):
                    for c in range(2):
                        last = nc.tensor.matmul(k_ps[:, m, :], wk0[:, c, m * P:(m + 1) * P], ctxT[0:DCC, c, :],
                                                start=(c == 0), stop=(c == 1))
                last.then_inc(k_in_psum, 1)
                pe.wait_ge(xnT_ready, b + 1)
                for t in range(3):
                    for c in range(2):
                        last = nc.tensor.matmul(v_ps[0:rows[t], t, :], ctxT[0:DCC + c, c, t * P:t * P + rows[t]],
                                                wv0[0:DCC + c, c, :], start=(c == 0), stop=(c == 1))
                last.then_inc(v_in_psum, 1)
                for m in range(2):
                    for c in range(2):
                        last = nc.tensor.matmul(q_ps[:, m, :], wq0[:, c, m * P:(m + 1) * P], xnT[:, c, :],
                                                start=(c == 0), stop=(c == 1))
                last.then_inc(q_in_psum, 1)

    def act_project0(act):
        act_std(act, 0)
        act.wait_ge(w0_loaded, 16 * N_W0)
        nc.scalar.activation(bq0s[:, :], bq0[:, :], ACT.Copy, scale=SCALE0).then_inc(bq_scaled, 1)
        act.wait_ge(bq_scaled, 1)
        with act.Fori(0, B) as b:
            act.wait_ge(ctxT_in_psum, b + 1)
            nc.scalar.activation(ctxT[0:DCC, :, :], ctxT_ps, ACT.Copy).then_inc(ctxT_ready, 1)
            act.wait_ge(k_in_psum, b + 1)
            for m in range(2):
                nc.scalar.activation(A0.kT[:, m, bass.ds(b * NKV, NKV)], k_ps[:, m, :], ACT.Identity,
                                     bias=bk0[:, m:m + 1]).then_inc(k_stored, 1)
            act.wait_ge(q_in_psum, b + 1)
            for m in range(2):
                nc.scalar.activation(A0.qT[:, m, bass.ds(b * NQ, NQ)], q_ps[:, m, :], ACT.Identity,
                                     bias=bq0s[:, m:m + 1], scale=SCALE0).then_inc(q_stored, 1)

    def sp_attend(sp, L, v_ready):
        v_ready(sp)

        def load(b, p):
            sp.dma_start(vs[p][:, 0:FULL, :], v_all[:, b, 0:FULL, :]).then_inc(L.vs_loaded[p], 16)
            sp.dma_start(vs[p][0:L.tail, FULL, :], v_all[0:L.tail, b, FULL, :]).then_inc(L.vs_loaded[p], 16)
        load(0, 0)
        load(1, 1)
        with sp.Fori(1, B // 2) as i:
            for p in range(2):
                sp.wait_ge(L.attended, 2 * i + p)
                load(2 * i + p, p)

    def pool_attend(pool, L, q_ready, mask):
        q_ready(pool)

        def spread(b, p):
            for c in range(L.chunks):
                nc.gpsimd.tensor_tensor(
                    qm[p][:, c * L.hpc:(c + 1) * L.hpc, :],
                    L.qT[:, c, bass.ds(b * NQ, NQ)].unsqueeze(1).broadcast_to([P, L.hpc, NQ]),
                    mask.unsqueeze(2).broadcast_to([P, L.hpc, NQ]), ALU.mult).then_inc(L.qm_ready, 1)
        for b in range(2):
            spread(b, b)
        with pool.Fori(1, B // 2) as i:
            for p in range(2):
                pool.wait_ge(L.scores_ready, L.ppb * (2 * i + p - 1))
                spread(2 * i + p, p)
        pool.wait_ge(L.scores_ready, L.ppb * (B - 1))
        spread(B, 0)

    def pe_attend(pe, L, ready):
        ready(pe)
        nrows = [P, P, L.tail]

        def scores(j, b, clipped):
            h = 2 * (j % L.ppb)
            p = (j // L.ppb) % 2
            if clipped is not None:
                pe.wait_ge(L.clipped, clipped)
            if j % L.ppb == 0:
                pe.wait_ge(L.qm_ready, L.chunks * (b + 1))
            for hh in range(2):
                last = nc.tensor.matmul(score_ps[j % 2][0:NQ, hh, 0:L.nk], qm[p][:, h + hh, :],
                                        L.kT[:, (h + hh) // L.hpc, bass.ds(b * L.nk, L.nk)], start=True, stop=True)
            last.then_inc(L.scores_ready, 1)

        def finish_transpose(b):
            pe.wait_ge(L.out_taken, b + 1)
            for g in range(4):
                last = nc.tensor.transpose(y_ps[0:NQ, g * P:(g + 1) * P], oT[:, g, :], ident[:, :])
            last.then_inc(L.tok_ready, 1)

        def finish_transpose_back(b):
            pe.wait_ge(L.normalised, b + 1)
            for c in range(L.chunks):
                last = nc.tensor.transpose(y_ps[:, c * NQ:(c + 1) * NQ], o_tok[:, c * P:(c + 1) * P],
                                           ident[0:NQ, 0:NQ])
            last.then_inc(L.tokT_in_psum, 1)

        def finish_project(b):
            pe.wait_ge(L.tokT_ready, b + 1)
            for c in range(L.chunks):
                last = nc.tensor.matmul(y_ps[0:NQ, 0:D], o_tokT[:, c, :], L.wo[:, c, :], start=(c == 0),
                                        stop=(c == L.chunks - 1 and L.bo is None))
            if L.bo is not None:
                last = nc.tensor.matmul(y_ps[0:NQ, 0:D], ones_row[0:1, 0:NQ], L.bo, start=False, stop=True)
            last.then_inc(L.projected, 1)
        finish = [finish_transpose, finish_transpose_back, finish_project]

        pe.sem_inc(L.transposed, NPB)
        pe.sem_inc(L.attended, 1)
        for j in range(LOOK):
            scores(j, 0, j - 1 if j >= 2 else None)
        with pe.Fori(0, B // 2) as i:
            for j in range(2 * L.ppb):
                n = 2 * L.ppb * i + j
                b = 2 * i + j // L.ppb
                p = (j // L.ppb) % 2
                s = j % L.ppb
                pe.wait_ge(L.exp_done, n + 1)
                for t in range(3):
                    for hh in range(2):
                        last = nc.tensor.transpose(pT_ps[0:nrows[t], t, hh * NQ:(hh + 1) * NQ],
                                                   probs[:, j % NPB, hh, t * P:t * P + nrows[t]], ident[0:NQ, 0:NQ])
                last.then_inc(L.transposed, 1)
                scores(j + LOOK, 2 * i + (j + LOOK) // L.ppb, n + LOOK - 1)
                if s < len(finish):
                    finish[s](b)
                pe.wait_ge(L.probsT_ready, n + 1)
                if s == 0:
                    pe.wait_ge(L.vs_loaded[p], 32 * i + 32)
                    pe.wait_ge(L.out_taken, b + 1)
                for hh in range(2):
                    h = 2 * s + hh
                    g, strip = (h * L.vcols) // P, (h * L.vcols) % P
                    for t in range(3):
                        last = nc.tensor.matmul(o_ps[strip:strip + L.vcols, g, :],
                                                vs[p][0:nrows[t], t, h * L.vcols:(h + 1) * L.vcols],
                                                probsT[j % 2][0:nrows[t], t, hh * NQ:(hh + 1) * NQ],
                                                start=(t == 0), stop=(t == 2))
                if s == L.ppb - 1:
                    last.then_inc(L.attended, 1)
        for step in finish:
            step(B)

    def act_attend(act, L):
        def exps(j, n, b):
            p = (j // L.ppb) % 2
            if j % L.ppb == 0:
                act.wait_ge(L.normalised, b)
            act.wait_ge(L.max_ready, n + 1)
            for hh in range(2):
                h = 2 * (j % L.ppb) + hh
                last = nc.scalar.activation(probs[:, j % NPB, hh, 0:L.nk], probs[:, j % NPB, hh, 0:L.nk], ACT.Exp,
                                            bias=negmax[:, j % NPB, hh:hh + 1], scale=L.exp_scale,
                                            accum_out=sums[:, p, h:h + 1])
            last.then_inc(L.exp_done, 1)

        def finish_take(b):
            act.wait_ge(L.attended, b + 1)
            nc.scalar.activation(oT[:, :, :], o_ps, ACT.Copy).then_inc(L.out_taken, 1)

        def finish_takeT(b):
            act.wait_ge(L.tokT_in_psum, b + 1)
            nc.scalar.activation(o_tokT[:, 0:L.chunks, :], y_ps[:, 0:L.chunks * NQ].rearrange(
                "p (c n) -> p c n", c=L.chunks), ACT.Copy).then_inc(L.tokT_ready, 1)
        finish = {0: finish_take, 2: finish_takeT}

        if L.mask_bias is not None:
            act.wait_ge(mask_null, 3)
            L.mask_bias(act, 0, 0)
        for j in range(AHEAD):
            exps(j, j, 0)
        with act.Fori(0, B // 2) as i:
            for j in range(2 * L.ppb):
                n = 2 * L.ppb * i + j
                b = 2 * i + j // L.ppb
                if j % L.ppb in finish:
                    finish[j % L.ppb](b)
                if j % L.ppb == 1 and L.mask_bias is not None:
                    L.mask_bias(act, b + 1, 1 - (j // L.ppb) % 2)
                act.wait_ge(L.transposed, n + 1 + NPB)
                nc.scalar.activation(probsT[j % 2][:, 0:FULL, :], pT_ps[:, 0:FULL, :], ACT.Copy)
                nc.scalar.activation(probsT[j % 2][0:L.tail, FULL, :], pT_ps[0:L.tail, FULL, :], ACT.Copy
                                     ).then_inc(L.probsT_ready, 1)
                exps(j + AHEAD, n + AHEAD, 2 * i + (j + AHEAD) // L.ppb)
        for s in finish:
            finish[s](B)

    def dve_attend(dve, L):
        def normalise(b, p):
            dve.wait_ge(L.tok_ready, b + 1)
            nc.vector.reciprocal(inv_sums[:, 0:L.heads], sums[:, p, 0:L.heads]).then_inc(L.inv_ready, 1)
            dve.wait_ge(L.inv_ready, b + 1)
            nc.vector.tensor_tensor(
                o_tok[:, 0:L.heads * L.hd].rearrange("q (h e) -> q h e", e=L.hd),
                y_ps[0:NQ, :].rearrange("q (h e) -> q h e", e=L.vcols)[:, :, 0:L.hd],
                inv_sums[:, 0:L.heads].unsqueeze(2).broadcast_to([NQ, L.heads, L.hd]), ALU.mult
            ).then_inc(L.normalised, 1)

        L.prepare(dve)
        for j in range(AHEAD):
            L.masked_max(dve, j, j, 0)
        with dve.Fori(0, B // 2) as i:
            for j in range(2 * L.ppb):
                n = 2 * L.ppb * i + j
                b = 2 * i + j // L.ppb
                s = j % L.ppb
                if s == 1:
                    normalise(b, (j // L.ppb + 1) % 2)
                if s == 3:
                    L.take(dve, b)
                L.masked_max(dve, j + AHEAD, n + AHEAD, 2 * i + (j + AHEAD) // L.ppb)
        normalise(B, 1)
        L.take(dve, B)

    A0.wo, A0.bo = wo0, bo0[0:1, :]

    def a0_prepare(dve):
        dve.wait_ge(q_stored, 2 * B)
        nc.vector.memset(o_ps, 0.0).then_inc(A0.out_cleared, 1)
    A0.out_cleared = sem("L0_out_cleared")
    A0.prepare = a0_prepare

    def a0_masked_max(dve, j, n, b):
        k = j % NPB
        dve.wait_ge(A0.scores_ready, n + 1)
        dve.wait_ge(A0.transposed, n + 1)
        nc.vector.tensor_scalar(probs[:, k, :, 0:NKV], score_ps[j % 2][0:NQ, :, 0:NKV], -CLAMP, CLAMP, ALU.max, ALU.min
                                ).then_inc(A0.clipped, 1)
        dve.wait_ge(A0.clipped, n + 1)
        nc.vector.tensor_reduce(negmax[:, k, :], probs[:, k, :, 0:NKV], AX.X, ALU.max, negate=True
                                ).then_inc(A0.max_ready, 1)
    A0.masked_max = a0_masked_max

    def a0_take(dve, b):
        dve.wait_ge(A0.projected, b + 1)
        nc.vector.tensor_tensor(x[:, b, :], x[:, b, :], y_ps[0:NQ, 0:D], ALU.add).then_inc(A0.added, 1)
        dve.wait_ge(A0.added, b + 1)
        nc.vector.bn_stats(stats[:, b, :], x[:, b, :]).then_inc(A0.stats_ready, 1)
    A0.take = a0_take

    g_xnT_ps = psum[:, 0, 0:2 * NQ].rearrange("p (c n) -> p c n", c=2)
    logits_ps = psum[0:NQ, 1, 0:B * E0].rearrange("p (b e) -> p b e", b=B)
    ranks_ps = psum[0:NQ, 2, 0:B * E0].rearrange("p (b e) -> p b e", b=B)
    totals_ps = psum[:, 3, 0:B * E0].rearrange("p (b e) -> p b e", b=B)
    xsT_ps = [psum[:, k, 0:2 * P] .rearrange("p (c n) -> p c n", c=2) for k in range(2)]
    b1_ps = [psum[:, k, 2 * P:2 * P + HC] for k in range(2)]
    hid_ps = [psum[:, 2 + k, :].rearrange("p (m n) -> p m n", m=4) for k in range(4)]
    ys_ps = [psum[:, 6 + k, 0:D] for k in range(2)]

    def pool_consts_moe(pool):
        nc.gpsimd.memset(earlier[:, :], 1.0).then_inc(consts_ready, 1)
        nc.gpsimd.memset(ones_sq[:, :], 1.0).then_inc(consts_ready, 1)
        nc.gpsimd.memset(below8[:, :, :], 1.0).then_inc(consts_ready, 1)
        nc.gpsimd.iota(iota16[:, :], [[1, 16]], base=0, channel_multiplier=0, allow_small_or_imprecise_dtypes=True
                       ).then_inc(consts_ready, 1)
        nc.gpsimd.memset(zeros[:, :], 0.0).then_inc(consts_ready, 1)
        pool.wait_ge(consts_ready, N_CONSTS + 5)
        nc.gpsimd.affine_select(out=earlier[:, :], in_=earlier[:, :], compare_op=ALU.is_gt, fill=0.0, base=0,
                                pattern=[[1, NQ]], channel_multiplier=-1).then_inc(consts_ready, 1)
        nc.gpsimd.affine_select(out=below8[:, :, :], in_=below8[:, :, :], compare_op=ALU.is_gt, fill=0.0, base=0,
                                pattern=[[1, 8], [-1, 8]], channel_multiplier=0).then_inc(consts_ready, 1)
    N_MOE_CONSTS = 7

    def sp_load_moe(sp):
        sp.dma_start(wg0[:, :, :], a["L0_ffn_Wg"].rearrange("(c p) e -> p c e", p=P)).then_inc(gate_loaded, 16)
        sp.dma_start(bg0[:, :], a["L0_ffn_bg"].rearrange("(o e) -> o e", o=1)).then_inc(gate_loaded, 16)
        sp.wait_ge(consts_ready, N_CONSTS + N_MOE_CONSTS)
        sp.dma_start(xs_dram.rearrange("(i p) d -> p i d", p=P), zeros[:, :].unsqueeze(1).broadcast_to([P, NBLK, D])
                     ).then_inc(xs_cleared, 16)

    def dve_gate(dve):
        dve.wait_ge(A0.stats_ready, B + 1)
        dve_ln_finish(dve, 1)
        with dve.Fori(0, B) as b:
            dve.wait_ge(xnT_in_psum, B + b)
            nc.vector.tensor_scalar(xn[:, :], x[:, b + 1, :], mv[:, b, 0:1], rstd[:, bass.ds(b, 1)], ALU.subtract,
                                    ALU.mult).then_inc(xn_ready, 1)
            dve.wait_ge(xnT_in_psum, B + b + 1)
            nc.vector.tensor_copy(xnT[:, :, :], g_xnT_ps).then_inc(xnT_ready, 1)
            dve.wait_ge(xn_kept, b + 1)
        dve.wait_ge(gate_logits, B)
        dve.wait_ge(consts_ready, N_CONSTS + N_MOE_CONSTS)
        step(dve, nc.vector.tensor_copy(logits[:, :, :], logits_ps))
        step(dve, nc.vector.tensor_reduce(top_logit[:, :], logits[:, :, :], AX.X, ALU.max))
        top = top_logit[:, :].unsqueeze(2).broadcast_to([NQ, B, E0])
        grid = route_a[0:NQ, 0:B * E0].rearrange("q (b e) -> q b e", b=B)
        step(dve, nc.vector.tensor_tensor(choice[:, :, :], logits[:, :, :], top, ALU.is_equal))
        back = route_a[0:NQ, 64:64 + E0]
        step(dve, nc.vector.tensor_scalar(back, iota16[0:NQ, 0:E0], -1.0, float(E0), ALU.mult, ALU.add))
        each = back.unsqueeze(1).broadcast_to([NQ, B, E0])
        step(dve, nc.vector.tensor_tensor(grid, choice[:, :, :], each, ALU.mult))
        step(dve, nc.vector.tensor_reduce(slot_f[:, :], grid, AX.X, ALU.max))
        nc.vector.tensor_tensor(choice[:, :, :], each, slot_f[:, :].unsqueeze(2).broadcast_to([NQ, B, E0]),
                                ALU.is_equal).then_inc(choice_ready, 1)
        nc.vector.tensor_tensor(logits[:, :, :], logits[:, :, :], top, ALU.subtract).then_inc(g_centred, 1)
        dve.wait_ge(g_exp, 1)
        step(dve, nc.vector.tensor_reduce(top_weight[:, :], logits[:, :, :], AX.X, ALU.add))
        step(dve, nc.vector.reciprocal(top_weight[:, :], top_weight[:, :]))
        dve.wait_ge(ranks_ready, 1)
        step(dve, nc.vector.tensor_copy(counts[:, :, :], totals_ps))
        tokens, blocks, first, end = (per_expert[:, k, :] for k in range(4))
        step(dve, nc.vector.tensor_reduce(tokens, counts[:, :, :].rearrange("p b e -> p e b"), AX.X, ALU.add))
        nj = -(-B * NQ // P)
        over = route_a[:, 0:E0 * nj].rearrange("p (e j) -> p e j", e=E0)
        step(dve, nc.vector.tensor_scalar(block_expert[:, 0:nj], iota16[:, 0:nj], float(P), None, ALU.mult))
        step(dve, nc.vector.tensor_tensor(over, tokens.unsqueeze(2).broadcast_to([P, E0, nj]),
                                     block_expert[:, 0:nj].unsqueeze(1).broadcast_to([P, E0, nj]), ALU.is_gt))
        step(dve, nc.vector.tensor_reduce(blocks, over, AX.X, ALU.add))
        pairs = route_a[:, 0:64].rearrange("p (i j) -> p i j", i=8)
        step(dve, nc.vector.tensor_tensor(pairs, below8[:, :, :], blocks.unsqueeze(1).broadcast_to([P, E0, E0]), ALU.mult))
        step(dve, nc.vector.tensor_reduce(first, pairs, AX.X, ALU.add))
        step(dve, nc.vector.tensor_tensor(end, first, blocks, ALU.add))
        ended = route_a[:, 0:NBLK * E0].rearrange("p (i e) -> p i e", i=NBLK)
        step(dve, nc.vector.tensor_tensor(ended, end.unsqueeze(1).broadcast_to([P, NBLK, E0]),
                                     iota16[:, 0:NBLK].unsqueeze(2).broadcast_to([P, NBLK, E0]), ALU.is_le))
        step(dve, nc.vector.tensor_reduce(block_expert[:, :], ended, AX.X, ALU.add))
        nc.vector.tensor_scalar(block_expert_i[:, :], block_expert[:, :], float(E0 - 1), None, ALU.min
                                ).then_inc(slots_ready, 1)
        before = route_a[:, :].rearrange("p (b e k) -> p b e k", b=B, e=E0)
        step(dve, nc.vector.tensor_tensor(
            before, counts[:, :, :].rearrange("p k e -> p e k").unsqueeze(1).broadcast_to([P, B, E0, B]),
            below8[:, :, :].unsqueeze(2).broadcast_to([P, B, E0, B]), ALU.mult))
        step(dve, nc.vector.tensor_reduce(route_b[:, :, :], before, AX.X, ALU.add))
        step(dve, nc.vector.scalar_tensor_tensor(route_b[:, :, :], first.unsqueeze(1).broadcast_to([P, B, E0]), float(P),
                                            route_b[:, :, :], ALU.mult, ALU.add))
        step(dve, nc.vector.tensor_tensor(route_b[0:NQ], ranks_ps, route_b[0:NQ], ALU.add))
        step(dve, nc.vector.tensor_tensor(route_b[0:NQ], route_b[0:NQ], choice[:, :, :], ALU.mult))
        step(dve, nc.vector.tensor_reduce(slot_f[:, :], route_b[0:NQ], AX.X, ALU.add))
        nc.vector.tensor_copy(slot[:, :], slot_f[:, :]).then_inc(slots_ready, 1)

    def act_gate(act):
        act_std(act, 1)
        with act.Fori(0, B) as b:
            act.wait_ge(xn_ready, B + b + 1)
            nc.scalar.activation(xn_all[:, b, :], xn[:, :], ACT.Copy).then_inc(xn_kept, 1)
        act.wait_ge(g_centred, 1)
        nc.scalar.activation(logits[:, :, :], logits[:, :, :], ACT.Exp).then_inc(g_exp, 1)

    def pe_gate(pe):
        pe.wait_ge(gate_loaded, 32)
        pe.wait_ge(A0.added, B + 1)
        with pe.Fori(0, B) as b:
            pe.wait_ge(xn_ready, B + b + 1)
            pe.wait_ge(xnT_ready, B + b)
            for c in range(2):
                last = nc.tensor.transpose(g_xnT_ps[:, c, :], xn[:, c * P:(c + 1) * P], ident[0:NQ, 0:NQ])
            last.then_inc(xnT_in_psum, 1)
            pe.wait_ge(xnT_ready, B + b + 1)
            for c in range(2):
                nc.tensor.matmul(logits_ps[:, b, :], xnT[:, c, :], wg0[:, c, :], start=(c == 0), stop=False)
            nc.tensor.matmul(logits_ps[:, b, :], ones_row[0:1, 0:NQ], bg0[0:1, :], start=False, stop=True
                             ).then_inc(gate_logits, 1)
        pe.wait_ge(choice_ready, 1)
        nc.tensor.matmul(ranks_ps, earlier[:, :], choice[:, :, :], start=True, stop=True)
        nc.tensor.matmul(totals_ps, ones_sq[:, :], choice[:, :, :], start=True, stop=True).then_inc(ranks_ready, 1)

    def pool_dispatch(pool):
        pool.wait_ge(slots_ready, 2)
        pool.wait_ge(xn_kept, B)
        pool.wait_ge(xs_cleared, 16)
        for b in range(B):
            nc.gpsimd.indirect_dma_start(
                out=xs_dram, out_offset=bass.IndirectOffsetOnAxis(ap=slot[:, b:b + 1], axis=0),
                in_=xn_all[:, b, :], in_offset=None).then_inc(xs_scattered, 16)

    def pool_combine(pool):
        for p in range(2):
            pool.wait_ge(ys_stored[p], 16 * (NBLK // 2) + 16)
        for b in range(B):
            nc.gpsimd.indirect_dma_start(
                out=y_tok[:, b, :], out_offset=None, in_=ys_dram,
                in_offset=bass.IndirectOffsetOnAxis(ap=slot[:, b:b + 1], axis=0)).then_inc(y_gathered[b], 16)

    def sp_experts(sp):
        sp.wait_ge(slots_ready, 1)
        with sp.Fori(0, NBLK // 2) as i:
            for p in range(2):
                n = 2 * i + p
                e = sp.value_load(block_expert_i[0:1, bass.ds(n, 1)], min_val=0, max_val=E0 - 1)
                sp.wait_ge(expert_used, n + 1)
                sp.dma_start(w1_e[p], a["L0_ffn_W1"].rearrange("e (c q) h -> q (e c) h", q=P)[:, bass.ds(2 * e, 2), :]
                             ).then_inc(w1_loaded[p], 16)
                sp.dma_start(b1_rows[p][:, :], a["L0_ffn_b1"][e].rearrange("(m q) -> m q", q=P)
                             ).then_inc(w1_loaded[p], 16)
                if p == 0:
                    sp.wait_ge(xs_scattered, 16 * B)
                sp.wait_ge(rows_used, n + 1)
                sp.dma_start(xs_rows[p], xs_dram[bass.ds(n * P, P), :]).then_inc(xs_loaded[p], 16)
                sp.dma_start(w2_e[p], a["L0_ffn_W2"].rearrange("e (m q) d -> q (e m) d", q=P)[:, bass.ds(HC * e, HC), :]
                             ).then_inc(w2_loaded[p], 16)
                sp.dma_start(b2_row[p][:, :], a["L0_ffn_b2"][bass.ds(e, 1), :]).then_inc(w2_loaded[p], 16)

    def act_store_ys(act, n, p):
        act.wait_ge(ys_ready, n + 1)
        act.dma_start(ys_dram[bass.ds(n * P, P), :], ys_rows[p]).then_inc(ys_stored[p], 16)

    def pe_experts(pe):
        def rows(n, i, p):
            pe.wait_ge(xs_loaded[p], 16 * i + 16)
            pe.wait_ge(w1_loaded[p], 32 * i + 32)
            for c in range(2):
                nc.tensor.transpose(xsT_ps[p][:, c, :], xs_rows[p][:, c * P:(c + 1) * P], ident[:, :])
            nc.tensor.transpose(b1_ps[p], b1_rows[p][:, :], ident[0:HC, 0:HC]).then_inc(rows_used, 1)

        pe.wait_ge(slots_ready, 2)
        pe.sem_inc(expert_used, 2)
        pe.sem_inc(rows_used, 2)
        with pe.Fori(0, NBLK // 2) as i:
            for p in range(2):
                n = 2 * i + p
                rows(n, i, p)
                pe.wait_ge(xsT_ready, n + 1)
                for m in range(HC):
                    for c in range(2):
                        last = nc.tensor.matmul(hid_ps[2 * p + m // 4][:, m % 4, :], w1_e[p][:, c, m * P:(m + 1) * P],
                                                xsT[p][:, c, :], start=(c == 0), stop=(c == 1))
                    if m % 4 == 3:
                        last.then_inc(hidden_in_psum, 1)
                pe.wait_ge(w2_loaded[p], 32 * i + 32)
                nc.tensor.matmul(ys_ps[p], ones_row[0:1, :], b2_row[p][0:1, :], start=True, stop=False)
                for m in range(HC):
                    if m % 4 == 0:
                        pe.wait_ge(hidden_ready, 2 * n + 1 + m // 4)
                    last = nc.tensor.matmul(ys_ps[p], hT[p][:, m, :], w2_e[p][:, m, :], start=False, stop=(m == HC - 1))
                last.then_inc(expert_used, 1)

    def act_experts(act):
        for p in range(2):
            act.sem_inc(ys_stored[p], 16)
        with act.Fori(0, NBLK // 2) as i:
            for p in range(2):
                n = 2 * i + p
                act.wait_ge(xsT_ready, n + 1)
                for half in range(2):
                    act.wait_ge(hidden_in_psum, 2 * n + half + 1)
                    for m in range(4 * half, 4 * half + 4):
                        last = nc.scalar.activation(hT[p][:, m, :], hid_ps[2 * p + half][:, m % 4, :], ACT.Silu,
                                                    bias=b1_col[p][:, m:m + 1])
                    last.then_inc(hidden_ready, 1)
                act_store_ys(act, n, p)

    def dve_experts(dve):
        with dve.Fori(0, NBLK // 2) as i:
            for p in range(2):
                n = 2 * i + p
                dve.wait_ge(rows_used, n + 3)
                dve.wait_ge(expert_used, n + 1)
                nc.vector.tensor_copy(b1_col[p][:, :], b1_ps[p])
                nc.vector.tensor_copy(xsT[p], xsT_ps[p]).then_inc(xsT_ready, 1)
                dve.wait_ge(expert_used, n + 3)
                dve.wait_ge(ys_stored[p], 16 * i + 16)
                nc.vector.tensor_copy(ys_rows[p], ys_ps[p]).then_inc(ys_ready, 1)
        for b in range(B):
            dve.wait_ge(y_gathered[b], 16)
            mark(nc.vector.scalar_tensor_tensor(x[:, b + 1, :], y_tok[:, b, :], top_weight[:, b:b + 1], x[:, b + 1, :],
                                           ALU.mult, ALU.add))
            marked(dve)
            nc.vector.bn_stats(stats[:, b + 1, :], x[:, b + 1, :]).then_inc(x1_stats, 1)


    A1.wo, A1.bo = wo1, None

    def sp_load1(sp):
        for dst, src in (
            (wo1[:, :, :], a["L1_xattn_Wo"].rearrange("(c p) n -> p c n", p=P)),
            (g_norm[:, :], a["L1_xattn_g_norm"].rearrange("(o d) -> o d", o=1).broadcast_to([NQ, D])),
            (g_out[:, :], a["L1_xattn_g_out"].rearrange("(o d) -> o d", o=1).broadcast_to([NQ, D])),
            (mask_u8[:, 0:B, :], a["mask_BxS2_bf1"].rearrange("(o b) n -> o b n", o=1).broadcast_to([NQ, B, NKV])),
            (mask_u8[:, B, :], a["mask_BxS2_bf1"][0:1, :].broadcast_to([NQ, NKV])),
            (null_row[:, :], a["L1_xattn_null_kv"][0:1, :].broadcast_to([P, HD1])),
        ):
            sp.dma_start(dst, src).then_inc(const1_loaded, 16)
        for half in range(2):
            rows64 = slice(half * HD1, (half + 1) * HD1)
            for col, src in (
                (null_col, a["L1_xattn_null_kv"][0, :]),
                (q_scale_col, a["L1_xattn_q_scale"]),
                (k_scale_col, a["L1_xattn_k_scale"]),
            ):
                sp.dma_start(col[rows64, :], src.rearrange("(d o) -> d o", o=1), allow_slow_non_contiguous=True
                             ).then_inc(const1_loaded, 16)

    N_CONST1 = 12

    def sp_load1_weights(sp):
        sp.wait_ge(A0.added, B + 1)
        wkv = a["L1_xattn_Wkv"].rearrange("(c p) n -> p c n", p=DCC)
        sp.dma_start(wk1, wkv[:, :, 0:512]).then_inc(w1x_loaded, 16)
        sp.dma_start(wv1, wkv[:, :, 512:1024]).then_inc(w1x_loaded, 16)
        sp.dma_start(wq1, a["L1_xattn_Wq"].rearrange("(c p) n -> p c n", p=P)).then_inc(w1x_loaded, 16)

    def sp_project1(sp):
        def load(b, p):
            src = a["ctx_768"][b]
            sp.dma_start(ctx_nat[p][:, 0:FULL, :], src[0:FULL * P, :].rearrange("(t p) d -> p t d", p=P)
                         ).then_inc(ctx_loaded[p], 16)
            sp.dma_start(ctx_nat[p][0:TAIL, FULL, :], src[FULL * P:NKV, :]).then_inc(ctx_loaded[p], 16)
        sp.wait_ge(x1_stats, B)
        for h in range(8):
            sp.dma_start(v_all[TAIL:TAIL + 1, :, FULL, h * HD1:(h + 1) * HD1],
                         a["L1_xattn_null_kv"][1:2, :].unsqueeze(1).broadcast_to([1, B, HD1])).then_inc(null_v_stored, 16)
        load(0, 0)
        load(1, 1)
        with sp.Fori(1, B // 2) as i:
            for p in range(2):
                sp.wait_ge(ctxT_in_psum, B + 2 * i + p - 1)
                load(2 * i + p, p)

    def pool_consts1(pool):
        nc.gpsimd.memset(halfmask[:, :], -SCALE1).then_inc(consts_ready, 1)
        nc.gpsimd.memset(key_ss[:, :, :], 1.0).then_inc(consts_ready, 1)
        pool.wait_ge(consts_ready, N_CONSTS + N_MOE_CONSTS + 2)
        nc.gpsimd.affine_select(out=halfmask[:, :], in_=halfmask[:, :], compare_op=ALU.is_ge, fill=0.0, base=0,
                                pattern=[[-HD1, 2]], channel_multiplier=1).then_inc(consts_ready, 1)
        pool.wait_ge(consts_ready, N_CONSTS + N_MOE_CONSTS + 3)
        nc.gpsimd.affine_select(out=halfmask[:, :], in_=halfmask[:, :], compare_op=ALU.is_ge, fill=0.0, base=HD1 - 1,
                                pattern=[[HD1, 2]], channel_multiplier=-1).then_inc(consts_ready, 1)
        pool.wait_ge(consts_ready, N_CONSTS + N_MOE_CONSTS + 4)
        pool.wait_ge(const1_loaded, 16 * N_CONST1)
        nc.gpsimd.memset(flt_max[:, :], FLT_MAX).then_inc(mask_null, 1)
        nc.gpsimd.tensor_scalar(halfmask[:, :], halfmask[:, :], q_scale_col[:, 0:1], k_scale_col[:, 0:1], ALU.mult,
                                ALU.mult).then_inc(consts_ready, 1)

    def pool_clear1(pool):
        pool.wait_ge(x1_stats, B)
        nc.gpsimd.memset(A1.kT[:, :, B * A1.nk:(B + 1) * A1.nk], 0.0).then_inc(kq1_cleared, 1)
        nc.gpsimd.memset(A1.qT[:, :, B * NQ:(B + 1) * NQ], 0.0).then_inc(kq1_cleared, 1)

    def pool_mask_clear(pool):
        pool.wait_ge(ctxT_in_psum, 2 * B)
        for p in range(2):
            nc.gpsimd.memset(mask_bias[p][:, NKV:NKV + 1], 0.0).then_inc(mask_null, 1)

    def act_mask_bias(act, b, p):
        nc.scalar.activation(mask_bias[p][:, 0:NKV], mask_u8[:, b, :], ACT.Identity, bias=flt_max[:, 0:1],
                             scale=-FLT_MAX).then_inc(mask_ready, 1)
    A1.mask_bias = act_mask_bias

    def dve_project1(dve):
        dve.wait_ge(x1_stats, B)
        dve_ln_finish(dve, 2)
        for b in range(B):
            mark(nc.vector.tensor_scalar(y_all[:, b, :], x[:, b + 1, :], mv[:, b, 0:1], rstd[:, b:b + 1], ALU.subtract,
                                    ALU.mult))
        marked(dve)
        mark(nc.vector.tensor_reduce(row_max[:, :], y_all, AX.X, ALU.max))
        marked(dve)
        mark(nc.vector.reciprocal(row_max[:, :], row_max[:, :]))
        marked(dve)
        mark(nc.vector.tensor_tensor(y_all, y_all, row_max[:, :].unsqueeze(2).broadcast_to([NQ, B, D]), ALU.mult
                                ))
        marked(dve)
        for b in range(B):
            mark(nc.vector.bn_stats(stats[:, b + 1, :], y_all[:, b, :]))
        marked(dve)
        dve_ln_finish(dve, 3)
        for b in range(B):
            mark(nc.vector.tensor_scalar(y_all[:, b, :], y_all[:, b, :], mv[:, b, 0:1], rstd[:, b:b + 1], ALU.subtract,
                                    ALU.mult))
        dve.wait_ge(null_norm, 1)
        mark(nc.vector.tensor_scalar(null_ss[:, :], null_ss[:, :], 1e-12, None, ALU.max))
        marked(dve)
        mark(nc.vector.reciprocal(null_ss[:, :], null_ss[:, :]))
        marked(dve)
        mark(nc.vector.tensor_tensor(null_col[:, :], null_col[:, :], null_ss[:, :], ALU.mult))
        marked(dve)
        nc.vector.tensor_copy(
            A1.kT[:, :, 0:B * A1.nk].rearrange("p c (b n) -> p c b n", n=A1.nk)[:, :, :, NKV],
            null_col[:, :].unsqueeze(2).broadcast_to([P, 4, B])).then_inc(null_k_stored, 1)
        dve.wait_ge(const1_loaded, 16 * N_CONST1)

        def invert(ss, norm, b, ready):
            dve.wait_ge(norm, b + 1)
            nc.vector.tensor_scalar(ss, ss, 1e-12, None, ALU.max).then_inc(ready, 1)
            dve.wait_ge(ready, 2 * b + 1)
            nc.vector.reciprocal(ss, ss).then_inc(ready, 1)
            dve.wait_ge(ready, 2 * b + 2)

        def keep_v(b, t):
            dve.wait_ge(v1_in_psum, 3 * b + t + 1)
            nc.vector.tensor_copy(v_all[0:rows[t], b, t, :], v1_ps[t][0:rows[t], :]).then_inc(v1_stored, 1)

        with dve.Fori(0, B) as b:
            dve.wait_ge(xnT_in_psum, 2 * B + b)
            nc.vector.tensor_tensor(xn[:, :], y_all[:, b, :], g_norm[:, :], ALU.mult).then_inc(xn_ready, 1)
            dve.wait_ge(xnT_in_psum, 2 * B + b + 1)
            nc.vector.tensor_copy(xnT[:, :, :], xnT1_ps).then_inc(xnT_ready, 1)
            dve.wait_ge(k1_squared, 2 * b + 2)
            nc.vector.tensor_reduce(key_ss[:, 0:FULL, :], k_tok[:, 0:FULL, :].rearrange("p t (h e) -> p t h e", e=HD1),
                                    AX.X, ALU.add).then_inc(k1_ss, 1)
            nc.vector.tensor_reduce(key_ss[0:TAIL, FULL, :], k_tok[0:TAIL, FULL, :].rearrange("p (h e) -> p h e", e=HD1),
                                    AX.X, ALU.add).then_inc(k1_ss, 1)
            keep_v(b, 0)
            invert(key_ss[:, :, :], k1_norm, b, k1_inv)
            each = key_ss[:, :, :].unsqueeze(3).broadcast_to([P, 3, 8, HD1])
            for t in range(3):
                nc.vector.tensor_tensor(k_tok[0:rows[t], t, :].rearrange("p (h e) -> p h e", e=HD1),
                                        k1_ps[0:rows[t], t, :].rearrange("p (h e) -> p h e", e=HD1),
                                        each[0:rows[t], t], ALU.mult).then_inc(k1_scaled, 1)
            keep_v(b, 1)
            dve.wait_ge(q1_squared, b + 1)
            heads = lambda v: v.rearrange("p (h e) -> p h e", e=HD1)
            nc.vector.tensor_reduce(q_ss[:, :], heads(o_tok[:, :]), AX.X, ALU.add).then_inc(q1_ss, 1)
            keep_v(b, 2)
            invert(q_ss[:, :], q1_norm, b, q1_inv)
            nc.vector.tensor_tensor(heads(o_tok[:, :]), heads(q1_ps[0:NQ, :]),
                                    q_ss[:, :].unsqueeze(2).broadcast_to([NQ, 8, HD1]), ALU.mult).then_inc(q1_scaled, 1)

    def pe_project1(pe):
        pe.wait_ge(w1x_loaded, 48)
        pe.wait_ge(x1_stats, B)
        with pe.Fori(0, B // 2) as i:
            for p in range(2):
                b = 2 * i + p
                pe.wait_ge(ctx_loaded[p], 32 * (B // 2) + 32 * i + 32)
                pe.wait_ge(ctxT_ready, B + b)
                for c in range(2):
                    for t in range(3):
                        last = nc.tensor.transpose(ctxT_ps[:, c, t * P:t * P + rows[t]],
                                                   ctx_nat[p][0:rows[t], t, c * DCC:(c + 1) * DCC],
                                                   ident[0:rows[t], 0:rows[t]])
                last.then_inc(ctxT_in_psum, 1)
                pe.wait_ge(ctxT_ready, B + b + 1)
                for t in range(3):
                    for c in range(2):
                        last = nc.tensor.matmul(k1_ps[0:rows[t], t, :], ctxT[0:DCC, c, t * P:t * P + rows[t]],
                                                wk1[:, c, :], start=(c == 0), stop=(c == 1))
                last.then_inc(k1_in_psum, 1)
                pe.wait_ge(xn_ready, 2 * B + b + 1)
                for c in range(2):
                    last = nc.tensor.transpose(xnT1_ps[:, c, :], xn[:, c * P:(c + 1) * P], ident[0:NQ, 0:NQ])
                last.then_inc(xnT_in_psum, 1)
                pe.wait_ge(xnT_ready, 2 * B + b + 1)
                for t in range(3):
                    if t == 2:
                        pe.wait_ge(v1_stored, 3 * b + 1)
                    for c in range(2):
                        last = nc.tensor.matmul(v1_ps[t][0:rows[t], :], ctxT[0:DCC, c, t * P:t * P + rows[t]],
                                                wv1[:, c, :], start=(c == 0), stop=(c == 1))
                    last.then_inc(v1_in_psum, 1)
                    if t == 1:
                        for c in range(2):
                            last = nc.tensor.matmul(q1_ps[0:NQ, :], xnT[:, c, :], wq1[:, c, :], start=(c == 0), stop=(c == 1))
                        last.then_inc(q1_in_psum, 1)
                for t in range(3):
                    pe.wait_ge(k1_scaled, 3 * b + t + 1)
                    for c in range(4):
                        last = nc.tensor.transpose(k1_ps[:, t, c * P:c * P + rows[t]],
                                                   k_tok[0:rows[t], t, c * P:(c + 1) * P], ident[0:rows[t], 0:rows[t]])
                    last.then_inc(kT1_in_psum, 1)
                pe.wait_ge(q1_scaled, b + 1)
                for c in range(4):
                    last = nc.tensor.transpose(q1_ps[:, c * NQ:(c + 1) * NQ], o_tok[:, c * P:(c + 1) * P],
                                               ident[0:NQ, 0:NQ])
                last.then_inc(qT1_in_psum, 1)

    def act_project1(act):
        act_std(act, 2)
        act.wait_ge(const1_loaded, 16 * N_CONST1)
        act.wait_ge(consts_ready, N_CONSTS + N_MOE_CONSTS + 5)
        nc.scalar.activation(null_row[:, :], null_row[:, :], ACT.Square, accum_out=null_ss[:, :]).then_inc(null_sq, 1)
        act.wait_ge(null_sq, 1)
        nc.scalar.activation(null_ss[:, :], null_ss[:, :], ACT.Sqrt).then_inc(null_norm, 1)
        act_std(act, 3)
        with act.Fori(0, B) as b:
            act.wait_ge(ctxT_in_psum, B + b + 1)
            nc.scalar.activation(ctxT[0:DCC, :, :], ctxT_ps, ACT.Copy).then_inc(ctxT_ready, 1)
            act.wait_ge(k1_in_psum, b + 1)
            nc.scalar.activation(k_tok[:, 0:FULL, :], k1_ps[:, 0:FULL, :], ACT.Square).then_inc(k1_squared, 1)
            nc.scalar.activation(k_tok[0:TAIL, FULL, :], k1_ps[0:TAIL, FULL, :], ACT.Square).then_inc(k1_squared, 1)
            act.wait_ge(q1_in_psum, b + 1)
            nc.scalar.activation(o_tok[:, :], q1_ps[0:NQ, :], ACT.Square).then_inc(q1_squared, 1)
            act.wait_ge(k1_ss, 2 * b + 2)
            nc.scalar.activation(key_ss[:, :, :], key_ss[:, :, :], ACT.Sqrt).then_inc(k1_norm, 1)
            act.wait_ge(q1_ss, b + 1)
            nc.scalar.activation(q_ss[:, :], q_ss[:, :], ACT.Sqrt).then_inc(q1_norm, 1)
            for t in range(3):
                act.wait_ge(kT1_in_psum, 3 * b + t + 1)
                nc.scalar.activation(A1.kT[:, :, bass.ds(b * A1.nk + t * P, rows[t])],
                                     k1_ps[:, t, :].rearrange("p (c n) -> p c n", c=4)[:, :, 0:rows[t]], ACT.Copy
                                     ).then_inc(kT1_stored, 1)
            act.wait_ge(qT1_in_psum, b + 1)
            nc.scalar.activation(A1.qT[:, :, bass.ds(b * NQ, NQ)],
                                 q1_ps[:, 0:4 * NQ].rearrange("p (c n) -> p c n", c=4), ACT.Copy).then_inc(qT1_stored, 1)

    def a1_prepare(dve):
        dve.wait_ge(mask_null, 3)
    A1.prepare = a1_prepare
    A1.clipped = A1.max_ready

    def a1_masked_max(dve, j, n, b):
        k = j % NPB
        p = (j // A1.ppb) % 2
        dve.wait_ge(A1.scores_ready, n + 1)
        dve.wait_ge(A1.transposed, n + 1)
        if j % A1.ppb == 0:
            dve.wait_ge(mask_ready, b + 1)
        nc.vector.memset(turn[:, k:k + 1], 0.0)
        for hh in range(2):
            last = nc.vector.tensor_tensor_reduce(
                out=probs[:, k, hh, 0:A1.nk], in0=score_ps[j % 2][0:NQ, hh, 0:A1.nk], in1=mask_bias[p],
                op0=ALU.add, op1=ALU.min, scale=1.0, scalar=FLT_MAX, accum_out=negmax[:, k, hh:hh + 1])
        last.then_inc(A1.max_ready, 1)
    A1.masked_max = a1_masked_max

    def a1_take(dve, b):
        dve.wait_ge(A1.projected, b + 1)
        nc.vector.tensor_reduce(top_out[:, :], y_ps[0:NQ, 0:D], AX.X, ALU.max).then_inc(take_step, 1)
        dve.wait_ge(take_step, 2 * b + 1)
        nc.vector.reciprocal(top_out[:, :], top_out[:, :]).then_inc(take_step, 1)
        dve.wait_ge(take_step, 2 * b + 2)
        nc.vector.tensor_scalar(z_all[:, b, :], y_ps[0:NQ, 0:D], top_out[:, 0:1], None, ALU.mult).then_inc(A1.added, 1)
        dve.wait_ge(A1.added, b + 1)
        nc.vector.bn_stats(stats[:, b, :], z_all[:, b, :]).then_inc(A1.stats_ready, 1)
    A1.take = a1_take

    def dve_add1(dve):
        dve.wait_ge(A1.stats_ready, B + 1)
        dve_ln_finish(dve, 4)
        for b in range(B):
            mark(nc.vector.tensor_scalar(z_all[:, b + 1, :], z_all[:, b + 1, :], mv[:, b, 0:1], rstd[:, b:b + 1],
                                    ALU.subtract, ALU.mult))
        marked(dve)
        mark(nc.vector.tensor_tensor(z_all[:, 1:B + 1, :], z_all[:, 1:B + 1, :],
                                g_out[:, :].unsqueeze(1).broadcast_to([NQ, B, D]), ALU.mult))
        marked(dve)
        mark(nc.vector.tensor_tensor(x[:, 1:B + 1, :], x[:, 1:B + 1, :], z_all[:, 1:B + 1, :], ALU.add))
        marked(dve)
        for b in range(B):
            nc.vector.bn_stats(stats[:, b + 1, :], x[:, b + 1, :]).then_inc(x3_stats, 1)

    def act_add1(act):
        act_std(act, 4)


    gu_ps = [psum[:, k, 0:HT] for k in range(4)]
    y1_ps = [psum[0:NQ, 4 + k, :].rearrange("q (b d) -> q b d", b=2) for k in range(4)]
    r_logits_ps = psum[0:NQ, 4, :].rearrange("q (b e) -> q b e", b=B)
    r_xnT_ps = psum[:, 5, 0:2 * NQ].rearrange("p (c n) -> p c n", c=2)
    r_wT_ps = psum[:, 6, 0:2 * E1].rearrange("p (c e) -> p c e", c=2)
    r_count_ps = psum[0:E1, 7, 0:1]
    r_before_ps = psum[0:E1, 7, 8:9]
    r_total_ps = psum[0:E1, 7, 16:17]
    r_list_ps = psum[0:1, 7, 64:64 + E1]
    sh_y_ps = [psum[0:NQ, k, :].rearrange("q (b d) -> q b d", b=2) for k in range(4)]

    def pool_consts_ffn1(pool):
        nc.gpsimd.iota(iota64[:, :], [[1, E1]], base=0, channel_multiplier=0, allow_small_or_imprecise_dtypes=True
                       ).then_inc(consts_ready, 1)
        nc.gpsimd.iota(e_col[:, :], [[1, 1]], base=0, channel_multiplier=1, allow_small_or_imprecise_dtypes=True
                       ).then_inc(consts_ready, 1)

    def sp_load_ffn1(sp):
        for p in range(2):
            sp.wait_ge(A1.vs_loaded[p], 32 * (B // 2))
        sp.dma_start(router_rows, a["L1_ffn_router_w"]).then_inc(router_loaded, 16)
        sp.dma_start(e_bias[:, :], a["L1_ffn_e_bias"].rearrange("(o e) -> o e", o=1).broadcast_to([NQ, E1])
                     ).then_inc(router_loaded, 16)
        for dst, name in ((swg, "SWg"), (swu, "SWu"), (swd, "SWd")):
            sp.dma_start(dst, a["L1_ffn_" + name].rearrange("(c p) n -> p c n", p=P)).then_inc(sh_loaded, 16)

    def sp_experts1(sp):
        sp.wait_ge(list_ready, 1)
        total = sp.value_load(n_used[0:1, 0:1], min_val=0, max_val=E1)
        with sp.Fori(0, E1 // (2 * PAIRS)) as o:
            with sp.If(2 * PAIRS * o < total):
                with sp.Fori(0, PAIRS) as k:
                    i = o * PAIRS + k
                    with sp.If(2 * i < total):
                        for p in range(2):
                            n = 2 * i + p
                            e = sp.value_load(expert_list[0:1, bass.ds(n, 1)], min_val=0, max_val=E1 - 1)
                            sp.wait_ge(we_split, 4 * i + p + 3)
                            for at, name in ((0, "Wg"), (2 * H1, "Wu")):
                                sp.dma_start(we[p][:, at:at + 2 * H1].rearrange("q (c h) -> q c h", c=2),
                                             a["L1_ffn_" + name].rearrange("e (c q) h -> q (e c) h", q=P)[
                                                 :, bass.ds(2 * e, 2), :]).then_inc(we_loaded[p], 16)
                            sp.dma_start(we[p][:, WGU:WALL], a["L1_ffn_Wd"].rearrange("e q d -> (e q) d")[
                                bass.ds(e * H1, H1), :]).then_inc(we_loaded[p], 16)

    def pe_gate1(pe):
        pe.wait_ge(router_loaded, 32)
        pe.wait_ge(A1.added, B + 1)
        for c in range(2):
            last = nc.tensor.transpose(r_wT_ps[:, c, :], router_rows[:, c * P:(c + 1) * P], ident[0:E1, 0:E1])
        last.then_inc(r_wT_in_psum, 1)
        pe.wait_ge(r_wT_ready, 1)
        with pe.Fori(0, B) as b:
            pe.wait_ge(xn_ready, 3 * B + b + 1)
            pe.wait_ge(xnT_ready, 3 * B + b)
            pe.wait_ge(xn_kept, B + b)
            for c in range(2):
                last = nc.tensor.transpose(r_xnT_ps[:, c, :], xn[:, c * P:(c + 1) * P], ident[0:NQ, 0:NQ])
            last.then_inc(xnT_in_psum, 1)
            pe.wait_ge(xnT_ready, 3 * B + b + 1)
            for c in range(2):
                last = nc.tensor.matmul(r_logits_ps[:, b, :], xnT[:, c, :], routerT[:, c, :], start=(c == 0),
                                        stop=(c == 1))
            last.then_inc(gate_logits, 1)

    def pe_shared(pe):
        pe.wait_ge(sh_loaded, 48)
        pe.wait_ge(xn_kept, 2 * B)
        for m in range(2):
            for half in range(2):
                for k, w in enumerate((swg, swu)):
                    if m == 1:
                        pe.wait_ge((sh_g_taken, sh_u_taken)[k], half + 1)
                    for c in range(2):
                        last = nc.tensor.matmul(gu_ps[2 * half + k], w[:, c, m * P:(m + 1) * P],
                                                xnT_all[:, c, half * HT:(half + 1) * HT], start=(c == 0), stop=(c == 1))
                    last.then_inc(sh_in_psum, 1)
        pe.wait_ge(sh_h_ready, 4)
        for b in range(B):
            for m in range(2):
                last = nc.tensor.matmul(sh_y_ps[b // 2][:, b % 2, :], sh_hT[:, m, b * NQ:(b + 1) * NQ], swd[:, m, :],
                                        start=(m == 0), stop=(m == 1))
            if b % 2 == 1:
                last.then_inc(sh_y_in_psum, 1)

    def pe_list1(pe):
        pe.wait_ge(r_taken, 1)
        nc.tensor.matmul(r_count_ps, taken[:, :], ones_sq[0:NQ, 0:1], start=True, stop=True).then_inc(r_counted, 1)
        pe.wait_ge(r_used, 1)
        nc.tensor.matmul(r_before_ps, earlier[0:E1, 0:E1], used[:, 0:1], start=True, stop=True)
        nc.tensor.matmul(r_total_ps, ones_sq[0:E1, 0:E1], used[:, 0:1], start=True, stop=True).then_inc(r_placed, 1)
        pe.wait_ge(r_place_ready, 1)
        nc.tensor.matmul(r_list_ps, e_col[:, 0:1], place[:, :], start=True, stop=True).then_inc(r_listed, 1)

    def act_shared(act):
        act_std(act, 5)
        act.wait_ge(r_wT_in_psum, 1)
        nc.scalar.activation(routerT, r_wT_ps, ACT.Copy).then_inc(r_wT_ready, 1)
        with act.Fori(0, B) as b:
            act.wait_ge(xnT_ready, 3 * B + b + 1)
            nc.scalar.activation(xnT_all[:, :, bass.ds(b * NQ, NQ)], xnT[:, :, :], ACT.Copy).then_inc(xn_kept, 1)
        act.wait_ge(xn_kept, 2 * B)
        nc.scalar.activation(xT_high, xnT_all, ACT.Copy).then_inc(x_high_ready, 1)
        act.wait_ge(gate_logits, 2 * B)
        nc.scalar.activation(scores1, r_logits_ps, ACT.Sigmoid).then_inc(r_scores, 1)
        for m in range(2):
            for half in range(2):
                n = 2 * m + half
                if m == 1:
                    act.wait_ge(sh_h_ready, half + 1)
                act.wait_ge(sh_in_psum, 2 * n + 1)
                nc.scalar.activation(sh_g[half], gu_ps[2 * half], ACT.Silu).then_inc(sh_g_taken, 1)
                act.wait_ge(sh_in_psum, 2 * n + 2)
                nc.scalar.activation(sh_u[half], gu_ps[2 * half + 1], ACT.Copy).then_inc(sh_u_taken, 1)
        for k in range(4):
            act.wait_ge(sh_y_in_psum, k + 1)
            nc.scalar.activation(sh_y[:, 2 * k:2 * k + 2, :], sh_y_ps[k], ACT.Copy).then_inc(sh_y_taken, 1)

    def pool_shared(pool):
        for m in range(2):
            for half in range(2):
                n = 2 * m + half
                pool.wait_ge(sh_g_taken, n + 1)
                pool.wait_ge(sh_u_taken, n + 1)
                nc.gpsimd.tensor_tensor(sh_hT[:, m, half * HT:(half + 1) * HT], sh_g[half], sh_u[half], ALU.mult
                                        ).then_inc(sh_h_ready, 1)
        pool.wait_ge(sh_y_taken, 4)
        nc.gpsimd.tensor_tensor(x[:, 1:B + 1, :], x[:, 1:B + 1, :], sh_y, ALU.add).then_inc(sh_added, 1)

    def dve_gate1(dve):
        dve.wait_ge(x3_stats, B)
        dve_ln_finish(dve, 5)
        with dve.Fori(0, B) as b:
            dve.wait_ge(xnT_in_psum, 3 * B + b)
            nc.vector.tensor_scalar(xn[:, :], x[:, b + 1, :], mv[:, b, 0:1], rstd[:, bass.ds(b, 1)], ALU.subtract,
                                    ALU.mult).then_inc(xn_ready, 1)
            dve.wait_ge(xnT_in_psum, 3 * B + b + 1)
            dve.wait_ge(gate_logits, B + b)
            dve.wait_ge(xn_kept, B + b)
            nc.vector.tensor_copy(xnT[:, :, :], r_xnT_ps).then_inc(xnT_ready, 1)

    def dve_route1(dve):

        dve.wait_ge(r_scores, 1)
        dve.wait_ge(router_loaded, 32)
        dve.wait_ge(consts_ready, N_CONSTS + N_MOE_CONSTS + 5 + 2)
        step(dve, nc.vector.tensor_tensor(sfc, scores1, e_bias[:, :].unsqueeze(1).broadcast_to([NQ, B, E1]), ALU.add))
        eights = sfc.rearrange("q b (g k) -> q (b g) k", k=G1)
        grid = lambda k, n: group2[:, k, 0:B * G1 * n].rearrange("q (g n) -> q g n", n=n)
        high, low = grid(0, 4), grid(1, 4)
        nc.vector.tensor_tensor(high, eights[:, :, 0:4], eights[:, :, 4:8], ALU.max)
        step(dve, nc.vector.tensor_tensor(low, eights[:, :, 0:4], eights[:, :, 4:8], ALU.min))
        for n, to in ((2, 2), (1, 0)):
            top, second = grid(to, n), grid(to + 1, n)
            below = work1.rearrange("q b e -> q (b e)")[:, 0:B * G1 * n].rearrange("q (g n) -> q g n", n=n)
            nc.vector.tensor_tensor(top, high[:, :, 0:n], high[:, :, n:2 * n], ALU.max)
            nc.vector.tensor_tensor(below, high[:, :, 0:n], high[:, :, n:2 * n], ALU.min)
            step(dve, nc.vector.tensor_tensor(second, low[:, :, 0:n], low[:, :, n:2 * n], ALU.max))
            step(dve, nc.vector.tensor_tensor(second, second, below, ALU.max))
            high, low = top, second
        step(dve, nc.vector.tensor_tensor(group_sum[:, :, :].rearrange("q b (g o) -> q (b g) o", o=1), high, low, ALU.add))
        ij = lambda t: t.rearrange("q b (i j) -> q b i j", j=G1)
        mine = group_sum[:, :, :].unsqueeze(3).broadcast_to([NQ, B, G1, G1])
        other = group_sum[:, :, :].unsqueeze(2).broadcast_to([NQ, B, G1, G1])
        nc.vector.tensor_tensor(ij(work1), other, mine, ALU.is_gt)
        step(dve, nc.vector.tensor_tensor(ij(work2), other, mine, ALU.is_equal))
        step(dve, nc.vector.tensor_tensor(ij(work2), ij(work2),
                                     below8[0:NQ, :, :].unsqueeze(1).broadcast_to([NQ, B, G1, G1]), ALU.mult))
        step(dve, nc.vector.tensor_tensor(work1, work1, work2, ALU.add))
        step(dve, nc.vector.tensor_reduce(group_kept[:, :, :], ij(work1), AX.X, ALU.add))
        step(dve, nc.vector.tensor_scalar(group_kept[:, :, :], group_kept[:, :, :], float(TOPG), None, ALU.is_lt))
        step(dve, nc.vector.tensor_tensor(sfc.rearrange("q b (g k) -> q b g k", k=G1),
                                     sfc.rearrange("q b (g k) -> q b g k", k=G1),
                                     group_kept[:, :, :].unsqueeze(3).broadcast_to([NQ, B, G1, G1]), ALU.mult))
        for b in range(B):
            last = nc.vector.max(top8[:, b, :], sfc[:, b, :])
        step(dve, last)
        for b in range(B):
            last = nc.vector.match_replace(out=picked[:, b, :], in_to_replace=top8[:, b, :], in_values=sfc[:, b, :],
                                           imm_value=-FLT_MAX)
        step(dve, last)
        step(dve, nc.vector.tensor_scalar(picked, picked, -FLT_MAX, None, ALU.is_equal))
        step(dve, nc.vector.tensor_reduce(taken[:, :], picked.rearrange("q b e -> q e b"), AX.X, ALU.add))
        dve.sem_inc(r_taken, 1)
        step(dve, nc.vector.tensor_tensor(work1, scores1, picked, ALU.mult))
        step(dve, nc.vector.tensor_reduce(weight_sum[:, :], work1, AX.X, ALU.add))
        step(dve, nc.vector.tensor_scalar(weight_sum[:, :], weight_sum[:, :], 1e-20, None, ALU.add))
        step(dve, nc.vector.reciprocal(weight_sum[:, :], weight_sum[:, :]))
        step(dve, nc.vector.scalar_tensor_tensor(coef, work1, SCALE2, weight_sum[:, :].unsqueeze(2).broadcast_to([NQ, B, E1]),
                                            ALU.mult, ALU.mult))
        dve.wait_ge(r_counted, 1)
        nc.vector.tensor_scalar(used[:, 0:1], r_count_ps, 0.0, None, ALU.is_gt).then_inc(r_used, 1)
        dve.wait_ge(r_placed, 1)
        step(dve, nc.vector.tensor_scalar(used[:, 2:3], r_total_ps, e_col[:, 0:1], r_before_ps, ALU.add, ALU.subtract))
        step(dve, nc.vector.tensor_tensor(used[:, 1:2], r_before_ps, used[:, 2:3], ALU.subtract))
        step(dve, nc.vector.scalar_tensor_tensor(used[:, 1:2], used[:, 1:2], used[:, 0:1], used[:, 2:3], ALU.mult, ALU.add))
        nc.vector.tensor_copy(n_used[:, :], r_total_ps[0:1, :])
        nc.vector.tensor_scalar(place[:, :], iota64[:, :], used[:, 1:2], None, ALU.is_equal).then_inc(r_place_ready, 1)
        dve.wait_ge(r_listed, 1)
        nc.vector.tensor_copy(expert_list[:, :], r_list_ps).then_inc(list_ready, 1)

    def pe_experts1(pe):
        pe.wait_ge(list_ready, 1)
        pe.wait_ge(sh_y_taken, 4)
        pe.wait_ge(x_low_ready, 1)
        pe.sem_inc(gu_in_psum, 8)
        pe.sem_inc(y1_in_psum, 8)

        def gate_up(i, p):
            n = 2 * i + p
            pe.wait_ge(we_split, 4 * i + p + 1 + 4)
            for half in range(2):
                tok = slice(half * HT, (half + 1) * HT)
                pe.wait_ge(h1_full, 2 * n + half + 1)
                for k in range(2):
                    for c in range(2):
                        col = slice((2 * k + c) * H1, (2 * k + c + 1) * H1)
                        ps = gu_ps[2 * half + k]
                        nc.tensor.matmul(ps, we_high[p][:, col], xT_high[:, c, tok], start=(c == 0), stop=False)
                        nc.tensor.matmul(ps, we_high[p][:, col], xT_low[:, c, tok], start=False, stop=False)
                        last = nc.tensor.matmul(ps, we_low[p][:, col], xT_high[:, c, tok], start=False, stop=(c == 1))
                    last.then_inc(gu_in_psum, 1)

        def down(i, p):
            n = 2 * i + p
            pe.wait_ge(we_split, 4 * i + 2 + p + 1 + 4)
            for k in range(4):
                if k % 2 == 0:
                    pe.wait_ge(h1_ready, 2 * n + k // 2 + 1 + 2)
                pe.wait_ge(y1_added, 4 * n + k + 1)
                for bb in range(2):
                    b = 2 * k + bb
                    tok = slice(b * NQ, (b + 1) * NQ)
                    ps = y1_ps[k][:, bb, :]
                    nc.tensor.matmul(ps, h1_high[p][:, tok], we_high[p][:, WGU:WALL], start=True, stop=False)
                    nc.tensor.matmul(ps, h1_high[p][:, tok], we_low[p][:, WGU:WALL], start=False, stop=False)
                    last = nc.tensor.matmul(ps, h1_low[p][:, tok], we_high[p][:, WGU:WALL], start=False, stop=True)
                last.then_inc(y1_in_psum, 1)

        total = pe.value_load(n_used[0:1, 0:1], min_val=0, max_val=E1)
        with pe.Fori(0, E1 // (2 * PAIRS)) as o:
            with pe.If(2 * PAIRS * o < total):
                with pe.Fori(0, PAIRS) as k:
                    i = o * PAIRS + k
                    with pe.If(2 * i < total):
                        for p in range(2):
                            gate_up(i, p)
                        for p in range(2):
                            down(i, p)

    def act_experts1(act):
        def split_gate_up(i, p):
            act.wait_ge(we_loaded[p], 48 * i + 48)
            act.wait_ge(gu_in_psum, 4 * (2 * i + p) + 4)
            nc.scalar.activation(we_high[p][:, 0:WGU], we[p][:, 0:WGU], ACT.Copy).then_inc(we_high_ready, 1)

        def split_down(i, p):
            act.wait_ge(y1_in_psum, 4 * (2 * i + p) + 4)
            nc.scalar.activation(we_high[p][:, WGU:WALL], we[p][:, WGU:WALL], ACT.Copy).then_inc(we_high_ready, 1)

        def hidden(i, p):
            n = 2 * i + p
            for half in range(2):
                act.wait_ge(gu_in_psum, 4 * n + 2 * half + 1 + 8)
                act.wait_ge(h1_full, 2 * n + half + 1)
                nc.scalar.activation(g_act[half], gu_ps[2 * half], ACT.Silu).then_inc(silu_done, 1)
                act.wait_ge(h1_full, 2 * n + half + 1 + 2)
                tok = slice(half * HT, (half + 1) * HT)
                nc.scalar.activation(h1_high[p][:, tok], h1T[:, tok], ACT.Copy).then_inc(h1_high_ready, 1)

        act.wait_ge(list_ready, 1)
        total = act.value_load(n_used[0:1, 0:1], min_val=0, max_val=E1)
        with act.Fori(0, E1 // (2 * PAIRS)) as o:
            with act.If(2 * PAIRS * o < total):
                with act.Fori(0, PAIRS) as k:
                    i = o * PAIRS + k
                    with act.If(2 * i < total):
                        for p in range(2):
                            split_gate_up(i, p)
                        for p in range(2):
                            split_down(i, p)
                        for p in range(2):
                            hidden(i, p)

    def pool_experts1(pool):
        def split(i, p, part, cols):
            pool.wait_ge(we_high_ready, 4 * i + 2 * part + p + 1)
            nc.gpsimd.tensor_tensor(we_low[p][:, cols], we[p][:, cols], we_high[p][:, cols].bitcast(F32), ALU.subtract
                                    ).then_inc(we_split, 1)

        def hidden(i, p):
            n = 2 * i + p
            for half in range(2):
                tok = slice(half * HT, (half + 1) * HT)
                pool.wait_ge(h1_high_ready, 2 * n + half + 1)
                pool.wait_ge(y1_in_psum, 4 * n + 4)
                nc.gpsimd.tensor_tensor(h1_low[p][:, tok], h1T[:, tok], h1_high[p][:, tok].bitcast(F32), ALU.subtract
                                        ).then_inc(h1_ready, 1)

        pool.wait_ge(x_high_ready, 1)
        nc.gpsimd.tensor_tensor(xT_low, xnT_all, xT_high.bitcast(F32), ALU.subtract).then_inc(x_low_ready, 1)
        pool.wait_ge(list_ready, 1)
        pool.sem_inc(we_split, 4)
        pool.sem_inc(h1_ready, 2)
        total = pool.value_load(n_used[0:1, 0:1], min_val=0, max_val=E1)
        with pool.Fori(0, E1 // (2 * PAIRS)) as o:
            with pool.If(2 * PAIRS * o < total):
                with pool.Fori(0, PAIRS) as k:
                    i = o * PAIRS + k
                    with pool.If(2 * i < total):
                        for p in range(2):
                            split(i, p, 0, slice(0, WGU))
                        for p in range(2):
                            split(i, p, 1, slice(WGU, WALL))
                        for p in range(2):
                            hidden(i, p)

    def dve_experts1(dve):
        def hidden(i, p):
            n = 2 * i + p
            for half in range(2):
                dve.wait_ge(silu_done, 2 * n + half + 1)
                dve.wait_ge(gu_in_psum, 4 * n + 2 * half + 2 + 8)
                dve.wait_ge(h1_ready, 2 * n + half + 1)
                nc.vector.tensor_tensor(h1T[:, half * HT:(half + 1) * HT], g_act[half], gu_ps[2 * half + 1], ALU.mult
                                        ).then_inc(h1_full, 1)

        def add(i, p):
            n = 2 * i + p
            e = dve.value_load(expert_list[0:1, bass.ds(n, 1)], min_val=0, max_val=E1 - 1)
            for k in range(4):
                dve.wait_ge(y1_in_psum, 4 * n + k + 1 + 8)
                dve.wait_ge(y1_added, 4 * n + k + 1)
                for bb in range(2):
                    b = 2 * k + bb
                    last = nc.vector.scalar_tensor_tensor(
                        x[:, b + 1, :], y1_ps[k][:, bb, :], coef[:, b, bass.ds(e, 1)], x[:, b + 1, :],
                        ALU.mult, ALU.add)
                last.then_inc(y1_added, 1)

        dve.wait_ge(list_ready, 1)
        dve.wait_ge(sh_added, 1)
        dve.sem_inc(h1_full, 2)
        dve.sem_inc(y1_added, 4)
        total = dve.value_load(n_used[0:1, 0:1], min_val=0, max_val=E1)
        with dve.Fori(0, E1 // (2 * PAIRS)) as o:
            with dve.If(2 * PAIRS * o < total):
                with dve.Fori(0, PAIRS) as k:
                    i = o * PAIRS + k
                    with dve.If(2 * i < total):
                        for p in range(2):
                            hidden(i, p)
                        for p in range(2):
                            add(i, p)
        nc.vector.memset(row_max[:, :], 0.0).then_inc(x_final, 1)

    with nc.Block() as block:
        @block.sync
        def _(sp):
            sp_load0(sp)
            sp_project0(sp)
            sp_load1(sp)

            def v0_ready(e):
                e.wait_ge(v_stored, 2 * B)
                e.wait_ge(consts_ready, N_CONSTS)
            sp_attend(sp, A0, v0_ready)
            sp_load_moe(sp)
            sp_load1_weights(sp)
            sp_experts(sp)
            sp_project1(sp)

            def v1_ready(e):
                e.wait_ge(v1_stored, 3 * B)
                e.wait_ge(null_v_stored, 16 * 8)
            sp_attend(sp, A1, v1_ready)
            sp_load_ffn1(sp)
            sp_experts1(sp)
            sp.wait_ge(x_final, 1)
            sp.dma_start(a["out"].rearrange("b q d -> q b d"), x[:, 1:B + 1, :]).then_inc(out_stored, 16)
            sp.wait_ge(out_stored, 16)

        @block.gpsimd
        def _(pool):
            pool_consts(pool)

            def q0_ready(e):
                e.wait_ge(q_stored, 2 * B)
                e.wait_ge(consts_ready, N_CONSTS)
            pool_consts_moe(pool)
            pool_consts1(pool)
            pool_consts_ffn1(pool)
            pool_attend(pool, A0, q0_ready, headmask[:, :])
            pool_dispatch(pool)
            pool_combine(pool)
            pool_clear1(pool)
            pool_mask_clear(pool)

            def q1_ready(e):
                e.wait_ge(qT1_stored, B)
                e.wait_ge(kT1_in_psum, 3 * B)
                e.wait_ge(kq1_cleared, 2)
            pool_attend(pool, A1, q1_ready, halfmask[:, :])
            pool_shared(pool)
            pool_experts1(pool)

        @block.vector
        def _(dve):
            dve_project0(dve)
            dve_attend(dve, A0)
            dve_gate(dve)
            dve_experts(dve)
            dve_project1(dve)
            dve_attend(dve, A1)
            dve_add1(dve)
            dve_gate1(dve)
            dve_route1(dve)
            dve_experts1(dve)

        @block.scalar
        def _(act):
            act_project0(act)
            act_attend(act, A0)
            act_gate(act)
            act_experts(act)
            act_project1(act)
            act_attend(act, A1)
            act_add1(act)
            act_shared(act)
            act_experts1(act)

        @block.tensor
        def _(pe):
            pe_project0(pe)

            def p0_ready(e):
                e.wait_ge(q_stored, 2 * B)
                e.wait_ge(k_stored, 2 * B)
                e.wait_ge(v_stored, 2 * B)
                e.wait_ge(A0.out_cleared, 1)
                e.wait_ge(wo0_loaded, 32)
            pe_attend(pe, A0, p0_ready)
            pe_gate(pe)
            pe_experts(pe)
            pe_project1(pe)

            def p1_ready(e):
                e.wait_ge(qT1_stored, B)
                e.wait_ge(kT1_stored, 3 * B)
                e.wait_ge(v1_stored, 3 * B)
                e.wait_ge(null_k_stored, 1)
                e.wait_ge(kq1_cleared, 2)
            pe_attend(pe, A1, p1_ready)
            pe_gate1(pe)
            pe_shared(pe)
            pe_list1(pe)
            pe_experts1(pe)


_INS = ["x", "ctx_768", "mask_BxS2_bf1", "L0_xattn_Wq", "L0_xattn_bq", "L0_xattn_Wk", "L0_xattn_bk", "L0_xattn_Wv",
        "L0_xattn_bv", "L0_xattn_Wo", "L0_xattn_bo", "L0_ffn_Wg", "L0_ffn_bg", "L0_ffn_W1", "L0_ffn_b1", "L0_ffn_W2",
        "L0_ffn_b2", "L1_xattn_g_norm", "L1_xattn_Wq", "L1_xattn_Wkv", "L1_xattn_null_kv", "L1_xattn_q_scale",
        "L1_xattn_k_scale", "L1_xattn_Wo", "L1_xattn_g_out", "L1_ffn_router_w", "L1_ffn_e_bias", "L1_ffn_Wg",
        "L1_ffn_Wu", "L1_ffn_Wd", "L1_ffn_SWg", "L1_ffn_SWu", "L1_ffn_SWd"]


def kernel(**inputs):
    import concourse.bacc as _bacc
    from concourse.bass_utils import run_bass_kernel_spmd as _run

    nc = _bacc.Bacc("TRN2", target_bir_lowering=False, num_devices=1)
    arrays, aps = {}, {}
    for name in _INS:
        array = np.ascontiguousarray(inputs[name])
        if array.dtype == np.bool_:
            array = array.view(np.uint8)
        arrays[f"in_{name}_dram"] = array
        aps[name] = nc.dram_tensor(f"in_{name}_dram", array.shape, mybir.dt.from_np(array.dtype),
                                   kind="ExternalInput").ap()
    aps["out"] = nc.dram_tensor("out_0_dram", (B, NQ, D), F32, kind="ExternalOutput").ap()
    build(nc, aps)
    r = _run(nc, [arrays], core_ids=[0])
    return r.results[0]["out_0_dram"]
```

```python
import numpy as np
import concourse.bass as bass
from concourse import mybir

F32 = mybir.dt.float32
F32R = mybir.dt.float32r
I32 = mybir.dt.int32
U32 = mybir.dt.uint32
U8 = mybir.dt.uint8
ACT = mybir.ActivationFunctionType
ALU = mybir.AluOpType
AX = mybir.AxisListType

P = 128
B, NQ, D = 8, 100, 256
NKV, DC = 361, 192
DCC = DC // 2
FULL, TAIL = 2, NKV - 2 * P
EPS = 1e-5
CLAMP = 10000.0
SCALE0 = 16 ** -0.5
LOOK = 3
AHEAD = 2
NPB = 4
SLOT_V = 3 * 512


def build(nc, a):
    sb = nc.alloc_sbuf_tensor
    sem = nc.alloc_semaphore

    psum = nc.alloc_psum_tensor("psum", [P, 8, 512], F32)
    x = sb("x", [NQ, B + 1, D], F32)
    ident = sb("ident", [P, P], F32)
    ones_row = sb("ones_row", [1, P], F32)
    eps_col = sb("eps_col", [P, 1], F32)
    stats = sb("stats", [NQ, B + 1, 6], F32)
    mv = sb("mv", [NQ, B, 2], F32)
    rstd = sb("rstd", [NQ, B], F32)
    std = sb("std", [NQ, B], F32)
    keys_at = nc.sbuf_base
    kT_all = sb("kT_all", [P, 4 * (B + 1) * (NKV + 1)], F32)
    vals_at = nc.sbuf_base
    v_all = sb("v_all", [P, B, 3, 512], F32)
    qT_all = sb("qT_all", [P, 4 * (B + 1) * NQ], F32)
    qm, vs, qm_at, vs_at = [], [], [], []
    for p in range(2):
        qm_at.append(nc.sbuf_base)
        qm.append(sb(f"qm{p}", [P, 16, NQ], F32))
    for p in range(2):
        vs_at.append(nc.sbuf_base)
        vs.append(sb(f"vs{p}", [P, 3, 512], F32))
    probs_at = nc.sbuf_base
    probs = sb("probs", [NQ, NPB, 2, NKV + 1], F32)
    negmax = sb("negmax", [NQ, NPB, 2], F32)
    sums = sb("sums", [NQ, 2, 16], F32)
    inv_sums = sb("inv_sums", [NQ, 16], F32)
    probsT = [sb(f"probsT{p}", [P, 3, 2 * NQ], F32) for p in range(2)]
    oT = sb("oT", [P, 4, NQ], F32)
    o_tok = sb("o_tok", [NQ, 512], F32)
    o_tokT = sb("o_tokT", [P, 4, NQ], F32)

    ctx_nat = [sb(f"ctx_nat{p}", [P, 3, DC], F32) for p in range(2)]
    ctxT_at = nc.sbuf_base
    ctxT = sb("ctxT", [DCC + 1, 2, NKV], F32)
    xn = sb("xn", [NQ, D], F32)
    xnT = sb("xnT", [P, 2, NQ], F32)

    headmask = sb("headmask", [P, 8], F32)
    early = sb("early", [P, (B + 1) * D], F32)
    wq0, wk0, wv0, wo0 = (early[:, k * 2 * D:(k + 1) * 2 * D].rearrange("p (c n) -> p c n", c=2) for k in range(4))
    wk0 = wk0[0:DCC]
    wv0 = wv0[0:DCC + 1]
    z_all = early[0:NQ, :].rearrange("q (b d) -> q b d", d=D)
    bq0 = sb("bq0", [P, 2], F32)
    bq0s = sb("bq0s", [P, 2], F32)
    bk0 = sb("bk0", [P, 2], F32)
    bo0 = sb("bo0", [1, D], F32)

    E0, H0 = 8, 1024
    HC = H0 // P
    NBLK = (B * NQ + E0 * (P - 1)) // P
    keys_arena = kT_all[:, :]
    vals_arena = v_all[:, :, :, :].rearrange("p b t n -> p (b t n)")

    def carve(arena, at, shape):
        n = int(np.prod(shape))
        view = arena[:, at[0]:at[0] + n]
        at[0] += n
        names = " ".join("abc"[:len(shape)])
        return view.rearrange(f"p ({names}) -> p {names}", **{k: v for k, v in zip("abc", shape)})

    def carve_r(name, base, at, shape):
        n = int(np.prod(shape))
        view = nc.alloc_sbuf_tensor_at(name, [P, n], F32R, offset=base + 4 * at[0])[:, :]
        at[0] += n
        names = " ".join("abc"[:len(shape)])
        return view.rearrange(f"p ({names}) -> p {names}", **{k: v for k, v in zip("abc", shape)})
    at_k, at_v = [0], [0]
    w1_e = [carve(vals_arena, at_v, (2, H0)) for _ in range(2)]
    w2_e = [carve(vals_arena, at_v, (HC, D)) for _ in range(2)]
    xn_all = carve(keys_arena, at_k, (B, D))[0:NQ]
    xnT0 = carve(keys_arena, at_k, (2, B * NQ))
    xs_rows = [carve(keys_arena, at_k, (D,)) for _ in range(2)]
    xsT = [carve(keys_arena, at_k, (2, P)) for _ in range(2)]
    hT = [carve(keys_arena, at_k, (HC, P)) for _ in range(2)]
    ys_rows = [carve(keys_arena, at_k, (D,)) for _ in range(2)]
    b1_rows = [sb(f"b1_rows{p}", [HC, P], F32) for p in range(2)]
    b1_col = [sb(f"b1_col{p}", [P, HC], F32) for p in range(2)]
    b2_row = [sb(f"b2_row{p}", [1, D], F32) for p in range(2)]
    wg0 = sb("wg0", [P, 2, E0], F32)
    bg0 = sb("bg0", [1, E0], F32)
    earlier = sb("earlier", [NQ, NQ], F32)
    ones_sq = sb("ones_sq", [NQ, P], F32)
    below8 = sb("below8", [P, 8, 8], F32)
    iota16 = sb("iota16", [P, 16], F32)
    logits = sb("logits", [NQ, B, E0], F32)
    top_logit = sb("top_logit", [NQ, B], F32)
    top_weight = sb("top_weight", [NQ, B], F32)
    choice = sb("choice", [NQ, B, E0], F32)
    route_a = sb("route_a", [P, B * E0 * 8], F32)
    route_b = sb("route_b", [P, B, E0], F32)
    counts = sb("counts", [P, B, E0], F32)
    per_expert = sb("per_expert", [P, 4, E0], F32)
    block_expert = sb("block_expert", [P, NBLK], F32)
    n_pairs = sb("n_pairs", [P, 1], I32)
    block_expert_i = sb("block_expert_i", [P, NBLK], I32)
    slot_f = sb("slot_f", [NQ, B], F32)
    slot = sb("slot", [NQ, B], U32)
    zeros = sb("zeros", [P, D], F32)
    xs_dram = nc.dram_tensor("xs_dram", [NBLK * P, D], F32, kind="Internal").ap()
    ys_dram = nc.dram_tensor("ys_dram", [NBLK * P, D], F32, kind="Internal").ap()

    HD1, SCALE1 = 64, 8.0
    FLT_MAX = float(np.finfo(np.float32).max)
    flat = lambda t: t[:, :, :].rearrange("p a b -> p (a b)")
    two = lambda v: v[:, 0:1024].rearrange("p (c n) -> p c n", c=2)
    wk1, wv1 = (two(vals_arena[:, 6 * SLOT_V + k * 1024:])[0:DCC] for k in range(2))
    wk1_high, wk1_low = (two(nc.alloc_sbuf_tensor_at(f"wk1_{n}", [DCC, 1024], F32R, offset=at)[:, :])
                         for n, at in zip(("high", "low"), qm_at))
    wv1_high, wv1_low = (two(nc.alloc_sbuf_tensor_at(f"wv1_{n}", [DCC, 1024], F32R, offset=at)[:, :])
                         for n, at in zip(("high", "low"), vs_at))
    wq1 = two(early[:, :])
    k_tok_full = early[:, 1024:2048].rearrange("p (t n) -> p t n", t=2)
    k_tok = [k_tok_full[:, 0, :], k_tok_full[:, 1, :], flat(probsT[0])[:, 0:512]]
    probs_row = probs[:, :, :, :].rearrange("q a b n -> q (a b n)")
    y_tok = probs_row[:, 0:2 * D].rearrange("q (p d) -> q p d", p=2)
    y_row = probs_row[:, 2 * D:3 * D]
    ctxT_high = nc.alloc_sbuf_tensor_at("ctxT_high", [DCC, 2, NKV], F32R, offset=ctxT_at)
    ctxT_low = nc.alloc_sbuf_tensor_at("ctxT_low", [DCC, 2, NKV], F32R, offset=probs_at + 4 * 3 * D)
    mask_bias = [flat(ctx_nat[p])[0:NQ, 0:NKV + 1] for p in range(2)]
    wo1 = sb("wo1", [P, 4, D], F32)
    g_norm = sb("g_norm", [NQ, D], F32)
    g_out = sb("g_out", [NQ, D], F32)
    turn = sb("turn", [NQ, NPB], F32)
    pool_turn = sb("pool_turn", [1, 1], F32)
    flt_max = sb("flt_max", [NQ, 1], F32)
    mask_u8 = sb("mask_u8", [NQ, B + 1, NKV], U8)
    null_row = sb("null_row", [P, HD1], F32)
    null_col = sb("null_col", [P, 1], F32)
    null_ss = sb("null_ss", [P, 1], F32)
    q_scale_col = sb("q_scale_col", [P, 1], F32)
    k_scale_col = sb("k_scale_col", [P, 1], F32)
    halfmask = sb("halfmask", [P, 2], F32)
    key_ss = sb("key_ss", [P, 3, 8], F32)
    q_ss = sb("q_ss", [NQ, 8], F32)
    row_max = sb("row_max", [NQ, B], F32)
    top_out = sb("top_out", [NQ, 1], F32)

    E1, H1, HS = 64, 128, 256
    G1, TOPG, SCALE2 = 8, 4, 2.5
    HT = B * NQ // 2
    PAIRS = 4
    at_k, at_v = [0], [0]
    xnT_all = carve(keys_arena, at_k, (2, B * NQ))
    xT_high = carve_r("xT_high", keys_at, at_k, (2, B * NQ))
    xT_low = carve_r("xT_low", keys_at, at_k, (2, B * NQ))
    g_act = [carve(keys_arena, at_k, (HT,)) for _ in range(2)]
    sh_hT = carve(keys_arena, at_k, (2, B * NQ))
    sh_g = [carve(keys_arena, at_k, (HT,)) for _ in range(2)]
    sh_u = [carve(keys_arena, at_k, (HT,)) for _ in range(2)]
    sh_y = carve(keys_arena, at_k, (B, D))[0:NQ]
    scores1 = carve(keys_arena, at_k, (B, E1))[0:NQ]
    sfc = carve(keys_arena, at_k, (B, E1))[0:NQ]
    picked = carve(keys_arena, at_k, (B, E1))[0:NQ]
    work1 = carve(keys_arena, at_k, (B, E1))[0:NQ]
    swg = carve(vals_arena, at_v, (2, HS))
    swu = carve(vals_arena, at_v, (2, HS))
    swd = carve(vals_arena, at_v, (2, D))
    router_rows = carve(vals_arena, at_v, (D,))[0:E1]
    routerT = carve(vals_arena, at_v, (2, E1))
    WGU, WALL = 4 * H1, 4 * H1 + D
    we = [carve(vals_arena, at_v, (WALL,)) for _ in range(2)]
    we_high = [carve_r(f"we_high{p}", vals_at, at_v, (WALL,)) for p in range(2)]
    we_low = [carve_r(f"we_low{p}", vals_at, at_v, (WALL,)) for p in range(2)]
    h1T = carve(vals_arena, at_v, (B * NQ,))
    h1_high = [carve_r(f"h1_high{p}", vals_at, at_v, (B * NQ,)) for p in range(2)]
    group2 = vals_arena[0:NQ, at_v[0]:at_v[0] + 4 * B * G1 * 4].rearrange("q (k n) -> q k n", k=4)
    h1_low = [carve_r(f"h1_low{p}", vals_at, at_v, (B * NQ,)) for p in range(2)]
    coef = carve(vals_arena, at_v, (B, E1))[0:NQ]
    work2 = carve(vals_arena, at_v, (B, E1))[0:NQ]
    e_bias = carve(vals_arena, at_v, (E1,))[0:NQ]
    iota64 = sb("iota64", [E1, E1], F32)
    e_col = sb("e_col", [E1, 1], F32)
    group_sum = carve(vals_arena, at_v, (B, G1))[0:NQ]
    group_kept = carve(vals_arena, at_v, (B, G1))[0:NQ]
    top8 = carve(vals_arena, at_v, (B, 8))[0:NQ]
    weight_sum = sb("weight_sum", [NQ, B], F32)
    taken = carve(vals_arena, at_v, (E1,))[0:NQ]
    used = sb("used", [E1, 4], F32)
    place = carve(vals_arena, at_v, (E1,))[0:E1]
    expert_list = sb("expert_list", [1, E1], I32)
    n_used = sb("n_used", [1, 1], I32)

    consts_ready = sem("consts_ready")
    x_loaded = sem("x_loaded")
    w0_loaded, wo0_loaded = sem("w0_loaded"), sem("wo0_loaded")
    N_W0 = 6
    dve_step = sem("dve_step")
    ln_stats, ln_std = sem("ln_stats"), sem("ln_std")
    bq_scaled = sem("bq_scaled")

    ctx_loaded = [sem(f"ctx_loaded{p}") for p in range(2)]
    ctxT_in_psum, ctxT_ready = sem("ctxT_in_psum"), sem("ctxT_ready")
    xn_ready, xnT_in_psum, xnT_ready = sem("xn_ready"), sem("xnT_in_psum"), sem("xnT_ready")
    k_in_psum, k_stored = sem("k_in_psum"), sem("k_stored")
    v_in_psum, v_stored = sem("v_in_psum"), sem("v_stored")
    q_in_psum, q_stored = sem("q_in_psum"), sem("q_stored")

    gate_loaded, xs_cleared = sem("gate_loaded"), sem("xs_cleared")
    gate_logits = sem("gate_logits")
    g_centred, g_exp = sem("g_centred"), sem("g_exp")
    choice_ready, ranks_ready, slots_ready = sem("choice_ready"), sem("ranks_ready"), sem("slots_ready")
    xs_scattered = sem("xs_scattered")
    expert_used = sem("expert_used")
    rows_used = sem("rows_used")
    w1_loaded = [sem(f"w1_loaded{p}") for p in range(2)]
    w2_loaded = [sem(f"w2_loaded{p}") for p in range(2)]
    xs_loaded = [sem(f"xs_loaded{p}") for p in range(2)]
    xsT_ready = sem("xsT_ready")
    hidden_in_psum, hidden_ready = sem("hidden_in_psum"), sem("hidden_ready")
    ys_ready = sem("ys_ready")
    ys_stored = [sem(f"ys_stored{p}") for p in range(2)]
    y_gathered = [sem(f"y_gathered{p}") for p in range(2)]
    x2_added, x2_step = sem("x2_added"), sem("x2_step")
    w1x_high, w1x_split = sem("w1x_high"), sem("w1x_split")
    ctxT_split = sem("ctxT_split")

    const1_loaded = sem("const1_loaded")
    w1x_loaded = sem("w1x_loaded")
    null_v_stored = sem("null_v_stored")
    kq1_cleared = sem("kq1_cleared")
    mask_null = sem("mask_null")
    mask_ready = sem("mask_ready")
    null_norm = sem("null_norm")
    null_sq = sem("null_sq")
    null_k_stored = sem("null_k_stored")
    v1_in_psum = sem("v1_in_psum")
    v1_stored = sem("v1_stored")
    q1_in_psum = sem("q1_in_psum")
    k1_squared = sem("k1_squared")
    k1_ss = sem("k1_ss")
    k1_norm = sem("k1_norm")
    k1_inv = sem("k1_inv")
    k1_scaled = sem("k1_scaled")
    q1_squared = sem("q1_squared")
    q1_ss = sem("q1_ss")
    q1_norm = sem("q1_norm")
    q1_inv = sem("q1_inv")
    q1_scaled = sem("q1_scaled")
    kT1_stored = sem("kT1_stored")
    kT1_in_psum = sem("kT1_in_psum")
    k1_in_psum = sem("k1_in_psum")
    qT1_stored = sem("qT1_stored")
    qT1_in_psum = sem("qT1_in_psum")
    take_step = sem("take_step")

    sh_loaded = sem("sh_loaded")
    router_loaded = sem("router_loaded")
    r_wT_in_psum = sem("r_wT_in_psum")
    r_wT_ready = sem("r_wT_ready")
    r_scores = sem("r_scores")
    r_taken = sem("r_taken")
    r_counted = sem("r_counted")
    r_used = sem("r_used")
    r_placed = sem("r_placed")
    r_place_ready = sem("r_place_ready")
    r_listed = sem("r_listed")
    list_ready = sem("list_ready")
    sh_in_psum = sem("sh_in_psum")
    sh_g_taken = sem("sh_g_taken")
    sh_u_taken = sem("sh_u_taken")
    sh_h_ready = sem("sh_h_ready")
    sh_y_in_psum = sem("sh_y_in_psum")
    sh_y_taken = sem("sh_y_taken")
    sh_added = sem("sh_added")
    x_high_ready = sem("x_high_ready")
    x_low_ready = sem("x_low_ready")
    we_high_ready = sem("we_high_ready")
    we_split = sem("we_split")
    h1_full = sem("h1_full")
    h1_high_ready = sem("h1_high_ready")
    gu_in_psum = sem("gu_in_psum")
    silu_done = sem("silu_done")
    h1_ready = sem("h1_ready")
    y1_in_psum = sem("y1_in_psum")
    y1_added = sem("y1_added")
    out_stored = sem("out_stored")
    x_final = sem("x_final")
    we_loaded = [sem(f"we_loaded{p}") for p in range(2)]

    class Attn:

        def __init__(s, n, heads, hd, nk, vcols, negated=False):
            s.exp_scale = -1.0 if negated else 1.0
            s.n, s.heads, s.hd, s.nk, s.vcols = n, heads, hd, nk, vcols
            s.ppb = heads // 2
            s.hpc = P // hd
            s.chunks = heads * hd // P
            s.tail = nk - 2 * P
            s.mask_bias = None
            s.kT = kT_all[:, 0:s.chunks * (B + 1) * nk].rearrange("p (c n) -> p c n", c=s.chunks)
            s.qT = qT_all[:, 0:s.chunks * (B + 1) * NQ].rearrange("p (c n) -> p c n", c=s.chunks)
            s.qm_ready = sem(f"L{n}_qm_ready")
            s.scores_ready = sem(f"L{n}_scores_ready")
            s.clipped = sem(f"L{n}_clipped")
            s.max_ready = sem(f"L{n}_max_ready")
            s.exp_done = sem(f"L{n}_exp_done")
            s.transposed = sem(f"L{n}_transposed")
            s.probsT_ready = sem(f"L{n}_probsT_ready")
            s.attended = sem(f"L{n}_attended")
            s.out_taken = sem(f"L{n}_out_taken")
            s.tok_ready = sem(f"L{n}_tok_ready")
            s.inv_ready = sem(f"L{n}_inv_ready")
            s.normalised = sem(f"L{n}_normalised")
            s.tokT_in_psum = sem(f"L{n}_tokT_in_psum")
            s.tokT_ready = sem(f"L{n}_tokT_ready")
            s.projected = sem(f"L{n}_projected")
            s.added = sem(f"L{n}_added")
            s.stats_ready = sem(f"L{n}_stats_ready")
            s.vs_loaded = [sem(f"L{n}_vs_loaded{p}") for p in range(2)]

    A0 = Attn(0, 16, 16, NKV, 32)
    A1 = Attn(1, 8, 64, NKV + 1, 64, negated=True)

    ctxT_ps = psum[0:DCC, 0:2, 0:NKV]
    k_ps = psum[:, 2:4, 0:NKV]
    v_ps = psum[:, 4:6, :].rearrange("p a (t n) -> p (a t) n", t=2)
    xnT_ps = psum[:, 6, 0:2 * NQ].rearrange("p (c n) -> p c n", c=2)
    q_ps = psum[:, 7, 0:2 * NQ].rearrange("p (c n) -> p c n", c=2)
    xnT1_ps = psum[:, 7, 0:2 * NQ].rearrange("p (c n) -> p c n", c=2)
    k1_ps = psum[:, 2:5, :]
    v1_ps = [psum[:, k, :] for k in (5, 6, 5)]
    q1_ps = psum[:, 7, :]
    score_ps = [psum[:, 2 * k:2 * k + 2, :] for k in range(2)]
    pT_ps = psum[:, 4:6, :].rearrange("p a (t n) -> p (a t) n", t=2)[:, 0:3, 0:2 * NQ]
    o_ps = psum[:, 6, 0:4 * NQ].rearrange("p (g n) -> p g n", g=4)
    y_ps = psum[:, 7, :]

    rows = [P, P, TAIL]

    def sp_load0(sp):
        sp.dma_start(x[:, 1:B + 1, :], a["x"].rearrange("b q d -> q b d")).then_inc(x_loaded, 16)
        sp_ctx(sp, 0, 0)
        for dst, src in (
            (wk0[:, :, :], a["L0_xattn_Wk"].rearrange("(c p) n -> p c n", p=DCC)),
            (wv0[0:DCC, :, :], a["L0_xattn_Wv"].rearrange("(c p) n -> p c n", p=DCC)),
            (wv0[DCC:DCC + 1, 1, :], a["L0_xattn_bv"].rearrange("(o n) -> o n", o=1)),
            (bk0[:, :], a["L0_xattn_bk"].rearrange("(c p) -> p c", p=P)),
            (wq0[:, :, :], a["L0_xattn_Wq"].rearrange("(c p) n -> p c n", p=P)),
            (bq0[:, :], a["L0_xattn_bq"].rearrange("(c p) -> p c", p=P)),
        ):
            sp.dma_start(dst, src, allow_slow_non_contiguous=True).then_inc(w0_loaded, 16)
        sp_ctx(sp, 1, 1)
        for dst, src in (
            (wo0[:, :, :], a["L0_xattn_Wo"].rearrange("(c p) n -> p c n", p=P)),
            (bo0[:, :], a["L0_xattn_bo"].rearrange("(o n) -> o n", o=1)),
        ):
            sp.dma_start(dst, src).then_inc(wo0_loaded, 16)

    def sp_ctx(sp, b, p):
        src = a["ctx_768"][b]
        sp.dma_start(ctx_nat[p][:, 0:FULL, :], src[0:FULL * P, :].rearrange("(t p) d -> p t d", p=P)
                     ).then_inc(ctx_loaded[p], 16)
        sp.dma_start(ctx_nat[p][0:TAIL, FULL, :], src[FULL * P:NKV, :]).then_inc(ctx_loaded[p], 16)

    def sp_project0(sp):
        with sp.Fori(1, B // 2) as i:
            for p in range(2):
                sp.wait_ge(ctxT_in_psum, 2 * i + p - 1)
                sp_ctx(sp, 2 * i + p, p)

    def pool_consts(pool):
        nc.gpsimd.memset(ident[:, :], 0.0).then_inc(consts_ready, 1)
        nc.gpsimd.memset(headmask[:, :], 1.0).then_inc(consts_ready, 1)
        nc.gpsimd.memset(eps_col[:, :], EPS).then_inc(consts_ready, 1)
        nc.gpsimd.memset(ones_row[:, :], 1.0).then_inc(consts_ready, 1)
        pool.wait_ge(consts_ready, 4)
        nc.gpsimd.memset(ctxT[DCC:DCC + 1, :, :], 1.0).then_inc(consts_ready, 1)
        pool.wait_ge(consts_ready, 5)
        nc.gpsimd.affine_select(out=ident[:, :], in_=ident[:, :], compare_op=ALU.not_equal, fill=1.0, base=0,
                                pattern=[[-1, P]], channel_multiplier=1).then_inc(consts_ready, 1)
        nc.gpsimd.affine_select(out=headmask[:, :], in_=headmask[:, :], compare_op=ALU.is_ge, fill=0.0, base=0,
                                pattern=[[-16, 8]], channel_multiplier=1).then_inc(consts_ready, 1)
        pool.wait_ge(consts_ready, 7)
        nc.gpsimd.affine_select(out=headmask[:, :], in_=headmask[:, :], compare_op=ALU.is_ge, fill=0.0, base=15,
                                pattern=[[16, 8]], channel_multiplier=-1).then_inc(consts_ready, 1)
        nc.gpsimd.memset(v_all[:, 0:B, :, :].rearrange("p b t (h e) -> p (b t h) e", e=32)[:, :, 16:32], 0.0
                         ).then_inc(consts_ready, 1)
        nc.gpsimd.memset(A0.kT[:, :, B * NKV:(B + 1) * NKV], 0.0).then_inc(consts_ready, 1)
        nc.gpsimd.memset(A0.qT[:, :, B * NQ:(B + 1) * NQ], 0.0).then_inc(consts_ready, 1)
        nc.gpsimd.memset(sums[:, :, :], 1.0).then_inc(consts_ready, 1)
        nc.gpsimd.memset(x[:, 0, :], 0.0).then_inc(consts_ready, 1)
    N_CONSTS = 13

    dve_steps = [0]

    def mark(ins):
        dve_steps[0] += 1
        ins.then_inc(dve_step, 1)

    def marked(dve):
        dve.wait_ge(dve_step, dve_steps[0])

    def step(dve, ins):
        mark(ins)
        marked(dve)

    def dve_ln_finish(dve, n_std):
        for b in range(B):
            nc.vector.bn_aggr(mv[:, b, :], stats[:, b + 1, :]).then_inc(ln_stats, 1)
        dve.wait_ge(ln_std, n_std)
        step(dve, nc.vector.reciprocal(rstd[:, :], std[:, :]))

    def act_std(act, k):
        act.wait_ge(ln_stats, B * (k + 1))
        act.wait_ge(consts_ready, N_CONSTS)
        nc.scalar.activation(std[:, :], mv[:, :, 1], ACT.Sqrt, bias=eps_col[0:NQ, :]).then_inc(ln_std, 1)

    def dve_project0(dve):
        dve.wait_ge(x_loaded, 16)
        for b in range(B):
            mark(nc.vector.bn_stats(stats[:, b + 1, :], x[:, b + 1, :]))
        marked(dve)
        dve_ln_finish(dve, 1)
        with dve.Fori(0, B) as b:
            nc.vector.tensor_scalar(xn[:, :], x[:, b + 1, :], mv[:, b, 0:1], rstd[:, bass.ds(b, 1)], ALU.subtract, ALU.mult
                                    ).then_inc(xn_ready, 1)
            dve.wait_ge(xnT_in_psum, b + 1)
            nc.vector.tensor_copy(xnT[:, :, :], xnT_ps).then_inc(xnT_ready, 1)
            dve.wait_ge(v_in_psum, b + 1)
            nc.vector.tensor_copy(
                v_all[:, b, 0:FULL, :].rearrange("p t (h e) -> p (t h) e", e=32)[:, :, 0:16],
                v_ps[:, 0:FULL, :].rearrange("p t (h e) -> p (t h) e", e=16)).then_inc(v_stored, 1)
            nc.vector.tensor_copy(
                v_all[0:TAIL, b, FULL, :].rearrange("p (h e) -> p h e", e=32)[:, :, 0:16],
                v_ps[0:TAIL, FULL, :].rearrange("p (h e) -> p h e", e=16)).then_inc(v_stored, 1)

    def pe_project0(pe):
        pe.wait_ge(consts_ready, N_CONSTS)
        pe.wait_ge(w0_loaded, 16 * N_W0)
        with pe.Fori(0, B // 2) as i:
            for p in range(2):
                b = 2 * i + p
                pe.wait_ge(ctx_loaded[p], 32 * i + 32)
                for c in range(2):
                    for t in range(3):
                        last = nc.tensor.transpose(ctxT_ps[:, c, t * P:t * P + rows[t]],
                                                   ctx_nat[p][0:rows[t], t, c * DCC:(c + 1) * DCC],
                                                   ident[0:rows[t], 0:rows[t]])
                last.then_inc(ctxT_in_psum, 1)
                pe.wait_ge(xn_ready, b + 1)
                for c in range(2):
                    last = nc.tensor.transpose(xnT_ps[:, c, :], xn[:, c * P:(c + 1) * P], ident[0:NQ, 0:NQ])
                last.then_inc(xnT_in_psum, 1)
                pe.wait_ge(ctxT_ready, b + 1)
                for m in range(2):
                    for c in range(2):
                        last = nc.tensor.matmul(k_ps[:, m, :], wk0[:, c, m * P:(m + 1) * P], ctxT[0:DCC, c, :],
                                                start=(c == 0), stop=(c == 1))
                last.then_inc(k_in_psum, 1)
                pe.wait_ge(xnT_ready, b + 1)
                for t in range(3):
                    for c in range(2):
                        last = nc.tensor.matmul(v_ps[0:rows[t], t, :], ctxT[0:DCC + c, c, t * P:t * P + rows[t]],
                                                wv0[0:DCC + c, c, :], start=(c == 0), stop=(c == 1))
                last.then_inc(v_in_psum, 1)
                for m in range(2):
                    for c in range(2):
                        last = nc.tensor.matmul(q_ps[:, m, :], wq0[:, c, m * P:(m + 1) * P], xnT[:, c, :],
                                                start=(c == 0), stop=(c == 1))
                last.then_inc(q_in_psum, 1)

    def act_project0(act):
        act_std(act, 0)
        act.wait_ge(w0_loaded, 16 * N_W0)
        nc.scalar.activation(bq0s[:, :], bq0[:, :], ACT.Copy, scale=SCALE0).then_inc(bq_scaled, 1)
        act.wait_ge(bq_scaled, 1)
        with act.Fori(0, B) as b:
            act.wait_ge(ctxT_in_psum, b + 1)
            nc.scalar.activation(ctxT[0:DCC, :, :], ctxT_ps, ACT.Copy).then_inc(ctxT_ready, 1)
            act.wait_ge(k_in_psum, b + 1)
            for m in range(2):
                nc.scalar.activation(A0.kT[:, m, bass.ds(b * NKV, NKV)], k_ps[:, m, :], ACT.Identity,
                                     bias=bk0[:, m:m + 1]).then_inc(k_stored, 1)
            act.wait_ge(q_in_psum, b + 1)
            for m in range(2):
                nc.scalar.activation(A0.qT[:, m, bass.ds(b * NQ, NQ)], q_ps[:, m, :], ACT.Identity,
                                     bias=bq0s[:, m:m + 1], scale=SCALE0).then_inc(q_stored, 1)

    def sp_attend(sp, L, v_ready):
        v_ready(sp)

        def load(b, p):
            sp.dma_start(vs[p][:, 0:FULL, :], v_all[:, b, 0:FULL, :]).then_inc(L.vs_loaded[p], 16)
            sp.dma_start(vs[p][0:L.tail, FULL, :], v_all[0:L.tail, b, FULL, :]).then_inc(L.vs_loaded[p], 16)
        load(0, 0)
        load(1, 1)
        with sp.Fori(1, B // 2) as i:
            for p in range(2):
                sp.wait_ge(L.attended, 2 * i + p)
                load(2 * i + p, p)

    def pool_attend(pool, L, q_ready, mask):
        q_ready(pool)

        def spread(b, p):
            for c in range(L.chunks):
                nc.gpsimd.tensor_tensor(
                    qm[p][:, c * L.hpc:(c + 1) * L.hpc, :],
                    L.qT[:, c, bass.ds(b * NQ, NQ)].unsqueeze(1).broadcast_to([P, L.hpc, NQ]),
                    mask.unsqueeze(2).broadcast_to([P, L.hpc, NQ]), ALU.mult).then_inc(L.qm_ready, 1)
        for b in range(2):
            spread(b, b)
        with pool.Fori(1, B // 2) as i:
            for p in range(2):
                pool.wait_ge(L.scores_ready, L.ppb * (2 * i + p - 1))
                spread(2 * i + p, p)
        pool.wait_ge(L.scores_ready, L.ppb * (B - 1))
        spread(B, 0)

    def pe_attend(pe, L, ready):
        ready(pe)
        nrows = [P, P, L.tail]

        def scores(j, b, clipped):
            h = 2 * (j % L.ppb)
            p = (j // L.ppb) % 2
            if clipped is not None:
                pe.wait_ge(L.clipped, clipped)
            if j % L.ppb == 0:
                pe.wait_ge(L.qm_ready, L.chunks * (b + 1))
            for hh in range(2):
                last = nc.tensor.matmul(score_ps[j % 2][0:NQ, hh, 0:L.nk], qm[p][:, h + hh, :],
                                        L.kT[:, (h + hh) // L.hpc, bass.ds(b * L.nk, L.nk)], start=True, stop=True)
            last.then_inc(L.scores_ready, 1)

        def finish_transpose(b):
            pe.wait_ge(L.out_taken, b + 1)
            for g in range(4):
                last = nc.tensor.transpose(y_ps[0:NQ, g * P:(g + 1) * P], oT[:, g, :], ident[:, :])
            last.then_inc(L.tok_ready, 1)

        def finish_transpose_back(b):
            pe.wait_ge(L.normalised, b + 1)
            for c in range(L.chunks):
                last = nc.tensor.transpose(y_ps[:, c * NQ:(c + 1) * NQ], o_tok[:, c * P:(c + 1) * P],
                                           ident[0:NQ, 0:NQ])
            last.then_inc(L.tokT_in_psum, 1)

        def finish_project(b):
            pe.wait_ge(L.tokT_ready, b + 1)
            for c in range(L.chunks):
                last = nc.tensor.matmul(y_ps[0:NQ, 0:D], o_tokT[:, c, :], L.wo[:, c, :], start=(c == 0),
                                        stop=(c == L.chunks - 1 and L.bo is None))
            if L.bo is not None:
                last = nc.tensor.matmul(y_ps[0:NQ, 0:D], ones_row[0:1, 0:NQ], L.bo, start=False, stop=True)
            last.then_inc(L.projected, 1)
        finish = [finish_transpose, finish_transpose_back, finish_project]

        pe.sem_inc(L.transposed, NPB)
        pe.sem_inc(L.attended, 1)
        for j in range(LOOK):
            scores(j, 0, j - 1 if j >= 2 else None)
        with pe.Fori(0, B // 2) as i:
            for j in range(2 * L.ppb):
                n = 2 * L.ppb * i + j
                b = 2 * i + j // L.ppb
                p = (j // L.ppb) % 2
                s = j % L.ppb
                pe.wait_ge(L.exp_done, n + 1)
                for t in range(3):
                    for hh in range(2):
                        last = nc.tensor.transpose(pT_ps[0:nrows[t], t, hh * NQ:(hh + 1) * NQ],
                                                   probs[:, j % NPB, hh, t * P:t * P + nrows[t]], ident[0:NQ, 0:NQ])
                last.then_inc(L.transposed, 1)
                scores(j + LOOK, 2 * i + (j + LOOK) // L.ppb, n + LOOK - 1)
                if s < len(finish):
                    finish[s](b)
                pe.wait_ge(L.probsT_ready, n + 1)
                if s == 0:
                    pe.wait_ge(L.vs_loaded[p], 32 * i + 32)
                    pe.wait_ge(L.out_taken, b + 1)
                for hh in range(2):
                    h = 2 * s + hh
                    g, strip = (h * L.vcols) // P, (h * L.vcols) % P
                    for t in range(3):
                        last = nc.tensor.matmul(o_ps[strip:strip + L.vcols, g, :],
                                                vs[p][0:nrows[t], t, h * L.vcols:(h + 1) * L.vcols],
                                                probsT[j % 2][0:nrows[t], t, hh * NQ:(hh + 1) * NQ],
                                                start=(t == 0), stop=(t == 2))
                if s == L.ppb - 1:
                    last.then_inc(L.attended, 1)
        for step in finish:
            step(B)

    def act_attend(act, L):
        def exps(j, n, b):
            p = (j // L.ppb) % 2
            if j % L.ppb == 0:
                act.wait_ge(L.normalised, b)
            act.wait_ge(L.max_ready, n + 1)
            for hh in range(2):
                h = 2 * (j % L.ppb) + hh
                last = nc.scalar.activation(probs[:, j % NPB, hh, 0:L.nk], probs[:, j % NPB, hh, 0:L.nk], ACT.Exp,
                                            bias=negmax[:, j % NPB, hh:hh + 1], scale=L.exp_scale,
                                            accum_out=sums[:, p, h:h + 1])
            last.then_inc(L.exp_done, 1)

        def finish_take(b):
            act.wait_ge(L.attended, b + 1)
            nc.scalar.activation(oT[:, :, :], o_ps, ACT.Copy).then_inc(L.out_taken, 1)

        def finish_takeT(b):
            act.wait_ge(L.tokT_in_psum, b + 1)
            nc.scalar.activation(o_tokT[:, 0:L.chunks, :], y_ps[:, 0:L.chunks * NQ].rearrange(
                "p (c n) -> p c n", c=L.chunks), ACT.Copy).then_inc(L.tokT_ready, 1)
        finish = {0: finish_take, 2: finish_takeT}

        if L.mask_bias is not None:
            act.wait_ge(mask_null, 3)
            L.mask_bias(act, 0, 0)
        for j in range(AHEAD):
            exps(j, j, 0)
        with act.Fori(0, B // 2) as i:
            for j in range(2 * L.ppb):
                n = 2 * L.ppb * i + j
                b = 2 * i + j // L.ppb
                if j % L.ppb in finish:
                    finish[j % L.ppb](b)
                if j % L.ppb == 1 and L.mask_bias is not None:
                    L.mask_bias(act, b + 1, 1 - (j // L.ppb) % 2)
                act.wait_ge(L.transposed, n + 1 + NPB)
                nc.scalar.activation(probsT[j % 2][:, 0:FULL, :], pT_ps[:, 0:FULL, :], ACT.Copy)
                nc.scalar.activation(probsT[j % 2][0:L.tail, FULL, :], pT_ps[0:L.tail, FULL, :], ACT.Copy
                                     ).then_inc(L.probsT_ready, 1)
                exps(j + AHEAD, n + AHEAD, 2 * i + (j + AHEAD) // L.ppb)
        for s in finish:
            finish[s](B)

    def dve_attend(dve, L):
        def normalise(b, p):
            dve.wait_ge(L.tok_ready, b + 1)
            nc.vector.reciprocal(inv_sums[:, 0:L.heads], sums[:, p, 0:L.heads]).then_inc(L.inv_ready, 1)
            dve.wait_ge(L.inv_ready, b + 1)
            nc.vector.tensor_tensor(
                o_tok[:, 0:L.heads * L.hd].rearrange("q (h e) -> q h e", e=L.hd),
                y_ps[0:NQ, :].rearrange("q (h e) -> q h e", e=L.vcols)[:, :, 0:L.hd],
                inv_sums[:, 0:L.heads].unsqueeze(2).broadcast_to([NQ, L.heads, L.hd]), ALU.mult
            ).then_inc(L.normalised, 1)

        L.prepare(dve)
        for j in range(AHEAD):
            L.masked_max(dve, j, j, 0)
        with dve.Fori(0, B // 2) as i:
            for j in range(2 * L.ppb):
                n = 2 * L.ppb * i + j
                b = 2 * i + j // L.ppb
                s = j % L.ppb
                if s == 1:
                    normalise(b, (j // L.ppb + 1) % 2)
                if s == 3:
                    L.take(dve, b)
                L.masked_max(dve, j + AHEAD, n + AHEAD, 2 * i + (j + AHEAD) // L.ppb)
        normalise(B, 1)
        L.take(dve, B)

    A0.wo, A0.bo = wo0, bo0[0:1, :]

    def a0_prepare(dve):
        dve.wait_ge(q_stored, 2 * B)
        nc.vector.memset(o_ps, 0.0).then_inc(A0.out_cleared, 1)
    A0.out_cleared = sem("L0_out_cleared")
    A0.prepare = a0_prepare

    def a0_masked_max(dve, j, n, b):
        k = j % NPB
        dve.wait_ge(A0.scores_ready, n + 1)
        dve.wait_ge(A0.transposed, n + 1)
        nc.vector.tensor_scalar(probs[:, k, :, 0:NKV], score_ps[j % 2][0:NQ, :, 0:NKV], -CLAMP, CLAMP, ALU.max, ALU.min
                                ).then_inc(A0.clipped, 1)
        dve.wait_ge(A0.clipped, n + 1)
        nc.vector.tensor_reduce(negmax[:, k, :], probs[:, k, :, 0:NKV], AX.X, ALU.max, negate=True
                                ).then_inc(A0.max_ready, 1)
    A0.masked_max = a0_masked_max

    def a0_take(dve, b):
        dve.wait_ge(A0.projected, b + 1)
        nc.vector.tensor_tensor(x[:, b, :], x[:, b, :], y_ps[0:NQ, 0:D], ALU.add).then_inc(A0.added, 1)
        dve.wait_ge(A0.added, b + 1)
        nc.vector.bn_stats(stats[:, b, :], x[:, b, :]).then_inc(A0.stats_ready, 1)
    A0.take = a0_take

    xnT_all_ps = [psum[:, k, 0:4 * NQ].rearrange("p (b c n) -> p b c n", b=2, c=2) for k in range(4)]
    logits_ps = psum[0:NQ, 4, 0:B * E0].rearrange("p (b e) -> p b e", b=B)
    ranks_ps = psum[0:NQ, 5, 0:B * E0].rearrange("p (b e) -> p b e", b=B)
    totals_ps = psum[:, 6, 0:B * E0].rearrange("p (b e) -> p b e", b=B)
    xsT_ps = [psum[:, k, 0:2 * P] .rearrange("p (c n) -> p c n", c=2) for k in range(2)]
    b1_ps = [psum[:, k, 2 * P:2 * P + HC] for k in range(2)]
    hid_ps = [psum[:, 2 + k, :].rearrange("p (m n) -> p m n", m=4) for k in range(4)]
    ys_ps = [psum[:, 6 + k, 0:D] for k in range(2)]

    def pool_consts_moe(pool):
        nc.gpsimd.memset(earlier[:, :], 1.0).then_inc(consts_ready, 1)
        nc.gpsimd.memset(ones_sq[:, :], 1.0).then_inc(consts_ready, 1)
        nc.gpsimd.memset(below8[:, :, :], 1.0).then_inc(consts_ready, 1)
        nc.gpsimd.iota(iota16[:, :], [[1, 16]], base=0, channel_multiplier=0, allow_small_or_imprecise_dtypes=True
                       ).then_inc(consts_ready, 1)
        nc.gpsimd.memset(zeros[:, :], 0.0).then_inc(consts_ready, 1)
        pool.wait_ge(consts_ready, N_CONSTS + 5)
        nc.gpsimd.affine_select(out=earlier[:, :], in_=earlier[:, :], compare_op=ALU.is_gt, fill=0.0, base=0,
                                pattern=[[1, NQ]], channel_multiplier=-1).then_inc(consts_ready, 1)
        nc.gpsimd.affine_select(out=below8[:, :, :], in_=below8[:, :, :], compare_op=ALU.is_gt, fill=0.0, base=0,
                                pattern=[[1, 8], [-1, 8]], channel_multiplier=0).then_inc(consts_ready, 1)
    N_MOE_CONSTS = 7

    def sp_load_moe(sp):
        sp.dma_start(wg0[:, :, :], a["L0_ffn_Wg"].rearrange("(c p) e -> p c e", p=P)).then_inc(gate_loaded, 16)
        sp.dma_start(bg0[:, :], a["L0_ffn_bg"].rearrange("(o e) -> o e", o=1)).then_inc(gate_loaded, 16)
        sp.wait_ge(consts_ready, N_CONSTS + N_MOE_CONSTS)
        sp.dma_start(xs_dram.rearrange("(i p) d -> p i d", p=P), zeros[:, :].unsqueeze(1).broadcast_to([P, NBLK, D])
                     ).then_inc(xs_cleared, 16)
        sp.dma_start(ys_dram.rearrange("(i p) d -> p i d", p=P), zeros[:, :].unsqueeze(1).broadcast_to([P, NBLK, D])
                     ).then_inc(xs_cleared, 16)

    slot_f_pairs = route_b[:, 0, 0:1]

    def dve_gate(dve):
        dve.wait_ge(A0.stats_ready, B + 1)
        dve_ln_finish(dve, 2)
        for b in range(B):
            nc.vector.tensor_scalar(xn_all[:, b, :], x[:, b + 1, :], mv[:, b, 0:1], rstd[:, b:b + 1], ALU.subtract,
                                    ALU.mult).then_inc(xn_ready, 1)
        dve.wait_ge(gate_logits, B)
        dve.wait_ge(consts_ready, N_CONSTS + N_MOE_CONSTS)
        step(dve, nc.vector.tensor_copy(logits[:, :, :], logits_ps))
        step(dve, nc.vector.tensor_reduce(top_logit[:, :], logits[:, :, :], AX.X, ALU.max))
        top = top_logit[:, :].unsqueeze(2).broadcast_to([NQ, B, E0])
        grid = route_a[0:NQ, 0:B * E0].rearrange("q (b e) -> q b e", b=B)
        step(dve, nc.vector.tensor_tensor(choice[:, :, :], logits[:, :, :], top, ALU.is_equal))
        back = route_a[0:NQ, 64:64 + E0]
        step(dve, nc.vector.tensor_scalar(back, iota16[0:NQ, 0:E0], -1.0, float(E0), ALU.mult, ALU.add))
        each = back.unsqueeze(1).broadcast_to([NQ, B, E0])
        step(dve, nc.vector.tensor_tensor(grid, choice[:, :, :], each, ALU.mult))
        step(dve, nc.vector.tensor_reduce(slot_f[:, :], grid, AX.X, ALU.max))
        nc.vector.tensor_tensor(choice[:, :, :], each, slot_f[:, :].unsqueeze(2).broadcast_to([NQ, B, E0]),
                                ALU.is_equal).then_inc(choice_ready, 1)
        nc.vector.tensor_tensor(logits[:, :, :], logits[:, :, :], top, ALU.subtract).then_inc(g_centred, 1)
        dve.wait_ge(g_exp, 1)
        step(dve, nc.vector.tensor_reduce(top_weight[:, :], logits[:, :, :], AX.X, ALU.add))
        step(dve, nc.vector.reciprocal(top_weight[:, :], top_weight[:, :]))
        dve.wait_ge(ranks_ready, 1)
        step(dve, nc.vector.tensor_copy(counts[:, :, :], totals_ps))
        tokens, blocks, first, end = (per_expert[:, k, :] for k in range(4))
        step(dve, nc.vector.tensor_reduce(tokens, counts[:, :, :].rearrange("p b e -> p e b"), AX.X, ALU.add))
        nj = -(-B * NQ // P)
        over = route_a[:, 0:E0 * nj].rearrange("p (e j) -> p e j", e=E0)
        step(dve, nc.vector.tensor_scalar(block_expert[:, 0:nj], iota16[:, 0:nj], float(P), None, ALU.mult))
        step(dve, nc.vector.tensor_tensor(over, tokens.unsqueeze(2).broadcast_to([P, E0, nj]),
                                     block_expert[:, 0:nj].unsqueeze(1).broadcast_to([P, E0, nj]), ALU.is_gt))
        step(dve, nc.vector.tensor_reduce(blocks, over, AX.X, ALU.add))
        pairs = route_a[:, 0:64].rearrange("p (i j) -> p i j", i=8)
        step(dve, nc.vector.tensor_tensor(pairs, below8[:, :, :], blocks.unsqueeze(1).broadcast_to([P, E0, E0]), ALU.mult))
        step(dve, nc.vector.tensor_reduce(first, pairs, AX.X, ALU.add))
        step(dve, nc.vector.tensor_tensor(end, first, blocks, ALU.add))
        ended = route_a[:, 0:NBLK * E0].rearrange("p (i e) -> p i e", i=NBLK)
        step(dve, nc.vector.tensor_tensor(ended, end.unsqueeze(1).broadcast_to([P, NBLK, E0]),
                                     iota16[:, 0:NBLK].unsqueeze(2).broadcast_to([P, NBLK, E0]), ALU.is_le))
        step(dve, nc.vector.tensor_reduce(block_expert[:, :], ended, AX.X, ALU.add))
        twos = route_a[:, 0:NBLK // 2]
        step(dve, nc.vector.tensor_scalar(twos, iota16[:, 0:NBLK // 2], 2.0, per_expert[:, 3, E0 - 1:E0], ALU.mult,
                                          ALU.is_lt))
        step(dve, nc.vector.tensor_reduce(slot_f_pairs, twos, AX.X, ALU.add))
        step(dve, nc.vector.tensor_copy(n_pairs[:, :], slot_f_pairs))
        nc.vector.tensor_scalar(block_expert_i[:, :], block_expert[:, :], float(E0 - 1), None, ALU.min
                                ).then_inc(slots_ready, 1)
        before = route_a[:, :].rearrange("p (b e k) -> p b e k", b=B, e=E0)
        step(dve, nc.vector.tensor_tensor(
            before, counts[:, :, :].rearrange("p k e -> p e k").unsqueeze(1).broadcast_to([P, B, E0, B]),
            below8[:, :, :].unsqueeze(2).broadcast_to([P, B, E0, B]), ALU.mult))
        step(dve, nc.vector.tensor_reduce(route_b[:, :, :], before, AX.X, ALU.add))
        step(dve, nc.vector.scalar_tensor_tensor(route_b[:, :, :], first.unsqueeze(1).broadcast_to([P, B, E0]), float(P),
                                            route_b[:, :, :], ALU.mult, ALU.add))
        step(dve, nc.vector.tensor_tensor(route_b[0:NQ], ranks_ps, route_b[0:NQ], ALU.add))
        step(dve, nc.vector.tensor_tensor(route_b[0:NQ], route_b[0:NQ], choice[:, :, :], ALU.mult))
        step(dve, nc.vector.tensor_reduce(slot_f[:, :], route_b[0:NQ], AX.X, ALU.add))
        nc.vector.tensor_copy(slot[:, :], slot_f[:, :]).then_inc(slots_ready, 1)

    def act_gate(act):
        act_std(act, 1)
        for k in range(B // 2):
            act.wait_ge(xnT_in_psum, B + 2 * k + 2)
            nc.scalar.activation(xnT0[:, :, 2 * k * NQ:2 * (k + 1) * NQ].rearrange("p c (b n) -> p b c n", b=2),
                                 xnT_all_ps[k], ACT.Copy).then_inc(xnT_ready, 2)
        act.wait_ge(g_centred, 1)
        nc.scalar.activation(logits[:, :, :], logits[:, :, :], ACT.Exp).then_inc(g_exp, 1)

    def pe_gate(pe):
        pe.wait_ge(gate_loaded, 32)
        pe.wait_ge(A0.added, B + 1)
        for b in range(B):
            pe.wait_ge(xn_ready, B + b + 1)
            for c in range(2):
                last = nc.tensor.transpose(xnT_all_ps[b // 2][:, b % 2, c, :], xn_all[:, b, c * P:(c + 1) * P],
                                           ident[0:NQ, 0:NQ])
            last.then_inc(xnT_in_psum, 1)
        for b in range(B):
            pe.wait_ge(xnT_ready, B + 2 * (b // 2) + 2)
            for c in range(2):
                nc.tensor.matmul(logits_ps[:, b, :], xnT0[:, c, b * NQ:(b + 1) * NQ], wg0[:, c, :], start=(c == 0),
                                 stop=False)
            nc.tensor.matmul(logits_ps[:, b, :], ones_row[0:1, 0:NQ], bg0[0:1, :], start=False, stop=True
                             ).then_inc(gate_logits, 1)
        pe.wait_ge(choice_ready, 1)
        nc.tensor.matmul(ranks_ps, earlier[:, :], choice[:, :, :], start=True, stop=True)
        nc.tensor.matmul(totals_ps, ones_sq[:, :], choice[:, :, :], start=True, stop=True).then_inc(ranks_ready, 1)

    def pool_dispatch(pool):
        pool.wait_ge(slots_ready, 2)
        pool.wait_ge(xn_ready, 2 * B)
        pool.wait_ge(xs_cleared, 32)
        for b in range(B):
            nc.gpsimd.indirect_dma_start(
                out=xs_dram, out_offset=bass.IndirectOffsetOnAxis(ap=slot[:, b:b + 1], axis=0),
                in_=xn_all[:, b, :], in_offset=None).then_inc(xs_scattered, 16)

    def pool_combine(pool):
        pairs = pool.value_load(n_pairs[0:1, 0:1], min_val=1, max_val=NBLK // 2)
        for p in range(2):
            pool.wait_ge(ys_stored[p], 16 * pairs + 16)
        nc.gpsimd.tensor_tensor(pool_turn[:, :], ones_row[0:1, 0:1], ones_row[0:1, 0:1], ALU.mult)
        for b in range(B):
            if b >= 2:
                pool.wait_ge(x2_added, b - 1)
            nc.gpsimd.indirect_dma_start(
                out=y_tok[:, b % 2, :], out_offset=None, in_=ys_dram,
                in_offset=bass.IndirectOffsetOnAxis(ap=slot[:, b:b + 1], axis=0)).then_inc(y_gathered[b % 2], 16)

    def sp_experts(sp):
        sp.wait_ge(slots_ready, 1)
        pairs = sp.value_load(n_pairs[0:1, 0:1], min_val=1, max_val=NBLK // 2)
        with sp.Fori(0, NBLK // 2) as i:
            with sp.If(i < pairs):
                for p in range(2):
                    n = 2 * i + p
                    e = sp.value_load(block_expert_i[0:1, bass.ds(n, 1)], min_val=0, max_val=E0 - 1)
                    sp.wait_ge(expert_used, n + 1)
                    sp.dma_start(w1_e[p], a["L0_ffn_W1"].rearrange("e (c q) h -> q (e c) h", q=P)[:, bass.ds(2 * e, 2), :]
                                 ).then_inc(w1_loaded[p], 16)
                    sp.dma_start(b1_rows[p][:, :], a["L0_ffn_b1"][e].rearrange("(m q) -> m q", q=P)
                                 ).then_inc(w1_loaded[p], 16)
                    if p == 0:
                        sp.wait_ge(xs_scattered, 16 * B)
                    sp.wait_ge(rows_used, n + 1)
                    sp.dma_start(xs_rows[p], xs_dram[bass.ds(n * P, P), :]).then_inc(xs_loaded[p], 16)
                    sp.dma_start(w2_e[p], a["L0_ffn_W2"].rearrange("e (m q) d -> q (e m) d", q=P)[:, bass.ds(HC * e, HC), :]
                                 ).then_inc(w2_loaded[p], 16)
                    sp.dma_start(b2_row[p][:, :], a["L0_ffn_b2"][bass.ds(e, 1), :]).then_inc(w2_loaded[p], 16)

    def act_store_ys(act, n, p):
        act.wait_ge(ys_ready, n + 1)
        act.dma_start(ys_dram[bass.ds(n * P, P), :], ys_rows[p]).then_inc(ys_stored[p], 16)

    def pe_experts(pe):
        def rows(n, i, p):
            pe.wait_ge(xs_loaded[p], 16 * i + 16)
            pe.wait_ge(w1_loaded[p], 32 * i + 32)
            for c in range(2):
                nc.tensor.transpose(xsT_ps[p][:, c, :], xs_rows[p][:, c * P:(c + 1) * P], ident[:, :])
            nc.tensor.transpose(b1_ps[p], b1_rows[p][:, :], ident[0:HC, 0:HC]).then_inc(rows_used, 1)

        pe.wait_ge(slots_ready, 2)
        pe.sem_inc(expert_used, 2)
        pe.sem_inc(rows_used, 2)
        pairs = pe.value_load(n_pairs[0:1, 0:1], min_val=1, max_val=NBLK // 2)
        with pe.Fori(0, NBLK // 2) as i:
            with pe.If(i < pairs):
                for p in range(2):
                    n = 2 * i + p
                    rows(n, i, p)
                    pe.wait_ge(xsT_ready, n + 1)
                    for m in range(HC):
                        for c in range(2):
                            last = nc.tensor.matmul(hid_ps[2 * p + m // 4][:, m % 4, :], w1_e[p][:, c, m * P:(m + 1) * P],
                                                    xsT[p][:, c, :], start=(c == 0), stop=(c == 1))
                        if m % 4 == 3:
                            last.then_inc(hidden_in_psum, 1)
                    pe.wait_ge(w2_loaded[p], 32 * i + 32)
                    nc.tensor.matmul(ys_ps[p], ones_row[0:1, :], b2_row[p][0:1, :], start=True, stop=False)
                    for m in range(HC):
                        if m % 4 == 0:
                            pe.wait_ge(hidden_ready, 2 * n + 1 + m // 4)
                        last = nc.tensor.matmul(ys_ps[p], hT[p][:, m, :], w2_e[p][:, m, :], start=False, stop=(m == HC - 1))
                    last.then_inc(expert_used, 1)

    def act_experts(act):
        for p in range(2):
            act.sem_inc(ys_stored[p], 16)
        act.wait_ge(slots_ready, 1)
        pairs = act.value_load(n_pairs[0:1, 0:1], min_val=1, max_val=NBLK // 2)
        with act.Fori(0, NBLK // 2) as i:
            with act.If(i < pairs):
                for p in range(2):
                    n = 2 * i + p
                    act.wait_ge(xsT_ready, n + 1)
                    for half in range(2):
                        act.wait_ge(hidden_in_psum, 2 * n + half + 1)
                        for m in range(4 * half, 4 * half + 4):
                            last = nc.scalar.activation(hT[p][:, m, :], hid_ps[2 * p + half][:, m % 4, :], ACT.Silu,
                                                        bias=b1_col[p][:, m:m + 1])
                        last.then_inc(hidden_ready, 1)
                    act_store_ys(act, n, p)

    def dve_experts(dve):
        dve.wait_ge(slots_ready, 1)
        pairs = dve.value_load(n_pairs[0:1, 0:1], min_val=1, max_val=NBLK // 2)
        with dve.Fori(0, NBLK // 2) as i:
            with dve.If(i < pairs):
                for p in range(2):
                    n = 2 * i + p
                    dve.wait_ge(rows_used, n + 3)
                    dve.wait_ge(expert_used, n + 1)
                    nc.vector.tensor_copy(b1_col[p][:, :], b1_ps[p])
                    nc.vector.tensor_copy(xsT[p], xsT_ps[p]).then_inc(xsT_ready, 1)
                    dve.wait_ge(expert_used, n + 3)
                    dve.wait_ge(ys_stored[p], 16 * i + 16)
                    nc.vector.tensor_copy(ys_rows[p], ys_ps[p]).then_inc(ys_ready, 1)

    A1.wo, A1.bo = wo1, None

    def sp_load1(sp):
        for dst, src in (
            (wo1[:, :, :], a["L1_xattn_Wo"].rearrange("(c p) n -> p c n", p=P)),
            (g_norm[:, :], a["L1_xattn_g_norm"].rearrange("(o d) -> o d", o=1).broadcast_to([NQ, D])),
            (g_out[:, :], a["L1_xattn_g_out"].rearrange("(o d) -> o d", o=1).broadcast_to([NQ, D])),
            (mask_u8[:, 0:B, :], a["mask_BxS2_bf1"].rearrange("(o b) n -> o b n", o=1).broadcast_to([NQ, B, NKV])),
            (mask_u8[:, B, :], a["mask_BxS2_bf1"][0:1, :].broadcast_to([NQ, NKV])),
            (null_row[:, :], a["L1_xattn_null_kv"][0:1, :].broadcast_to([P, HD1])),
        ):
            sp.dma_start(dst, src).then_inc(const1_loaded, 16)
        for half in range(2):
            rows64 = slice(half * HD1, (half + 1) * HD1)
            for col, src in (
                (null_col, a["L1_xattn_null_kv"][0, :]),
                (q_scale_col, a["L1_xattn_q_scale"]),
                (k_scale_col, a["L1_xattn_k_scale"]),
            ):
                sp.dma_start(col[rows64, :], src.rearrange("(d o) -> d o", o=1), allow_slow_non_contiguous=True
                             ).then_inc(const1_loaded, 16)

    N_CONST1 = 12

    def sp_load1_weights(sp):
        sp.wait_ge(A0.added, B + 1)
        for p in range(2):
            sp_ctx(sp, p, p)
        wkv = a["L1_xattn_Wkv"].rearrange("(c p) n -> p c n", p=DCC)
        sp.dma_start(wk1, wkv[:, :, 0:512]).then_inc(w1x_loaded, 16)
        sp.dma_start(wv1, wkv[:, :, 512:1024]).then_inc(w1x_loaded, 16)
        sp.dma_start(wq1, a["L1_xattn_Wq"].rearrange("(c p) n -> p c n", p=P)).then_inc(w1x_loaded, 16)

    def sp_project1(sp):
        def load(b, p):
            src = a["ctx_768"][b]
            sp.dma_start(ctx_nat[p][:, 0:FULL, :], src[0:FULL * P, :].rearrange("(t p) d -> p t d", p=P)
                         ).then_inc(ctx_loaded[p], 16)
            sp.dma_start(ctx_nat[p][0:TAIL, FULL, :], src[FULL * P:NKV, :]).then_inc(ctx_loaded[p], 16)
        pairs = sp.value_load(n_pairs[0:1, 0:1], min_val=1, max_val=NBLK // 2)
        for p in range(2):
            sp.wait_ge(ys_stored[p], 16 * pairs + 16)
        for h in range(8):
            sp.dma_start(v_all[TAIL:TAIL + 1, :, FULL, h * HD1:(h + 1) * HD1],
                         a["L1_xattn_null_kv"][1:2, :].unsqueeze(1).broadcast_to([1, B, HD1])).then_inc(null_v_stored, 16)
        with sp.Fori(1, B // 2) as i:
            for p in range(2):
                sp.wait_ge(ctxT_in_psum, B + 2 * i + p - 1)
                sp_ctx(sp, 2 * i + p, p)
        sp.wait_ge(ctxT_in_psum, B + B - 1)
        sp_ctx(sp, 0, 0)

    def pool_consts1(pool):
        nc.gpsimd.memset(halfmask[:, :], -SCALE1).then_inc(consts_ready, 1)
        nc.gpsimd.memset(key_ss[:, :, :], 1.0).then_inc(consts_ready, 1)
        pool.wait_ge(consts_ready, N_CONSTS + N_MOE_CONSTS + 2)
        nc.gpsimd.affine_select(out=halfmask[:, :], in_=halfmask[:, :], compare_op=ALU.is_ge, fill=0.0, base=0,
                                pattern=[[-HD1, 2]], channel_multiplier=1).then_inc(consts_ready, 1)
        pool.wait_ge(consts_ready, N_CONSTS + N_MOE_CONSTS + 3)
        nc.gpsimd.affine_select(out=halfmask[:, :], in_=halfmask[:, :], compare_op=ALU.is_ge, fill=0.0, base=HD1 - 1,
                                pattern=[[HD1, 2]], channel_multiplier=-1).then_inc(consts_ready, 1)
        pool.wait_ge(consts_ready, N_CONSTS + N_MOE_CONSTS + 4)
        pool.wait_ge(const1_loaded, 16 * N_CONST1)
        nc.gpsimd.memset(flt_max[:, :], FLT_MAX).then_inc(mask_null, 1)
        nc.gpsimd.tensor_scalar(halfmask[:, :], halfmask[:, :], q_scale_col[:, 0:1], k_scale_col[:, 0:1], ALU.mult,
                                ALU.mult).then_inc(consts_ready, 1)

    def pool_clear1(pool):
        nc.gpsimd.memset(A1.kT[:, :, B * A1.nk:(B + 1) * A1.nk], 0.0).then_inc(kq1_cleared, 1)
        nc.gpsimd.memset(A1.qT[:, :, B * NQ:(B + 1) * NQ], 0.0).then_inc(kq1_cleared, 1)

    def pool_mask_clear(pool):
        pool.wait_ge(ctxT_in_psum, 2 * B + 1)
        for p in range(2):
            nc.gpsimd.memset(mask_bias[p][:, NKV:NKV + 1], 0.0).then_inc(mask_null, 1)

    def act_mask_bias(act, b, p):
        nc.scalar.activation(mask_bias[p][:, 0:NKV], mask_u8[:, b, :], ACT.Identity, bias=flt_max[:, 0:1],
                             scale=-FLT_MAX).then_inc(mask_ready, 1)
    A1.mask_bias = act_mask_bias

    def act_split_weights1(act):
        act.wait_ge(w1x_loaded, 48)
        nc.scalar.activation(wk1_high, wk1, ACT.Copy).then_inc(w1x_high, 1)
        nc.scalar.activation(wv1_high, wv1, ACT.Copy).then_inc(w1x_high, 1)

    def pool_split_weights1(pool):
        for k, (w, high, low) in enumerate(((wk1, wk1_high, wk1_low), (wv1, wv1_high, wv1_low))):
            pool.wait_ge(w1x_high, k + 1)
            nc.gpsimd.tensor_tensor(low, w, high.bitcast(F32), ALU.subtract).then_inc(w1x_split, 1)

    def dve_project1(dve):
        pairs = dve.value_load(n_pairs[0:1, 0:1], min_val=1, max_val=NBLK // 2)
        for p in range(2):
            dve.wait_ge(ys_stored[p], 16 * pairs + 16)
        dve.wait_ge(null_norm, 1)
        mark(nc.vector.tensor_scalar(null_ss[:, :], null_ss[:, :], 1e-12, None, ALU.max))
        marked(dve)
        mark(nc.vector.reciprocal(null_ss[:, :], null_ss[:, :]))
        marked(dve)
        mark(nc.vector.tensor_tensor(null_col[:, :], null_col[:, :], null_ss[:, :], ALU.mult))
        marked(dve)
        nc.vector.tensor_copy(
            A1.kT[:, :, 0:B * A1.nk].rearrange("p c (b n) -> p c b n", n=A1.nk)[:, :, :, NKV],
            null_col[:, :].unsqueeze(2).broadcast_to([P, 4, B])).then_inc(null_k_stored, 1)
        dve.wait_ge(const1_loaded, 16 * N_CONST1)

        def invert(ss, norm, b, ready):
            dve.wait_ge(norm, b + 1)
            nc.vector.tensor_scalar(ss, ss, 1e-12, None, ALU.max).then_inc(ready, 1)
            dve.wait_ge(ready, 2 * b + 1)
            nc.vector.reciprocal(ss, ss).then_inc(ready, 1)
            dve.wait_ge(ready, 2 * b + 2)

        def keep_v(b, t):
            dve.wait_ge(v1_in_psum, 3 * b + t + 1)
            nc.vector.tensor_copy(v_all[0:rows[t], b, t, :], v1_ps[t][0:rows[t], :]).then_inc(v1_stored, 1)

        def split_ctx(n):
            dve.wait_ge(ctxT_ready, n)
            nc.vector.tensor_tensor(ctxT_low[:, :, :], ctxT_ps, ctxT_high[:, :, :].bitcast(F32), ALU.subtract
                                    ).then_inc(ctxT_split, 1)

        heads = lambda v: v.rearrange("p (h e) -> p h e", e=HD1)
        split_ctx(B + 1)
        with dve.Fori(0, B // 2) as i:
            for p in range(2):
                b = 2 * i + p
                count = [0]

                def chain(ins, wait=True):
                    count[0] += 1
                    ins.then_inc(x2_step, 1)
                    if wait:
                        dve.wait_ge(x2_step, X2_STEPS * b + count[0])

                def spread():
                    chain(nc.vector.memset(turn[:, 0:1], 0.0), wait=False)
                    nc.vector.bn_aggr(mv[:, 0, :], stats[:, 0, :]).then_inc(ln_stats, 1)

                dve.wait_ge(y_gathered[p], 16 * i + 16)
                chain(nc.vector.scalar_tensor_tensor(y_row, y_tok[:, p, :], top_weight[:, bass.ds(b, 1)], x[:, b + 1, :],
                                                     ALU.mult, ALU.add))
                chain(nc.vector.bn_stats(stats[:, 0, :], y_row), wait=False)
                nc.vector.tensor_copy(x[:, b + 1, :], y_row).then_inc(x2_added, 1)
                dve.wait_ge(x2_step, X2_STEPS * b + count[0])
                spread()
                dve.wait_ge(ln_std, 2 + 2 * b + 1)
                chain(nc.vector.reciprocal(rstd[:, 0:1], std[:, 0:1]))
                chain(nc.vector.tensor_scalar(y_row, y_row, mv[:, 0, 0:1], rstd[:, 0:1], ALU.subtract, ALU.mult))
                chain(nc.vector.tensor_reduce(row_max[:, 0:1], y_row, AX.X, ALU.max))
                chain(nc.vector.reciprocal(row_max[:, 0:1], row_max[:, 0:1]))
                chain(nc.vector.tensor_scalar(y_row, y_row, row_max[:, 0:1], None, ALU.mult))
                chain(nc.vector.bn_stats(stats[:, 0, :], y_row))
                spread()
                dve.wait_ge(ln_std, 2 + 2 * b + 2)
                chain(nc.vector.reciprocal(rstd[:, 0:1], std[:, 0:1]))
                chain(nc.vector.tensor_scalar(y_row, y_row, mv[:, 0, 0:1], rstd[:, 0:1], ALU.subtract, ALU.mult))
                dve.wait_ge(xnT_in_psum, 2 * B + b)
                nc.vector.tensor_tensor(xn[:, :], y_row, g_norm[:, :], ALU.mult).then_inc(xn_ready, 1)
                dve.wait_ge(xnT_in_psum, 2 * B + b + 1)
                nc.vector.tensor_copy(xnT[:, :, :], xnT1_ps).then_inc(xnT_ready, 1)
                dve.wait_ge(k1_squared, 2 * b + 1)
                nc.vector.tensor_reduce(key_ss[:, 0:FULL, :], k_tok_full.rearrange("p t (h e) -> p t h e", e=HD1),
                                        AX.X, ALU.add).then_inc(k1_ss, 1)
                keep_v(b, 0)
                dve.wait_ge(k1_squared, 2 * b + 2)
                nc.vector.tensor_reduce(key_ss[0:TAIL, FULL, :], heads(k_tok[FULL][0:TAIL, :]), AX.X, ALU.add
                                        ).then_inc(k1_ss, 1)
                invert(key_ss[:, :, :], k1_norm, b, k1_inv)
                each = key_ss[:, :, :].unsqueeze(3).broadcast_to([P, 3, 8, HD1])
                for t in range(3):
                    nc.vector.tensor_tensor(heads(k_tok[t][0:rows[t], :]), heads(k1_ps[0:rows[t], t, :]),
                                            each[0:rows[t], t], ALU.mult).then_inc(k1_scaled, 1)
                keep_v(b, 1)
                dve.wait_ge(q1_squared, b + 1)
                nc.vector.tensor_reduce(q_ss[:, :], heads(o_tok[:, :]), AX.X, ALU.add).then_inc(q1_ss, 1)
                keep_v(b, 2)
                invert(q_ss[:, :], q1_norm, b, q1_inv)
                nc.vector.tensor_tensor(heads(o_tok[:, :]), heads(q1_ps[0:NQ, :]),
                                        q_ss[:, :].unsqueeze(2).broadcast_to([NQ, 8, HD1]), ALU.mult
                                        ).then_inc(q1_scaled, 1)
                split_ctx(B + b + 2)
    X2_STEPS = 12

    def pe_project1(pe):
        def transpose_ctx(p, loaded):
            pe.wait_ge(ctx_loaded[p], loaded)
            for c in range(2):
                for t in range(3):
                    last = nc.tensor.transpose(ctxT_ps[:, c, t * P:t * P + rows[t]],
                                               ctx_nat[p][0:rows[t], t, c * DCC:(c + 1) * DCC],
                                               ident[0:rows[t], 0:rows[t]])
            last.then_inc(ctxT_in_psum, 1)

        def times(ps, t, high, low):
            for c in range(2):
                cols = slice(t * P, t * P + rows[t])
                nc.tensor.matmul(ps, ctxT_high[:, c, cols], high[:, c, :], start=(c == 0), stop=False)
                nc.tensor.matmul(ps, ctxT_high[:, c, cols], low[:, c, :], start=False, stop=False)
                last = nc.tensor.matmul(ps, ctxT_low[:, c, cols], high[:, c, :], start=False, stop=(c == 1))
            return last

        loads = 32 * (B // 2)
        pe.wait_ge(w1x_split, 2)
        transpose_ctx(0, loads + 32)
        with pe.Fori(0, B // 2) as i:
            for p in range(2):
                b = 2 * i + p
                pe.wait_ge(ctxT_split, b + 1)
                for t in range(3):
                    pe.wait_ge(kT1_stored, 3 * b + t + 1)
                    last = times(k1_ps[0:rows[t], t, :], t, wk1_high, wk1_low)
                last.then_inc(k1_in_psum, 1)
                pe.wait_ge(xn_ready, 2 * B + b + 1)
                pe.wait_ge(qT1_stored, b + 1)
                for c in range(2):
                    last = nc.tensor.transpose(xnT1_ps[:, c, :], xn[:, c * P:(c + 1) * P], ident[0:NQ, 0:NQ])
                last.then_inc(xnT_in_psum, 1)
                for t in range(3):
                    if t == 2:
                        pe.wait_ge(v1_stored, 3 * b + 1)
                    times(v1_ps[t][0:rows[t], :], t, wv1_high, wv1_low).then_inc(v1_in_psum, 1)
                    if t == 1:
                        pe.wait_ge(xnT_ready, 2 * B + b + 1)
                        for c in range(2):
                            last = nc.tensor.matmul(q1_ps[0:NQ, :], xnT[:, c, :], wq1[:, c, :], start=(c == 0),
                                                    stop=(c == 1))
                        last.then_inc(q1_in_psum, 1)
                transpose_ctx(1 - p, loads + 32 * i + 32 * (p + 1))
                for t in range(3):
                    pe.wait_ge(k1_scaled, 3 * b + t + 1)
                    for c in range(4):
                        last = nc.tensor.transpose(k1_ps[:, t, c * P:c * P + rows[t]],
                                                   k_tok[t][0:rows[t], c * P:(c + 1) * P], ident[0:rows[t], 0:rows[t]])
                    last.then_inc(kT1_in_psum, 1)
                pe.wait_ge(q1_scaled, b + 1)
                for c in range(4):
                    last = nc.tensor.transpose(q1_ps[:, c * NQ:(c + 1) * NQ], o_tok[:, c * P:(c + 1) * P],
                                               ident[0:NQ, 0:NQ])
                last.then_inc(qT1_in_psum, 1)

    def act_project1(act):
        def take_ctx(n):
            act.wait_ge(ctxT_in_psum, n)
            nc.scalar.activation(ctxT_high[:, :, :], ctxT_ps, ACT.Copy).then_inc(ctxT_ready, 1)

        act.wait_ge(const1_loaded, 16 * N_CONST1)
        act.sem_inc(kT1_stored, 3)
        act.sem_inc(qT1_stored, 1)
        take_ctx(B + 1)
        nc.scalar.activation(null_row[:, :], null_row[:, :], ACT.Square, accum_out=null_ss[:, :]).then_inc(null_sq, 1)
        act.wait_ge(null_sq, 1)
        nc.scalar.activation(null_ss[:, :], null_ss[:, :], ACT.Sqrt).then_inc(null_norm, 1)
        with act.Fori(0, B) as b:
            for k in range(2):
                act.wait_ge(ln_stats, 2 * B + 2 * b + k + 1)
                nc.scalar.activation(std[:, 0:1], mv[:, 0, 1:2], ACT.Sqrt, bias=eps_col[0:NQ, :]).then_inc(ln_std, 1)
            act.wait_ge(k1_in_psum, b + 1)
            nc.scalar.activation(k_tok_full, k1_ps[:, 0:FULL, :], ACT.Square).then_inc(k1_squared, 1)
            nc.scalar.activation(k_tok[FULL][0:TAIL, :], k1_ps[0:TAIL, FULL, :], ACT.Square).then_inc(k1_squared, 1)
            act.wait_ge(k1_ss, 2 * b + 2)
            nc.scalar.activation(key_ss[:, :, :], key_ss[:, :, :], ACT.Sqrt).then_inc(k1_norm, 1)
            act.wait_ge(q1_in_psum, b + 1)
            nc.scalar.activation(o_tok[:, :], q1_ps[0:NQ, :], ACT.Square).then_inc(q1_squared, 1)
            act.wait_ge(q1_ss, b + 1)
            nc.scalar.activation(q_ss[:, :], q_ss[:, :], ACT.Sqrt).then_inc(q1_norm, 1)
            take_ctx(B + b + 2)
            for t in range(3):
                act.wait_ge(kT1_in_psum, 3 * b + t + 1)
                nc.scalar.activation(A1.kT[:, :, bass.ds(b * A1.nk + t * P, rows[t])],
                                     k1_ps[:, t, :].rearrange("p (c n) -> p c n", c=4)[:, :, 0:rows[t]], ACT.Copy
                                     ).then_inc(kT1_stored, 1)
            act.wait_ge(qT1_in_psum, b + 1)
            nc.scalar.activation(A1.qT[:, :, bass.ds(b * NQ, NQ)],
                                 q1_ps[:, 0:4 * NQ].rearrange("p (c n) -> p c n", c=4), ACT.Copy).then_inc(qT1_stored, 1)

    def a1_prepare(dve):
        dve.wait_ge(mask_null, 3)
    A1.prepare = a1_prepare
    A1.clipped = A1.max_ready

    def a1_masked_max(dve, j, n, b):
        k = j % NPB
        p = (j // A1.ppb) % 2
        dve.wait_ge(A1.scores_ready, n + 1)
        dve.wait_ge(A1.transposed, n + 1)
        if j % A1.ppb == 0:
            dve.wait_ge(mask_ready, b + 1)
        nc.vector.memset(turn[:, k:k + 1], 0.0)
        for hh in range(2):
            last = nc.vector.tensor_tensor_reduce(
                out=probs[:, k, hh, 0:A1.nk], in0=score_ps[j % 2][0:NQ, hh, 0:A1.nk], in1=mask_bias[p],
                op0=ALU.add, op1=ALU.min, scale=1.0, scalar=FLT_MAX, accum_out=negmax[:, k, hh:hh + 1])
        last.then_inc(A1.max_ready, 1)
    A1.masked_max = a1_masked_max

    def a1_take(dve, b):
        dve.wait_ge(A1.projected, b + 1)
        nc.vector.tensor_reduce(top_out[:, :], y_ps[0:NQ, 0:D], AX.X, ALU.max).then_inc(take_step, 1)
        dve.wait_ge(take_step, 2 * b + 1)
        nc.vector.reciprocal(top_out[:, :], top_out[:, :]).then_inc(take_step, 1)
        dve.wait_ge(take_step, 2 * b + 2)
        nc.vector.tensor_scalar(z_all[:, b, :], y_ps[0:NQ, 0:D], top_out[:, 0:1], None, ALU.mult).then_inc(A1.added, 1)
        dve.wait_ge(A1.added, b + 1)
        nc.vector.bn_stats(stats[:, b, :], z_all[:, b, :]).then_inc(A1.stats_ready, 1)
    A1.take = a1_take

    def dve_add1(dve):
        dve.wait_ge(A1.stats_ready, B + 1)
        dve_ln_finish(dve, 2 + 2 * B + 1)
        halves = [range(0, B // 2), range(B // 2, B)]
        for half in halves:
            for b in half:
                mark(nc.vector.scalar_tensor_tensor(z_all[:, b + 1, :], z_all[:, b + 1, :], mv[:, b, 0:1], g_out[:, :],
                                                    ALU.subtract, ALU.mult))
            marked(dve)
            for b in half:
                mark(nc.vector.scalar_tensor_tensor(x[:, b + 1, :], z_all[:, b + 1, :], rstd[:, b:b + 1], x[:, b + 1, :],
                                                    ALU.mult, ALU.add))
            marked(dve)
            for b in half:
                mark(nc.vector.bn_stats(stats[:, b + 1, :], x[:, b + 1, :]))
            marked(dve)
            for b in half:
                nc.vector.bn_aggr(mv[:, b, :], stats[:, b + 1, :]).then_inc(ln_stats, 1)
        for k, half in enumerate(halves):
            dve.wait_ge(ln_std, 2 + 2 * B + 2 + k)
            cols = slice(half[0], half[-1] + 1)
            step(dve, nc.vector.reciprocal(rstd[:, cols], std[:, cols]))
            for b in half:
                nc.vector.tensor_scalar(z_all[:, b + 1, :], x[:, b + 1, :], mv[:, b, 0:1], rstd[:, b:b + 1], ALU.subtract,
                                        ALU.mult).then_inc(xn_ready, 1)

    def act_add1(act):
        act_std(act, 4)
        for k in range(2):
            cols = slice(k * B // 2, (k + 1) * B // 2)
            act.wait_ge(ln_stats, 5 * B + (k + 1) * B // 2)
            nc.scalar.activation(std[:, cols], mv[:, cols, 1], ACT.Sqrt, bias=eps_col[0:NQ, :]).then_inc(ln_std, 1)


    gu_ps = [psum[:, k, 0:HT] for k in range(4)]
    y1_ps = [psum[0:NQ, 4 + k, :].rearrange("q (b d) -> q b d", b=2) for k in range(4)]
    r_logits_ps = psum[0:NQ, 4, :].rearrange("q (b e) -> q b e", b=B)
    r_wT_ps = psum[:, 6, 0:2 * E1].rearrange("p (c e) -> p c e", c=2)
    r_count_ps = psum[0:E1, 7, 0:1]
    r_before_ps = psum[0:E1, 7, 8:9]
    r_total_ps = psum[0:E1, 7, 16:17]
    r_list_ps = psum[0:1, 7, 64:64 + E1]
    sh_y_ps = [psum[0:NQ, k, :].rearrange("q (b d) -> q b d", b=2) for k in range(4)]

    def pool_consts_ffn1(pool):
        nc.gpsimd.iota(iota64[:, :], [[1, E1]], base=0, channel_multiplier=0, allow_small_or_imprecise_dtypes=True
                       ).then_inc(consts_ready, 1)
        nc.gpsimd.iota(e_col[:, :], [[1, 1]], base=0, channel_multiplier=1, allow_small_or_imprecise_dtypes=True
                       ).then_inc(consts_ready, 1)

    def sp_load_ffn1(sp):
        for p in range(2):
            sp.wait_ge(A1.vs_loaded[p], 32 * (B // 2))
        sp.dma_start(router_rows, a["L1_ffn_router_w"]).then_inc(router_loaded, 16)
        sp.dma_start(e_bias[:, :], a["L1_ffn_e_bias"].rearrange("(o e) -> o e", o=1).broadcast_to([NQ, E1])
                     ).then_inc(router_loaded, 16)
        for dst, name in ((swg, "SWg"), (swu, "SWu"), (swd, "SWd")):
            sp.dma_start(dst, a["L1_ffn_" + name].rearrange("(c p) n -> p c n", p=P)).then_inc(sh_loaded, 16)

    def sp_experts1(sp):
        sp.wait_ge(list_ready, 1)
        total = sp.value_load(n_used[0:1, 0:1], min_val=0, max_val=E1)
        with sp.Fori(0, E1 // (2 * PAIRS)) as o:
            with sp.If(2 * PAIRS * o < total):
                with sp.Fori(0, PAIRS) as k:
                    i = o * PAIRS + k
                    with sp.If(2 * i < total):
                        for p in range(2):
                            n = 2 * i + p
                            e = sp.value_load(expert_list[0:1, bass.ds(n, 1)], min_val=0, max_val=E1 - 1)
                            sp.wait_ge(we_split, 4 * i + p + 3)
                            for at, name in ((0, "Wg"), (2 * H1, "Wu")):
                                sp.dma_start(we[p][:, at:at + 2 * H1].rearrange("q (c h) -> q c h", c=2),
                                             a["L1_ffn_" + name].rearrange("e (c q) h -> q (e c) h", q=P)[
                                                 :, bass.ds(2 * e, 2), :]).then_inc(we_loaded[p], 16)
                            sp.dma_start(we[p][:, WGU:WALL], a["L1_ffn_Wd"].rearrange("e q d -> (e q) d")[
                                bass.ds(e * H1, H1), :]).then_inc(we_loaded[p], 16)

    def pe_gate1(pe):
        pe.wait_ge(router_loaded, 32)
        pe.wait_ge(A1.added, B + 1)
        for c in range(2):
            last = nc.tensor.transpose(r_wT_ps[:, c, :], router_rows[:, c * P:(c + 1) * P], ident[0:E1, 0:E1])
        last.then_inc(r_wT_in_psum, 1)
        pe.wait_ge(r_wT_ready, 1)
        for b in range(B):
            pe.wait_ge(xn_ready, 3 * B + b + 1)
            for c in range(2):
                last = nc.tensor.transpose(xnT_all_ps[b // 2][:, b % 2, c, :], z_all[:, b + 1, c * P:(c + 1) * P],
                                           ident[0:NQ, 0:NQ])
            last.then_inc(xnT_in_psum, 1)
        for b in range(B):
            pe.wait_ge(xnT_ready, 3 * B + 2 * (b // 2) + 2)
            for c in range(2):
                last = nc.tensor.matmul(r_logits_ps[:, b, :], xnT_all[:, c, b * NQ:(b + 1) * NQ], routerT[:, c, :],
                                        start=(c == 0), stop=(c == 1))
            last.then_inc(gate_logits, 1)

    def pe_shared(pe):
        pe.wait_ge(sh_loaded, 48)
        pe.wait_ge(xnT_ready, 4 * B)
        for m in range(2):
            for half in range(2):
                for k, w in enumerate((swg, swu)):
                    if m == 1:
                        pe.wait_ge((sh_g_taken, sh_u_taken)[k], half + 1)
                    for c in range(2):
                        last = nc.tensor.matmul(gu_ps[2 * half + k], w[:, c, m * P:(m + 1) * P],
                                                xnT_all[:, c, half * HT:(half + 1) * HT], start=(c == 0), stop=(c == 1))
                    last.then_inc(sh_in_psum, 1)
        pe.wait_ge(r_taken, 1)
        nc.tensor.matmul(r_count_ps, taken[:, :], ones_sq[0:NQ, 0:1], start=True, stop=True).then_inc(r_counted, 1)
        pe.wait_ge(r_used, 1)
        nc.tensor.matmul(r_before_ps, earlier[0:E1, 0:E1], used[:, 0:1], start=True, stop=True)
        nc.tensor.matmul(r_total_ps, ones_sq[0:E1, 0:E1], used[:, 0:1], start=True, stop=True).then_inc(r_placed, 1)
        pe.wait_ge(sh_h_ready, 4)
        for b in range(B):
            for m in range(2):
                last = nc.tensor.matmul(sh_y_ps[b // 2][:, b % 2, :], sh_hT[:, m, b * NQ:(b + 1) * NQ], swd[:, m, :],
                                        start=(m == 0), stop=(m == 1))
            if b % 2 == 1:
                last.then_inc(sh_y_in_psum, 1)
            if b == 1:
                pe.wait_ge(r_place_ready, 1)
                nc.tensor.matmul(r_list_ps, e_col[:, 0:1], place[:, :], start=True, stop=True).then_inc(r_listed, 1)

    def act_shared(act):
        act.wait_ge(r_wT_in_psum, 1)
        nc.scalar.activation(routerT, r_wT_ps, ACT.Copy).then_inc(r_wT_ready, 1)
        for k in range(B // 2):
            act.wait_ge(xnT_in_psum, 3 * B + 2 * k + 2)
            nc.scalar.activation(xnT_all[:, :, 2 * k * NQ:2 * (k + 1) * NQ].rearrange("p c (b n) -> p b c n", b=2),
                                 xnT_all_ps[k], ACT.Copy).then_inc(xnT_ready, 2)
        act.wait_ge(xnT_ready, 4 * B)
        nc.scalar.activation(xT_high, xnT_all, ACT.Copy).then_inc(x_high_ready, 1)
        act.wait_ge(gate_logits, 2 * B)
        nc.scalar.activation(scores1, r_logits_ps, ACT.Sigmoid).then_inc(r_scores, 1)
        for m in range(2):
            for half in range(2):
                n = 2 * m + half
                if m == 1:
                    act.wait_ge(sh_h_ready, half + 1)
                act.wait_ge(sh_in_psum, 2 * n + 1)
                nc.scalar.activation(sh_g[half], gu_ps[2 * half], ACT.Silu).then_inc(sh_g_taken, 1)
                act.wait_ge(sh_in_psum, 2 * n + 2)
                nc.scalar.activation(sh_u[half], gu_ps[2 * half + 1], ACT.Copy).then_inc(sh_u_taken, 1)
        for k in range(4):
            act.wait_ge(sh_y_in_psum, k + 1)
            nc.scalar.activation(sh_y[:, 2 * k:2 * k + 2, :], sh_y_ps[k], ACT.Copy).then_inc(sh_y_taken, 1)

    def pool_shared(pool):
        pool.wait_ge(x_high_ready, 1)
        nc.gpsimd.tensor_tensor(xT_low, xnT_all, xT_high.bitcast(F32), ALU.subtract).then_inc(x_low_ready, 1)
        for m in range(2):
            for half in range(2):
                n = 2 * m + half
                pool.wait_ge(sh_g_taken, n + 1)
                pool.wait_ge(sh_u_taken, n + 1)
                nc.gpsimd.tensor_tensor(sh_hT[:, m, half * HT:(half + 1) * HT], sh_g[half], sh_u[half], ALU.mult
                                        ).then_inc(sh_h_ready, 1)

    def dve_route1(dve):

        dve.wait_ge(r_scores, 1)
        dve.wait_ge(router_loaded, 32)
        dve.wait_ge(consts_ready, N_CONSTS + N_MOE_CONSTS + 5 + 2)
        step(dve, nc.vector.tensor_tensor(sfc, scores1, e_bias[:, :].unsqueeze(1).broadcast_to([NQ, B, E1]), ALU.add))
        eights = sfc.rearrange("q b (g k) -> q (b g) k", k=G1)
        grid = lambda k, n: group2[:, k, 0:B * G1 * n].rearrange("q (g n) -> q g n", n=n)
        high, low = grid(0, 4), grid(1, 4)
        nc.vector.tensor_tensor(high, eights[:, :, 0:4], eights[:, :, 4:8], ALU.max)
        step(dve, nc.vector.tensor_tensor(low, eights[:, :, 0:4], eights[:, :, 4:8], ALU.min))
        for n, to in ((2, 2), (1, 0)):
            top, second = grid(to, n), grid(to + 1, n)
            below = work1.rearrange("q b e -> q (b e)")[:, 0:B * G1 * n].rearrange("q (g n) -> q g n", n=n)
            nc.vector.tensor_tensor(top, high[:, :, 0:n], high[:, :, n:2 * n], ALU.max)
            nc.vector.tensor_tensor(below, high[:, :, 0:n], high[:, :, n:2 * n], ALU.min)
            step(dve, nc.vector.tensor_tensor(second, low[:, :, 0:n], low[:, :, n:2 * n], ALU.max))
            step(dve, nc.vector.tensor_tensor(second, second, below, ALU.max))
            high, low = top, second
        step(dve, nc.vector.tensor_tensor(group_sum[:, :, :].rearrange("q b (g o) -> q (b g) o", o=1), high, low, ALU.add))
        ij = lambda t: t.rearrange("q b (i j) -> q b i j", j=G1)
        mine = group_sum[:, :, :].unsqueeze(3).broadcast_to([NQ, B, G1, G1])
        other = group_sum[:, :, :].unsqueeze(2).broadcast_to([NQ, B, G1, G1])
        nc.vector.tensor_tensor(ij(work1), other, mine, ALU.is_gt)
        step(dve, nc.vector.tensor_tensor(ij(work2), other, mine, ALU.is_equal))
        step(dve, nc.vector.tensor_tensor(ij(work2), ij(work2),
                                     below8[0:NQ, :, :].unsqueeze(1).broadcast_to([NQ, B, G1, G1]), ALU.mult))
        step(dve, nc.vector.tensor_tensor(work1, work1, work2, ALU.add))
        step(dve, nc.vector.tensor_reduce(group_kept[:, :, :], ij(work1), AX.X, ALU.add))
        step(dve, nc.vector.tensor_scalar(group_kept[:, :, :], group_kept[:, :, :], float(TOPG), None, ALU.is_lt))
        step(dve, nc.vector.tensor_tensor(sfc.rearrange("q b (g k) -> q b g k", k=G1),
                                     sfc.rearrange("q b (g k) -> q b g k", k=G1),
                                     group_kept[:, :, :].unsqueeze(3).broadcast_to([NQ, B, G1, G1]), ALU.mult))
        for b in range(B):
            last = nc.vector.max(top8[:, b, :], sfc[:, b, :])
        step(dve, last)
        for b in range(B):
            last = nc.vector.match_replace(out=picked[:, b, :], in_to_replace=top8[:, b, :], in_values=sfc[:, b, :],
                                           imm_value=-FLT_MAX)
        step(dve, last)
        step(dve, nc.vector.tensor_scalar(picked, picked, -FLT_MAX, None, ALU.is_equal))
        step(dve, nc.vector.tensor_reduce(taken[:, :], picked.rearrange("q b e -> q e b"), AX.X, ALU.add))
        dve.sem_inc(r_taken, 1)
        step(dve, nc.vector.tensor_tensor(work1, scores1, picked, ALU.mult))
        dve.wait_ge(r_counted, 1)
        nc.vector.tensor_scalar(used[:, 0:1], r_count_ps, 0.0, None, ALU.is_gt).then_inc(r_used, 1)
        step(dve, nc.vector.tensor_reduce(weight_sum[:, :], work1, AX.X, ALU.add))
        dve.wait_ge(r_placed, 1)
        step(dve, nc.vector.tensor_scalar(used[:, 2:3], r_total_ps, e_col[:, 0:1], r_before_ps, ALU.add, ALU.subtract))
        step(dve, nc.vector.tensor_tensor(used[:, 1:2], r_before_ps, used[:, 2:3], ALU.subtract))
        step(dve, nc.vector.scalar_tensor_tensor(used[:, 1:2], used[:, 1:2], used[:, 0:1], used[:, 2:3], ALU.mult, ALU.add))
        nc.vector.tensor_copy(n_used[:, :], r_total_ps[0:1, :])
        nc.vector.tensor_scalar(place[:, :], iota64[:, :], used[:, 1:2], None, ALU.is_equal).then_inc(r_place_ready, 1)
        step(dve, nc.vector.tensor_scalar(weight_sum[:, :], weight_sum[:, :], 1e-20, None, ALU.add))
        step(dve, nc.vector.reciprocal(weight_sum[:, :], weight_sum[:, :]))
        step(dve, nc.vector.scalar_tensor_tensor(coef, work1, SCALE2, weight_sum[:, :].unsqueeze(2).broadcast_to([NQ, B, E1]),
                                            ALU.mult, ALU.mult))
        dve.wait_ge(r_listed, 1)
        nc.vector.tensor_copy(expert_list[:, :], r_list_ps).then_inc(list_ready, 1)

    def pe_experts1(pe):
        pe.wait_ge(list_ready, 1)
        pe.wait_ge(sh_y_taken, 4)
        pe.wait_ge(x_low_ready, 1)
        pe.sem_inc(gu_in_psum, 8)
        pe.sem_inc(y1_in_psum, 8)

        def gate_up(i, p):
            n = 2 * i + p
            pe.wait_ge(we_split, 4 * i + p + 1 + 4)
            for half in range(2):
                tok = slice(half * HT, (half + 1) * HT)
                pe.wait_ge(h1_full, 2 * n + half + 1)
                for k in range(2):
                    for c in range(2):
                        col = slice((2 * k + c) * H1, (2 * k + c + 1) * H1)
                        ps = gu_ps[2 * half + k]
                        nc.tensor.matmul(ps, we_high[p][:, col], xT_high[:, c, tok], start=(c == 0), stop=False)
                        nc.tensor.matmul(ps, we_high[p][:, col], xT_low[:, c, tok], start=False, stop=False)
                        last = nc.tensor.matmul(ps, we_low[p][:, col], xT_high[:, c, tok], start=False, stop=(c == 1))
                    last.then_inc(gu_in_psum, 1)

        def down(i, p):
            n = 2 * i + p
            pe.wait_ge(we_split, 4 * i + 2 + p + 1 + 4)
            for k in range(4):
                if k % 2 == 0:
                    pe.wait_ge(h1_ready, 2 * n + k // 2 + 1 + 2)
                pe.wait_ge(y1_added, 4 * n + k + 1)
                for bb in range(2):
                    b = 2 * k + bb
                    tok = slice(b * NQ, (b + 1) * NQ)
                    ps = y1_ps[k][:, bb, :]
                    nc.tensor.matmul(ps, h1_high[p][:, tok], we_high[p][:, WGU:WALL], start=True, stop=False)
                    nc.tensor.matmul(ps, h1_high[p][:, tok], we_low[p][:, WGU:WALL], start=False, stop=False)
                    last = nc.tensor.matmul(ps, h1_low[p][:, tok], we_high[p][:, WGU:WALL], start=False, stop=True)
                last.then_inc(y1_in_psum, 1)

        total = pe.value_load(n_used[0:1, 0:1], min_val=0, max_val=E1)
        with pe.Fori(0, E1 // (2 * PAIRS)) as o:
            with pe.If(2 * PAIRS * o < total):
                with pe.Fori(0, PAIRS) as k:
                    i = o * PAIRS + k
                    with pe.If(2 * i < total):
                        for p in range(2):
                            gate_up(i, p)
                        for p in range(2):
                            down(i, p)

    def act_experts1(act):
        def split_gate_up(i, p):
            act.wait_ge(we_loaded[p], 48 * i + 48)
            act.wait_ge(gu_in_psum, 4 * (2 * i + p) + 4)
            nc.scalar.activation(we_high[p][:, 0:WGU], we[p][:, 0:WGU], ACT.Copy).then_inc(we_high_ready, 1)

        def split_down(i, p):
            act.wait_ge(y1_in_psum, 4 * (2 * i + p) + 4)
            nc.scalar.activation(we_high[p][:, WGU:WALL], we[p][:, WGU:WALL], ACT.Copy).then_inc(we_high_ready, 1)

        def hidden(i, p):
            n = 2 * i + p
            for half in range(2):
                act.wait_ge(gu_in_psum, 4 * n + 2 * half + 1 + 8)
                act.wait_ge(h1_full, 2 * n + half + 1)
                nc.scalar.activation(g_act[half], gu_ps[2 * half], ACT.Silu).then_inc(silu_done, 1)
                act.wait_ge(h1_full, 2 * n + half + 1 + 2)
                tok = slice(half * HT, (half + 1) * HT)
                nc.scalar.activation(h1_high[p][:, tok], h1T[:, tok], ACT.Copy).then_inc(h1_high_ready, 1)

        act.wait_ge(list_ready, 1)
        total = act.value_load(n_used[0:1, 0:1], min_val=0, max_val=E1)
        with act.Fori(0, E1 // (2 * PAIRS)) as o:
            with act.If(2 * PAIRS * o < total):
                with act.Fori(0, PAIRS) as k:
                    i = o * PAIRS + k
                    with act.If(2 * i < total):
                        for p in range(2):
                            split_gate_up(i, p)
                        for p in range(2):
                            split_down(i, p)
                        for p in range(2):
                            hidden(i, p)

    def pool_experts1(pool):
        def split(i, p, part, cols):
            pool.wait_ge(we_high_ready, 4 * i + 2 * part + p + 1)
            nc.gpsimd.tensor_tensor(we_low[p][:, cols], we[p][:, cols], we_high[p][:, cols].bitcast(F32), ALU.subtract
                                    ).then_inc(we_split, 1)

        def hidden(i, p):
            n = 2 * i + p
            for half in range(2):
                tok = slice(half * HT, (half + 1) * HT)
                pool.wait_ge(h1_high_ready, 2 * n + half + 1)
                pool.wait_ge(y1_in_psum, 4 * n + 4)
                nc.gpsimd.tensor_tensor(h1_low[p][:, tok], h1T[:, tok], h1_high[p][:, tok].bitcast(F32), ALU.subtract
                                        ).then_inc(h1_ready, 1)

        pool.wait_ge(list_ready, 1)
        pool.sem_inc(we_split, 4)
        pool.sem_inc(h1_ready, 2)
        total = pool.value_load(n_used[0:1, 0:1], min_val=0, max_val=E1)
        with pool.Fori(0, E1 // (2 * PAIRS)) as o:
            with pool.If(2 * PAIRS * o < total):
                with pool.Fori(0, PAIRS) as k:
                    i = o * PAIRS + k
                    with pool.If(2 * i < total):
                        for p in range(2):
                            split(i, p, 0, slice(0, WGU))
                        for p in range(2):
                            split(i, p, 1, slice(WGU, WALL))
                        for p in range(2):
                            hidden(i, p)

    def dve_experts1(dve):
        def hidden(i, p):
            n = 2 * i + p
            for half in range(2):
                dve.wait_ge(silu_done, 2 * n + half + 1)
                dve.wait_ge(gu_in_psum, 4 * n + 2 * half + 2 + 8)
                dve.wait_ge(h1_ready, 2 * n + half + 1)
                nc.vector.tensor_tensor(h1T[:, half * HT:(half + 1) * HT], g_act[half], gu_ps[2 * half + 1], ALU.mult
                                        ).then_inc(h1_full, 1)

        def add(i, p):
            n = 2 * i + p
            e = dve.value_load(expert_list[0:1, bass.ds(n, 1)], min_val=0, max_val=E1 - 1)
            for k in range(4):
                dve.wait_ge(y1_in_psum, 4 * n + k + 1 + 8)
                dve.wait_ge(y1_added, 4 * n + k + 1)
                for bb in range(2):
                    b = 2 * k + bb
                    last = nc.vector.scalar_tensor_tensor(
                        x[:, b + 1, :], y1_ps[k][:, bb, :], coef[:, b, bass.ds(e, 1)], x[:, b + 1, :],
                        ALU.mult, ALU.add)
                last.then_inc(y1_added, 1)

        dve.wait_ge(sh_y_taken, 4)
        nc.vector.tensor_tensor(x[:, 1:B + 1, :], x[:, 1:B + 1, :], sh_y, ALU.add).then_inc(sh_added, 1)
        dve.wait_ge(sh_added, 1)
        dve.wait_ge(list_ready, 1)
        dve.sem_inc(h1_full, 2)
        dve.sem_inc(y1_added, 4)
        total = dve.value_load(n_used[0:1, 0:1], min_val=0, max_val=E1)
        with dve.Fori(0, E1 // (2 * PAIRS)) as o:
            with dve.If(2 * PAIRS * o < total):
                with dve.Fori(0, PAIRS) as k:
                    i = o * PAIRS + k
                    with dve.If(2 * i < total):
                        for p in range(2):
                            hidden(i, p)
                        for p in range(2):
                            add(i, p)
        nc.vector.memset(row_max[:, :], 0.0).then_inc(x_final, 1)

    with nc.Block() as block:
        @block.sync
        def _(sp):
            sp_load0(sp)
            sp_project0(sp)
            sp_load1(sp)

            def v0_ready(e):
                e.wait_ge(v_stored, 2 * B)
                e.wait_ge(consts_ready, N_CONSTS)
            sp_attend(sp, A0, v0_ready)
            sp_load_moe(sp)
            sp_load1_weights(sp)
            sp_experts(sp)
            sp_project1(sp)

            def v1_ready(e):
                e.wait_ge(v1_stored, 3 * B)
                e.wait_ge(null_v_stored, 16 * 8)
            sp_attend(sp, A1, v1_ready)
            sp_load_ffn1(sp)
            sp_experts1(sp)
            sp.wait_ge(x_final, 1)
            sp.dma_start(a["out"].rearrange("b q d -> q b d"), x[:, 1:B + 1, :]).then_inc(out_stored, 16)
            sp.wait_ge(out_stored, 16)

        @block.gpsimd
        def _(pool):
            pool_consts(pool)

            def q0_ready(e):
                e.wait_ge(q_stored, 2 * B)
                e.wait_ge(consts_ready, N_CONSTS)
            pool_consts_moe(pool)
            pool_consts1(pool)
            pool_consts_ffn1(pool)
            pool_attend(pool, A0, q0_ready, headmask[:, :])
            pool_dispatch(pool)
            pool_split_weights1(pool)
            pool_combine(pool)
            pool_clear1(pool)
            pool_mask_clear(pool)

            def q1_ready(e):
                e.wait_ge(qT1_stored, B + 1)
                e.wait_ge(kT1_in_psum, 3 * B)
                e.wait_ge(kq1_cleared, 2)
            pool_attend(pool, A1, q1_ready, halfmask[:, :])
            pool_shared(pool)
            pool_experts1(pool)

        @block.vector
        def _(dve):
            dve_project0(dve)
            dve_attend(dve, A0)
            dve_gate(dve)
            dve_experts(dve)
            dve_project1(dve)
            dve_attend(dve, A1)
            dve_add1(dve)
            dve_route1(dve)
            dve_experts1(dve)

        @block.scalar
        def _(act):
            act_project0(act)
            act_attend(act, A0)
            act_gate(act)
            act_split_weights1(act)
            act_experts(act)
            act_project1(act)
            act_attend(act, A1)
            act_add1(act)
            act_shared(act)
            act_experts1(act)

        @block.tensor
        def _(pe):
            pe_project0(pe)

            def p0_ready(e):
                e.wait_ge(q_stored, 2 * B)
                e.wait_ge(k_stored, 2 * B)
                e.wait_ge(v_stored, 2 * B)
                e.wait_ge(A0.out_cleared, 1)
                e.wait_ge(wo0_loaded, 32)
            pe_attend(pe, A0, p0_ready)
            pe_gate(pe)
            pe_experts(pe)
            pe_project1(pe)

            def p1_ready(e):
                e.wait_ge(qT1_stored, B + 1)
                e.wait_ge(kT1_stored, 3 * B + 3)
                e.wait_ge(v1_stored, 3 * B)
                e.wait_ge(null_k_stored, 1)
                e.wait_ge(ctxT_split, B + 1)
                e.wait_ge(kq1_cleared, 2)
            pe_attend(pe, A1, p1_ready)
            pe_gate1(pe)
            pe_shared(pe)
            pe_experts1(pe)


_INS = ["x", "ctx_768", "mask_BxS2_bf1", "L0_xattn_Wq", "L0_xattn_bq", "L0_xattn_Wk", "L0_xattn_bk", "L0_xattn_Wv",
        "L0_xattn_bv", "L0_xattn_Wo", "L0_xattn_bo", "L0_ffn_Wg", "L0_ffn_bg", "L0_ffn_W1", "L0_ffn_b1", "L0_ffn_W2",
        "L0_ffn_b2", "L1_xattn_g_norm", "L1_xattn_Wq", "L1_xattn_Wkv", "L1_xattn_null_kv", "L1_xattn_q_scale",
        "L1_xattn_k_scale", "L1_xattn_Wo", "L1_xattn_g_out", "L1_ffn_router_w", "L1_ffn_e_bias", "L1_ffn_Wg",
        "L1_ffn_Wu", "L1_ffn_Wd", "L1_ffn_SWg", "L1_ffn_SWu", "L1_ffn_SWd"]


def kernel(**inputs):
    import concourse.bacc as _bacc
    from concourse.bass_utils import run_bass_kernel_spmd as _run

    nc = _bacc.Bacc("TRN2", target_bir_lowering=False, num_devices=1)
    arrays, aps = {}, {}
    for name in _INS:
        array = np.ascontiguousarray(inputs[name])
        if array.dtype == np.bool_:
            array = array.view(np.uint8)
        arrays[f"in_{name}_dram"] = array
        aps[name] = nc.dram_tensor(f"in_{name}_dram", array.shape, mybir.dt.from_np(array.dtype),
                                   kind="ExternalInput").ap()
    aps["out"] = nc.dram_tensor("out_0_dram", (B, NQ, D), F32, kind="ExternalOutput").ap()
    build(nc, aps)
    r = _run(nc, [arrays], core_ids=[0])
    return r.results[0]["out_0_dram"]
```

```python
import numpy as np
import concourse.bass as bass
from concourse import mybir

F32 = mybir.dt.float32
F32R = mybir.dt.float32r
I32 = mybir.dt.int32
U32 = mybir.dt.uint32
U8 = mybir.dt.uint8
ACT = mybir.ActivationFunctionType
ALU = mybir.AluOpType
AX = mybir.AxisListType

P = 128
B, NQ, D = 8, 100, 256
NKV, DC = 361, 192
DCC = DC // 2
FULL, TAIL = 2, NKV - 2 * P
EPS = 1e-5
CLAMP = 10000.0
SCALE0 = 16 ** -0.5
LOOK = 3
AHEAD = 2
NPB = 4
SLOT_V = 3 * 512


def build(nc, a):
    sb = nc.alloc_sbuf_tensor
    sem = nc.alloc_semaphore

    psum = nc.alloc_psum_tensor("psum", [P, 8, 512], F32)
    x = sb("x", [NQ, B + 1, D], F32)
    ident = sb("ident", [P, P], F32)
    ones_row = sb("ones_row", [1, P], F32)
    eps_col = sb("eps_col", [P, 1], F32)
    stats = sb("stats", [NQ, B + 1, 6], F32)
    mv = sb("mv", [NQ, B, 2], F32)
    rstd = sb("rstd", [NQ, B], F32)
    std = sb("std", [NQ, B], F32)
    keys_at = nc.sbuf_base
    kT_all = sb("kT_all", [P, 4 * (B + 1) * (NKV + 1)], F32)
    vals_at = nc.sbuf_base
    v_all = sb("v_all", [P, B, 3, 512], F32)
    qT_all = sb("qT_all", [P, 4 * (B + 1) * NQ], F32)
    qm_at = nc.sbuf_base
    qm = [sb(f"qm{p}", [P, 16, NQ], F32) for p in range(2)]
    vs = [sb(f"vs{p}", [P, 3, 512], F32) for p in range(2)]
    probs_at = nc.sbuf_base
    probs = sb("probs", [NQ, NPB, 2, NKV + 1], F32)
    negmax = sb("negmax", [NQ, NPB, 2], F32)
    sums = sb("sums", [NQ, 2, 16], F32)
    inv_sums = sb("inv_sums", [NQ, 16], F32)
    probsT = [sb("probsT0", [P, 3, 2 * NQ], F32)]
    probsT1_at = nc.sbuf_base
    probsT.append(sb("probsT1", [P, 3, 2 * NQ], F32))
    oT = sb("oT", [P, 4, NQ], F32)
    o_tok = sb("o_tok", [NQ, 512], F32)
    o_tokT = sb("o_tokT", [P, 4, NQ], F32)

    ctx_nat = [sb(f"ctx_nat{p}", [P, 3, DC], F32) for p in range(2)]
    ctxT_at = nc.sbuf_base
    ctxT = sb("ctxT", [DCC + 1, 2, NKV], F32)
    ctxT0 = [ctxT[:, :, :], probs[0:DCC + 1].rearrange("q a b n -> q (a b n)")[:, 0:2 * NKV].rearrange(
        "q (c n) -> q c n", c=2)]
    CTX0 = B + 1
    xn = sb("xn", [NQ, D], F32)
    xnT = sb("xnT", [P, 2, NQ], F32)

    headmask = sb("headmask", [P, 8], F32)
    early = sb("early", [P, (B + 1) * D], F32)
    wq0, wk0, wv0, wo0 = (early[:, k * 2 * D:(k + 1) * 2 * D].rearrange("p (c n) -> p c n", c=2) for k in range(4))
    wk0 = wk0[0:DCC]
    wv0 = wv0[0:DCC + 1]
    z_all = early[0:NQ, :].rearrange("q (b d) -> q b d", d=D)
    bq0 = sb("bq0", [P, 2], F32)
    bq0s = sb("bq0s", [P, 2], F32)
    bk0 = sb("bk0", [P, 2], F32)
    bo0 = sb("bo0", [1, D], F32)

    E0, H0 = 8, 1024
    HC = H0 // P
    NBLK = (B * NQ + E0 * P - 1) // P
    MAXB = -(-B * NQ // P)
    keys_arena = kT_all[:, :]
    vals_arena = v_all[:, :, :, :].rearrange("p b t n -> p (b t n)")

    def carve(arena, at, shape):
        n = int(np.prod(shape))
        view = arena[:, at[0]:at[0] + n]
        at[0] += n
        names = " ".join("abc"[:len(shape)])
        return view.rearrange(f"p ({names}) -> p {names}", **{k: v for k, v in zip("abc", shape)})

    def carve_r(name, base, at, shape):
        n = int(np.prod(shape))
        view = nc.alloc_sbuf_tensor_at(name, [P, n], F32R, offset=base + 4 * at[0])[:, :]
        at[0] += n
        names = " ".join("abc"[:len(shape)])
        return view.rearrange(f"p ({names}) -> p {names}", **{k: v for k, v in zip("abc", shape)})
    at_k, at_v = [0], [0]
    w1_e = [carve(vals_arena, at_v, (2, H0)) for _ in range(2)]
    w2_e = [carve(vals_arena, at_v, (HC, D)) for _ in range(2)]
    xn_all = carve(keys_arena, at_k, (B, D))[0:NQ]
    xnT0 = carve(keys_arena, at_k, (2, B * NQ))
    xs_rows = carve(keys_arena, at_k, (D,))
    xsT = carve(keys_arena, at_k, (2, P))
    hT = carve(keys_arena, at_k, (HC, P))
    ys_rows = carve(keys_arena, at_k, (D,))
    b1_rows = carve(keys_arena, at_k, (P,))[0:E0 * HC]
    b1_all = carve(keys_arena, at_k, (E0 + 1, HC))
    b1_col = [carve(keys_arena, at_k, (HC,)) for _ in range(2)]
    b2_row = carve(keys_arena, at_k, (E0 * D,))[0:1]
    wg0 = sb("wg0", [P, 2, E0], F32)
    bg0 = sb("bg0", [NQ, E0], F32)
    earlier = sb("earlier", [NQ, NQ], F32)
    ones_sq = sb("ones_sq", [NQ, P], F32)
    below8 = sb("below8", [P, 8, 8], F32)
    iota16 = sb("iota16", [P, 16], F32)
    logits = sb("logits", [NQ, B, E0], F32)
    top_logit = sb("top_logit", [NQ, B], F32)
    top_weight = sb("top_weight", [NQ, B], F32)
    choice = sb("choice", [NQ, B, E0], F32)
    route_a = sb("route_a", [P, B * E0 * 8], F32)
    route_b = sb("route_b", [P, B, E0], F32)
    counts = sb("counts", [P, B, E0], F32)
    per_expert = sb("per_expert", [P, 4, E0], F32)
    per_expert_i = sb("per_expert_i", [P, 3, E0], I32)
    block_starts = sb("block_starts", [P, MAXB], F32)
    slot_f = sb("slot_f", [NQ, B], F32)
    slot = sb("slot", [NQ, B], U32)
    zeros = sb("zeros", [P, D], F32)
    xs_dram = nc.dram_tensor("xs_dram", [(NBLK + 2) * P, D], F32, kind="Internal").ap()
    ys_dram = nc.dram_tensor("ys_dram", [NBLK * P, D], F32, kind="Internal").ap()

    HD1, SCALE1 = 64, 8.0
    FLT_MAX = float(np.finfo(np.float32).max)
    flat = lambda t: t[:, :, :].rearrange("p a b -> p (a b)")
    two = lambda v: v[:, 0:1024].rearrange("p (c n) -> p c n", c=2)
    wk1, wv1 = (two(vals_arena[:, 6 * SLOT_V + k * 1024:])[0:DCC] for k in range(2))
    wk1_high, wk1_low, wv1_high, wv1_low = (
        two(nc.alloc_sbuf_tensor_at(n, [DCC, 1024], F32R, offset=qm_at + 4 * 1024 * k)[:, :])
        for k, n in enumerate(("wk1_high", "wk1_low", "wv1_high", "wv1_low")))
    ctxT_full = nc.alloc_sbuf_tensor_at("ctxT_full", [DCC, 2, NKV], F32, offset=qm_at + 4 * 1024 * 4)
    wq1 = two(early[:, :])
    k_tok_full = early[:, 1024:2048].rearrange("p (t n) -> p t n", t=2)
    k_tok = [k_tok_full[:, 0, :], k_tok_full[:, 1, :], flat(probsT[0])[:, 0:512]]
    probs_row = probs[:, :, :, :].rearrange("q a b n -> q (a b n)")
    y_tok = probs_row[:, 0:2 * D].rearrange("q (p d) -> q p d", p=2)
    y_row = probs_row[:, 2 * D:3 * D]
    ctxT_high, ctxT_low = ([nc.alloc_sbuf_tensor_at(f"ctxT_{n}{p}", [DCC, 2, NKV], F32R, offset=at[p])
                            for p in range(2)] for n, at in (
        ("high", (ctxT_at, probs_at + 4 * (3 * D + 2 * (NKV + 3)))),
        ("low", (probs_at + 4 * 3 * D, probsT1_at))))
    mask_bias = [flat(ctx_nat[p])[0:NQ, 0:NKV + 1] for p in range(2)]
    wo1 = sb("wo1", [P, 4, D], F32)
    g_norm = sb("g_norm", [NQ, D], F32)
    g_out = sb("g_out", [NQ, D], F32)
    turn = sb("turn", [NQ, NPB], F32)
    pool_turn = sb("pool_turn", [1, 1], F32)
    flt_max = sb("flt_max", [NQ, 1], F32)
    mask_u8 = sb("mask_u8", [NQ, B + 1, NKV], U8)
    null_row = sb("null_row", [P, HD1], F32)
    null_col = sb("null_col", [P, 1], F32)
    null_ss = sb("null_ss", [P, 1], F32)
    q_scale_col = sb("q_scale_col", [P, 1], F32)
    k_scale_col = sb("k_scale_col", [P, 1], F32)
    halfmask = sb("halfmask", [P, 2], F32)
    key_ss = sb("key_ss", [P, 3, 8], F32)
    q_ss = sb("q_ss", [NQ, 8], F32)
    row_max = sb("row_max", [NQ, B], F32)
    top_out = sb("top_out", [NQ, 1], F32)

    E1, H1, HS = 64, 128, 256
    G1, TOPG, SCALE2 = 8, 4, 2.5
    HT = B * NQ // 2
    PAIRS = 8
    at_k, at_v = [0], [0]
    xnT_all = carve(keys_arena, at_k, (2, B * NQ))
    xT_high = carve_r("xT_high", keys_at, at_k, (2, B * NQ))
    xT_low = carve_r("xT_low", keys_at, at_k, (2, B * NQ))
    g_act = [carve(keys_arena, at_k, (HT,)) for _ in range(2)]
    sh_hT = carve(keys_arena, at_k, (2, B * NQ))
    coefT = keys_arena[0:E1, at_k[0]:at_k[0] + B * NQ]
    sh_g = [carve(keys_arena, at_k, (HT,)) for _ in range(2)]
    sh_u = [carve(keys_arena, at_k, (HT,)) for _ in range(2)]
    coef_rows = [carve(keys_arena, at_k, (B * NQ,)) for _ in range(2)]
    coefT_dram = nc.dram_tensor("coefT_dram", [E1, B * NQ], F32, kind="Internal").ap()
    scores1 = carve(keys_arena, at_k, (B, E1))[0:NQ]
    sfc = carve(keys_arena, at_k, (B, E1))[0:NQ]
    picked = carve(keys_arena, at_k, (B, E1))[0:NQ]
    work1 = carve(keys_arena, at_k, (B, E1))[0:NQ]
    swg = carve(vals_arena, at_v, (2, HS))
    swu = carve(vals_arena, at_v, (2, HS))
    swd = carve(vals_arena, at_v, (2, D))
    router_rows = carve(vals_arena, at_v, (D,))[0:E1]
    routerT = carve(vals_arena, at_v, (2, E1))
    WGU, WALL = 4 * H1, 4 * H1 + D
    we = [carve(vals_arena, at_v, (WALL,)) for _ in range(2)]
    we_high = [carve_r(f"we_high{p}", vals_at, at_v, (WALL,)) for p in range(2)]
    we_low = [carve_r(f"we_low{p}", vals_at, at_v, (WALL,)) for p in range(2)]
    h1T = carve(vals_arena, at_v, (B * NQ,))
    h1_high = [carve_r(f"h1_high{p}", vals_at, at_v, (B * NQ,)) for p in range(2)]
    group2 = vals_arena[0:NQ, at_v[0]:at_v[0] + 4 * B * G1 * 4].rearrange("q (k n) -> q k n", k=4)
    h1_low = [carve_r(f"h1_low{p}", vals_at, at_v, (B * NQ,)) for p in range(2)]
    coef = carve(vals_arena, at_v, (B, E1))[0:NQ]
    work2 = carve(vals_arena, at_v, (B, E1))[0:NQ]
    e_bias = carve(vals_arena, at_v, (E1,))[0:NQ]
    iota64 = sb("iota64", [E1, E1], F32)
    e_col = sb("e_col", [E1, 1], F32)
    group_sum = carve(vals_arena, at_v, (B, G1))[0:NQ]
    group_kept = carve(vals_arena, at_v, (B, G1))[0:NQ]
    top8 = carve(vals_arena, at_v, (B, 8))[0:NQ]
    weight_sum = sb("weight_sum", [NQ, B], F32)
    taken = carve(vals_arena, at_v, (E1,))[0:NQ]
    used = sb("used", [E1, 4], F32)
    place = carve(vals_arena, at_v, (E1,))[0:E1]
    expert_list = sb("expert_list", [1, E1 + 2], I32)
    n_used = sb("n_used", [1, 1], I32)

    consts_ready = sem("consts_ready")
    x_loaded = sem("x_loaded")
    w0_loaded, wo0_loaded = sem("w0_loaded"), sem("wo0_loaded")
    N_W0 = 6
    dve_step = sem("dve_step")
    ln_stats, ln_std = sem("ln_stats"), sem("ln_std")
    bq_scaled = sem("bq_scaled")

    ctx_loaded = [sem(f"ctx_loaded{p}") for p in range(2)]
    ctxT_in_psum, ctxT_ready = sem("ctxT_in_psum"), sem("ctxT_ready")
    xn_ready, xnT_in_psum, xnT_ready = sem("xn_ready"), sem("xnT_in_psum"), sem("xnT_ready")
    k_in_psum, k_stored = sem("k_in_psum"), sem("k_stored")
    v_in_psum, v_stored = sem("v_in_psum"), sem("v_stored")
    q_in_psum, q_stored = sem("q_in_psum"), sem("q_stored")

    gate_loaded, xs_cleared = sem("gate_loaded"), sem("xs_cleared")
    gate_logits = sem("gate_logits")
    g_centred, g_exp = sem("g_centred"), sem("g_exp")
    choice_ready, ranks_ready, slots_ready = sem("choice_ready"), sem("ranks_ready"), sem("slots_ready")
    xs_scattered = sem("xs_scattered")
    rows_used = sem("rows_used")
    b1_in_psum, b1_ready = sem("b1_in_psum"), sem("b1_ready")
    expert_begun = sem("expert_begun")
    experts_taken = sem("experts_taken")
    biases_loaded = sem("biases_loaded")
    xs_loaded, ys_in_psum, ys_stored = sem("xs_loaded"), sem("ys_in_psum"), sem("ys_stored")
    w1_loaded = [sem(f"w1_loaded{p}") for p in range(2)]
    w2_loaded = [sem(f"w2_loaded{p}") for p in range(2)]
    xsT_ready = sem("xsT_ready")
    hidden_in_psum, hidden_ready = sem("hidden_in_psum"), sem("hidden_ready")
    ys_ready = sem("ys_ready")
    y_gathered = [sem(f"y_gathered{p}") for p in range(2)]
    x2_added, x2_step = sem("x2_added"), sem("x2_step")
    w1x_high, w1x_split = sem("w1x_high"), sem("w1x_split")
    ctxT_split = sem("ctxT_split")

    const1_loaded = sem("const1_loaded")
    w1x_loaded = sem("w1x_loaded")
    null_v_stored = sem("null_v_stored")
    kq1_cleared = sem("kq1_cleared")
    mask_null = sem("mask_null")
    mask_ready = sem("mask_ready")
    null_norm = sem("null_norm")
    null_k_stored = sem("null_k_stored")
    v1_in_psum = sem("v1_in_psum")
    v1_stored = sem("v1_stored")
    q1_in_psum = sem("q1_in_psum")
    k1_squared = sem("k1_squared")
    k1_ss = sem("k1_ss")
    k1_norm = sem("k1_norm")
    k1_inv = sem("k1_inv")
    k1_scaled = sem("k1_scaled")
    q1_squared = sem("q1_squared")
    q1_ss = sem("q1_ss")
    q1_norm = sem("q1_norm")
    q1_inv = sem("q1_inv")
    q1_scaled = sem("q1_scaled")
    kT1_stored = sem("kT1_stored")
    kT1_in_psum = sem("kT1_in_psum")
    k1_in_psum = sem("k1_in_psum")
    qT1_stored = sem("qT1_stored")
    qT1_in_psum = sem("qT1_in_psum")
    take_step = sem("take_step")

    sh_loaded = sem("sh_loaded")
    router_loaded = sem("router_loaded")
    r_wT_in_psum = sem("r_wT_in_psum")
    r_wT_ready = sem("r_wT_ready")
    r_scores = sem("r_scores")
    route_step = sem("route_step")
    route_sums = sem("route_sums")
    sh_in_psum = sem("sh_in_psum")
    sh_g_taken = sem("sh_g_taken")
    sh_u_taken = sem("sh_u_taken")
    sh_h_ready = sem("sh_h_ready")
    sh_y_in_psum = sem("sh_y_in_psum")
    sh_added = sem("sh_added")
    x_high_ready = sem("x_high_ready")
    x_low_ready = sem("x_low_ready")
    we_high_ready = sem("we_high_ready")
    we_split = sem("we_split")
    h1_full = sem("h1_full")
    h1_high_ready = sem("h1_high_ready")
    gu_in_psum = sem("gu_in_psum")
    silu_done = sem("silu_done")
    h1_ready = sem("h1_ready")
    y1_in_psum = sem("y1_in_psum")
    coefT_taken, coefT_stored, coef_used = sem("coefT_taken"), sem("coefT_stored"), sem("coef_used")
    coef_loaded = [sem(f"coef_loaded{p}") for p in range(2)]
    experts_done, yT_taken, out_in_psum = sem("experts_done"), sem("yT_taken"), sem("out_in_psum")
    out_stored = sem("out_stored")
    x_final = sem("x_final")
    we_loaded = [sem(f"we_loaded{p}") for p in range(2)]

    class Attn:

        def __init__(s, n, heads, hd, nk, vcols, negated=False):
            s.exp_scale = -1.0 if negated else 1.0
            s.n, s.heads, s.hd, s.nk, s.vcols = n, heads, hd, nk, vcols
            s.ppb = heads // 2
            s.hpc = P // hd
            s.chunks = heads * hd // P
            s.tail = nk - 2 * P
            s.mask_bias = None
            s.kT = kT_all[:, 0:s.chunks * (B + 1) * nk].rearrange("p (c n) -> p c n", c=s.chunks)
            s.qT = qT_all[:, 0:s.chunks * (B + 1) * NQ].rearrange("p (c n) -> p c n", c=s.chunks)
            s.qm_ready = sem(f"L{n}_qm_ready")
            s.scores_ready = sem(f"L{n}_scores_ready")
            s.clipped = sem(f"L{n}_clipped")
            s.max_ready = sem(f"L{n}_max_ready")
            s.exp_done = sem(f"L{n}_exp_done")
            s.transposed = sem(f"L{n}_transposed")
            s.probsT_ready = sem(f"L{n}_probsT_ready")
            s.attended = sem(f"L{n}_attended")
            s.out_taken = sem(f"L{n}_out_taken")
            s.tok_ready = sem(f"L{n}_tok_ready")
            s.inv_ready = sem(f"L{n}_inv_ready")
            s.normalised = sem(f"L{n}_normalised")
            s.tokT_in_psum = sem(f"L{n}_tokT_in_psum")
            s.tokT_ready = sem(f"L{n}_tokT_ready")
            s.projected = sem(f"L{n}_projected")
            s.added = sem(f"L{n}_added")
            s.stats_ready = sem(f"L{n}_stats_ready")
            s.vs_loaded = [sem(f"L{n}_vs_loaded{p}") for p in range(2)]

    A0 = Attn(0, 16, 16, NKV, 32)
    A1 = Attn(1, 8, 64, NKV + 1, 64, negated=True)

    ctxT_ps = psum[0:DCC, 0:2, 0:NKV]
    k_ps = psum[:, 2:4, 0:NKV]
    v_ps = psum[:, 4:6, :].rearrange("p a (t n) -> p (a t) n", t=2)
    xnT_ps = psum[:, 6, 0:2 * NQ].rearrange("p (c n) -> p c n", c=2)
    q_ps = psum[:, 7, 0:2 * NQ].rearrange("p (c n) -> p c n", c=2)
    xnT1_ps = psum[:, 7, 0:2 * NQ].rearrange("p (c n) -> p c n", c=2)
    k1_ps = psum[:, 2:5, :]
    v1_ps = [psum[:, k, :] for k in (5, 6, 5)]
    q1_ps = psum[:, 7, :]
    score_ps = [psum[:, 2 * k:2 * k + 2, :] for k in range(2)]
    pT_ps = psum[:, 4:6, :].rearrange("p a (t n) -> p (a t) n", t=2)[:, 0:3, 0:2 * NQ]
    o_ps = psum[:, 6, 0:4 * NQ].rearrange("p (g n) -> p g n", g=4)
    y_ps = psum[:, 7, :]

    rows = [P, P, TAIL]

    def sp_load0(sp):
        sp.dma_start(x[:, 1:B + 1, :], a["x"].rearrange("b q d -> q b d")).then_inc(x_loaded, 16)
        sp_ctx(sp, 0, 0)
        for dst, src in (
            (wk0[:, :, :], a["L0_xattn_Wk"].rearrange("(c p) n -> p c n", p=DCC)),
            (wv0[0:DCC, :, :], a["L0_xattn_Wv"].rearrange("(c p) n -> p c n", p=DCC)),
            (wv0[DCC:DCC + 1, 1, :], a["L0_xattn_bv"].rearrange("(o n) -> o n", o=1)),
            (bk0[:, :], a["L0_xattn_bk"].rearrange("(c p) -> p c", p=P)),
            (wq0[:, :, :], a["L0_xattn_Wq"].rearrange("(c p) n -> p c n", p=P)),
            (bq0[:, :], a["L0_xattn_bq"].rearrange("(c p) -> p c", p=P)),
        ):
            sp.dma_start(dst, src, allow_slow_non_contiguous=True).then_inc(w0_loaded, 16)
        sp_ctx(sp, 1, 1)
        for dst, src in (
            (wo0[:, :, :], a["L0_xattn_Wo"].rearrange("(c p) n -> p c n", p=P)),
            (bo0[:, :], a["L0_xattn_bo"].rearrange("(o n) -> o n", o=1)),
        ):
            sp.dma_start(dst, src).then_inc(wo0_loaded, 16)

    def sp_ctx(sp, b, p):
        src = a["ctx_768"][b]
        sp.dma_start(ctx_nat[p][:, 0:FULL, :], src[0:FULL * P, :].rearrange("(t p) d -> p t d", p=P)
                     ).then_inc(ctx_loaded[p], 16)
        sp.dma_start(ctx_nat[p][0:TAIL, FULL, :], src[FULL * P:NKV, :]).then_inc(ctx_loaded[p], 16)

    def sp_project0(sp):
        with sp.Fori(1, B // 2) as i:
            for p in range(2):
                sp.wait_ge(ctxT_in_psum, 2 * i + p - 1)
                sp_ctx(sp, 2 * i + p, p)
        sp.wait_ge(ctxT_in_psum, B - 1)
        sp.sem_inc(ctx_loaded[0], 32)

    def pool_consts(pool):
        nc.gpsimd.memset(ident[:, :], 0.0).then_inc(consts_ready, 1)
        nc.gpsimd.memset(headmask[:, :], 1.0).then_inc(consts_ready, 1)
        nc.gpsimd.memset(eps_col[:, :], EPS).then_inc(consts_ready, 1)
        nc.gpsimd.memset(ones_row[:, :], 1.0).then_inc(consts_ready, 1)
        pool.wait_ge(consts_ready, 4)
        for p in range(2):
            nc.gpsimd.memset(ctxT0[p][DCC:DCC + 1], 1.0).then_inc(consts_ready, 1)
            pool.wait_ge(consts_ready, 5 + p)
        nc.gpsimd.affine_select(out=ident[:, :], in_=ident[:, :], compare_op=ALU.not_equal, fill=1.0, base=0,
                                pattern=[[-1, P]], channel_multiplier=1).then_inc(consts_ready, 1)
        nc.gpsimd.affine_select(out=headmask[:, :], in_=headmask[:, :], compare_op=ALU.is_ge, fill=0.0, base=0,
                                pattern=[[-16, 8]], channel_multiplier=1).then_inc(consts_ready, 1)
        pool.wait_ge(consts_ready, 8)
        nc.gpsimd.affine_select(out=headmask[:, :], in_=headmask[:, :], compare_op=ALU.is_ge, fill=0.0, base=15,
                                pattern=[[16, 8]], channel_multiplier=-1).then_inc(consts_ready, 1)
        nc.gpsimd.memset(v_all[:, 0:B, :, :].rearrange("p b t (h e) -> p (b t h) e", e=32)[:, :, 16:32], 0.0
                         ).then_inc(consts_ready, 1)
        nc.gpsimd.memset(A0.kT[:, :, B * NKV:(B + 1) * NKV], 0.0).then_inc(consts_ready, 1)
        nc.gpsimd.memset(A0.qT[:, :, B * NQ:(B + 1) * NQ], 0.0).then_inc(consts_ready, 1)
        nc.gpsimd.memset(sums[:, :, :], 1.0).then_inc(consts_ready, 1)
        nc.gpsimd.memset(x[:, 0, :], 0.0).then_inc(consts_ready, 1)
    N_CONSTS = 14
    N_FIRST = 7

    dve_steps = [0]

    def mark(ins):
        dve_steps[0] += 1
        ins.then_inc(dve_step, 1)

    def marked(dve):
        dve.wait_ge(dve_step, dve_steps[0])

    def step(dve, ins):
        mark(ins)
        marked(dve)

    def dve_ln_finish(dve, n_std):
        for b in range(B):
            nc.vector.bn_aggr(mv[:, b, :], stats[:, b + 1, :]).then_inc(ln_stats, 1)
        dve.wait_ge(ln_std, n_std)
        step(dve, nc.vector.reciprocal(rstd[:, :], std[:, :]))

    def act_std(act, k):
        act.wait_ge(ln_stats, B * (k + 1))
        act.wait_ge(consts_ready, N_FIRST)
        nc.scalar.activation(std[:, :], mv[:, :, 1], ACT.Sqrt, bias=eps_col[0:NQ, :]).then_inc(ln_std, 1)

    def dve_project0(dve):
        dve.wait_ge(x_loaded, 16)
        for b in range(B):
            mark(nc.vector.bn_stats(stats[:, b + 1, :], x[:, b + 1, :]))
        marked(dve)
        dve_ln_finish(dve, 1)
        with dve.Fori(0, B) as b:
            nc.vector.tensor_scalar(xn[:, :], x[:, b + 1, :], mv[:, b, 0:1], rstd[:, bass.ds(b, 1)], ALU.subtract, ALU.mult
                                    ).then_inc(xn_ready, 1)
            dve.wait_ge(xnT_in_psum, b + 1)
            nc.vector.tensor_copy(xnT[:, :, :], xnT_ps).then_inc(xnT_ready, 1)
            dve.wait_ge(v_in_psum, b + 1)
            nc.vector.tensor_copy(
                v_all[:, b, 0:FULL, :].rearrange("p t (h e) -> p (t h) e", e=32)[:, :, 0:16],
                v_ps[:, 0:FULL, :].rearrange("p t (h e) -> p (t h) e", e=16)).then_inc(v_stored, 1)
            nc.vector.tensor_copy(
                v_all[0:TAIL, b, FULL, :].rearrange("p (h e) -> p h e", e=32)[:, :, 0:16],
                v_ps[0:TAIL, FULL, :].rearrange("p (h e) -> p h e", e=16)).then_inc(v_stored, 1)

    def pe_project0(pe):
        pe.wait_ge(consts_ready, N_FIRST)
        def transpose_ctx(p, loaded):
            pe.wait_ge(ctx_loaded[p], loaded)
            for c in range(2):
                for t in range(3):
                    last = nc.tensor.transpose(ctxT_ps[:, c, t * P:t * P + rows[t]],
                                               ctx_nat[p][0:rows[t], t, c * DCC:(c + 1) * DCC],
                                               ident[0:rows[t], 0:rows[t]])
            last.then_inc(ctxT_in_psum, 1)

        transpose_ctx(0, 32)
        pe.wait_ge(w0_loaded, 16 * N_W0)
        with pe.Fori(0, B // 2) as i:
            for p in range(2):
                b = 2 * i + p
                pe.wait_ge(ctxT_ready, b + 1)
                for m in range(2):
                    for c in range(2):
                        last = nc.tensor.matmul(k_ps[:, m, :], wk0[:, c, m * P:(m + 1) * P], ctxT0[p][0:DCC, c, :],
                                                start=(c == 0), stop=(c == 1))
                last.then_inc(k_in_psum, 1)
                pe.wait_ge(xn_ready, b + 1)
                for c in range(2):
                    last = nc.tensor.transpose(xnT_ps[:, c, :], xn[:, c * P:(c + 1) * P], ident[0:NQ, 0:NQ])
                last.then_inc(xnT_in_psum, 1)
                transpose_ctx(1 - p, 32 * (i + p) + 32)
                pe.wait_ge(xnT_ready, b + 1)
                for t in range(3):
                    for c in range(2):
                        last = nc.tensor.matmul(v_ps[0:rows[t], t, :], ctxT0[p][0:DCC + c, c, t * P:t * P + rows[t]],
                                                wv0[0:DCC + c, c, :], start=(c == 0), stop=(c == 1))
                last.then_inc(v_in_psum, 1)
                pe.wait_ge(k_stored, 2 * b + 2)
                for m in range(2):
                    for c in range(2):
                        last = nc.tensor.matmul(q_ps[:, m, :], wq0[:, c, m * P:(m + 1) * P], xnT[:, c, :],
                                                start=(c == 0), stop=(c == 1))
                last.then_inc(q_in_psum, 1)

    def act_project0(act):
        act_std(act, 0)
        act.wait_ge(w0_loaded, 16 * N_W0)
        nc.scalar.activation(bq0s[:, :], bq0[:, :], ACT.Copy, scale=SCALE0).then_inc(bq_scaled, 1)
        act.wait_ge(bq_scaled, 1)

        def take_ctx(n, p):
            act.wait_ge(ctxT_in_psum, n + 1)
            nc.scalar.activation(ctxT0[p][0:DCC], ctxT_ps, ACT.Copy).then_inc(ctxT_ready, 1)

        take_ctx(0, 0)
        with act.Fori(0, B // 2) as i:
            for p in range(2):
                b = 2 * i + p
                act.wait_ge(k_in_psum, b + 1)
                for m in range(2):
                    nc.scalar.activation(A0.kT[:, m, bass.ds(b * NKV, NKV)], k_ps[:, m, :], ACT.Identity,
                                         bias=bk0[:, m:m + 1]).then_inc(k_stored, 1)
                take_ctx(b + 1, 1 - p)
                act.wait_ge(q_in_psum, b + 1)
                for m in range(2):
                    nc.scalar.activation(A0.qT[:, m, bass.ds(b * NQ, NQ)], q_ps[:, m, :], ACT.Identity,
                                         bias=bq0s[:, m:m + 1], scale=SCALE0).then_inc(q_stored, 1)

    def sp_attend(sp, L, v_ready):
        v_ready(sp)

        def load(b, p):
            sp.dma_start(vs[p][:, 0:FULL, :], v_all[:, b, 0:FULL, :]).then_inc(L.vs_loaded[p], 16)
            sp.dma_start(vs[p][0:L.tail, FULL, :], v_all[0:L.tail, b, FULL, :]).then_inc(L.vs_loaded[p], 16)
        load(0, 0)
        load(1, 1)
        with sp.Fori(1, B // 2) as i:
            for p in range(2):
                sp.wait_ge(L.attended, 2 * i + p)
                load(2 * i + p, p)

    def pool_attend(pool, L, q_ready, mask):
        q_ready(pool)

        def spread(b, p):
            for c in range(L.chunks):
                nc.gpsimd.tensor_tensor(
                    qm[p][:, c * L.hpc:(c + 1) * L.hpc, :],
                    L.qT[:, c, bass.ds(b * NQ, NQ)].unsqueeze(1).broadcast_to([P, L.hpc, NQ]),
                    mask.unsqueeze(2).broadcast_to([P, L.hpc, NQ]), ALU.mult).then_inc(L.qm_ready, 1)
        for b in range(2):
            spread(b, b)
        with pool.Fori(1, B // 2) as i:
            for p in range(2):
                pool.wait_ge(L.scores_ready, L.ppb * (2 * i + p - 1))
                spread(2 * i + p, p)
        pool.wait_ge(L.scores_ready, L.ppb * (B - 1))
        spread(B, 0)

    def pe_attend(pe, L, ready):
        ready(pe)
        nrows = [P, P, L.tail]

        def scores(j, b, clipped):
            h = 2 * (j % L.ppb)
            p = (j // L.ppb) % 2
            if clipped is not None:
                pe.wait_ge(L.clipped, clipped)
            if j % L.ppb == 0:
                pe.wait_ge(L.qm_ready, L.chunks * (b + 1))
            for hh in range(2):
                last = nc.tensor.matmul(score_ps[j % 2][0:NQ, hh, 0:L.nk], qm[p][:, h + hh, :],
                                        L.kT[:, (h + hh) // L.hpc, bass.ds(b * L.nk, L.nk)], start=True, stop=True)
            last.then_inc(L.scores_ready, 1)

        def finish_transpose(b):
            pe.wait_ge(L.out_taken, b + 1)
            for g in range(4):
                last = nc.tensor.transpose(y_ps[0:NQ, g * P:(g + 1) * P], oT[:, g, :], ident[:, :])
            last.then_inc(L.tok_ready, 1)

        def finish_transpose_back(b):
            pe.wait_ge(L.normalised, b + 1)
            for c in range(L.chunks):
                last = nc.tensor.transpose(y_ps[:, c * NQ:(c + 1) * NQ], o_tok[:, c * P:(c + 1) * P],
                                           ident[0:NQ, 0:NQ])
            last.then_inc(L.tokT_in_psum, 1)

        def finish_project(b):
            pe.wait_ge(L.tokT_ready, b + 1)
            for c in range(L.chunks):
                last = nc.tensor.matmul(y_ps[0:NQ, 0:D], o_tokT[:, c, :], L.wo[:, c, :], start=(c == 0),
                                        stop=(c == L.chunks - 1 and L.bo is None))
            if L.bo is not None:
                last = nc.tensor.matmul(y_ps[0:NQ, 0:D], ones_row[0:1, 0:NQ], L.bo, start=False, stop=True)
            last.then_inc(L.projected, 1)
        finish = [finish_transpose, finish_transpose_back, finish_project]

        pe.sem_inc(L.transposed, NPB)
        pe.sem_inc(L.attended, 1)
        for j in range(LOOK):
            scores(j, 0, j - 1 if j >= 2 else None)
        with pe.Fori(0, B // 2) as i:
            for j in range(2 * L.ppb):
                n = 2 * L.ppb * i + j
                b = 2 * i + j // L.ppb
                p = (j // L.ppb) % 2
                s = j % L.ppb
                pe.wait_ge(L.exp_done, n + 1)
                for t in range(3):
                    for hh in range(2):
                        last = nc.tensor.transpose(pT_ps[0:nrows[t], t, hh * NQ:(hh + 1) * NQ],
                                                   probs[:, j % NPB, hh, t * P:t * P + nrows[t]], ident[0:NQ, 0:NQ])
                last.then_inc(L.transposed, 1)
                scores(j + LOOK, 2 * i + (j + LOOK) // L.ppb, n + LOOK - 1)
                if s < len(finish):
                    finish[s](b)
                pe.wait_ge(L.probsT_ready, n + 1)
                if s == 0:
                    pe.wait_ge(L.vs_loaded[p], 32 * i + 32)
                    pe.wait_ge(L.out_taken, b + 1)
                for hh in range(2):
                    h = 2 * s + hh
                    g, strip = (h * L.vcols) // P, (h * L.vcols) % P
                    for t in range(3):
                        last = nc.tensor.matmul(o_ps[strip:strip + L.vcols, g, :],
                                                vs[p][0:nrows[t], t, h * L.vcols:(h + 1) * L.vcols],
                                                probsT[j % 2][0:nrows[t], t, hh * NQ:(hh + 1) * NQ],
                                                start=(t == 0), stop=(t == 2))
                if s == L.ppb - 1:
                    last.then_inc(L.attended, 1)
        for step in finish:
            step(B)

    def act_attend(act, L):
        def exps(j, n, b):
            p = (j // L.ppb) % 2
            if j % L.ppb == 0:
                act.wait_ge(L.normalised, b)
            act.wait_ge(L.max_ready, n + 1)
            for hh in range(2):
                h = 2 * (j % L.ppb) + hh
                last = nc.scalar.activation(probs[:, j % NPB, hh, 0:L.nk], probs[:, j % NPB, hh, 0:L.nk], ACT.Exp,
                                            bias=negmax[:, j % NPB, hh:hh + 1], scale=L.exp_scale,
                                            accum_out=sums[:, p, h:h + 1])
            last.then_inc(L.exp_done, 1)

        def finish_take(b):
            act.wait_ge(L.attended, b + 1)
            nc.scalar.activation(oT[:, :, :], o_ps, ACT.Copy).then_inc(L.out_taken, 1)

        def finish_takeT(b):
            act.wait_ge(L.tokT_in_psum, b + 1)
            nc.scalar.activation(o_tokT[:, 0:L.chunks, :], y_ps[:, 0:L.chunks * NQ].rearrange(
                "p (c n) -> p c n", c=L.chunks), ACT.Copy).then_inc(L.tokT_ready, 1)
        finish = {0: finish_take, 2: finish_takeT}

        if L.mask_bias is not None:
            act.wait_ge(mask_null, 3)
            L.mask_bias(act, 0, 0)
        for j in range(AHEAD):
            exps(j, j, 0)
        with act.Fori(0, B // 2) as i:
            for j in range(2 * L.ppb):
                n = 2 * L.ppb * i + j
                b = 2 * i + j // L.ppb
                if j % L.ppb in finish:
                    finish[j % L.ppb](b)
                if j % L.ppb == 1 and L.mask_bias is not None:
                    L.mask_bias(act, b + 1, 1 - (j // L.ppb) % 2)
                act.wait_ge(L.transposed, n + 1 + NPB)
                nc.scalar.activation(probsT[j % 2][:, 0:FULL, :], pT_ps[:, 0:FULL, :], ACT.Copy)
                nc.scalar.activation(probsT[j % 2][0:L.tail, FULL, :], pT_ps[0:L.tail, FULL, :], ACT.Copy
                                     ).then_inc(L.probsT_ready, 1)
                exps(j + AHEAD, n + AHEAD, 2 * i + (j + AHEAD) // L.ppb)
        finish_take(B)
        L.std_before_last(act)
        finish_takeT(B)

    def dve_attend(dve, L):
        def normalise(b, p):
            dve.wait_ge(L.tok_ready, b + 1)
            nc.vector.reciprocal(inv_sums[:, 0:L.heads], sums[:, p, 0:L.heads]).then_inc(L.inv_ready, 1)
            dve.wait_ge(L.inv_ready, b + 1)
            nc.vector.tensor_tensor(
                o_tok[:, 0:L.heads * L.hd].rearrange("q (h e) -> q h e", e=L.hd),
                y_ps[0:NQ, :].rearrange("q (h e) -> q h e", e=L.vcols)[:, :, 0:L.hd],
                inv_sums[:, 0:L.heads].unsqueeze(2).broadcast_to([NQ, L.heads, L.hd]), ALU.mult
            ).then_inc(L.normalised, 1)

        L.prepare(dve)
        for j in range(AHEAD):
            L.masked_max(dve, j, j, 0)
        with dve.Fori(0, B // 2) as i:
            for j in range(2 * L.ppb):
                n = 2 * L.ppb * i + j
                b = 2 * i + j // L.ppb
                s = j % L.ppb
                if s == 1:
                    normalise(b, (j // L.ppb + 1) % 2)
                if s == 3:
                    L.take(dve, b)
                L.masked_max(dve, j + AHEAD, n + AHEAD, 2 * i + (j + AHEAD) // L.ppb)
        L.before_last(dve)
        normalise(B, 1)
        L.while_projecting(dve)
        L.take(dve, B)

    A0.wo, A0.bo = wo0, bo0[0:1, :]

    def a0_prepare(dve):
        dve.wait_ge(q_stored, 2 * B)
        nc.vector.memset(o_ps, 0.0).then_inc(A0.out_cleared, 1)
    A0.out_cleared = sem("L0_out_cleared")
    A0.prepare = a0_prepare

    def a0_masked_max(dve, j, n, b):
        k = j % NPB
        dve.wait_ge(A0.scores_ready, n + 1)
        dve.wait_ge(A0.transposed, n + 1)
        nc.vector.tensor_scalar(probs[:, k, :, 0:NKV], score_ps[j % 2][0:NQ, :, 0:NKV], -CLAMP, CLAMP, ALU.max, ALU.min
                                ).then_inc(A0.clipped, 1)
        dve.wait_ge(A0.clipped, n + 1)
        nc.vector.tensor_reduce(negmax[:, k, :], probs[:, k, :, 0:NKV], AX.X, ALU.max, negate=True
                                ).then_inc(A0.max_ready, 1)
    A0.masked_max = a0_masked_max

    def a0_take(dve, b):
        dve.wait_ge(A0.projected, b + 1)
        nc.vector.tensor_tensor(x[:, b, :], x[:, b, :], y_ps[0:NQ, 0:D], ALU.add).then_inc(A0.added, 1)
        dve.wait_ge(A0.added, b + 1)
        nc.vector.bn_stats(stats[:, b, :], x[:, b, :]).then_inc(A0.stats_ready, 1)
    A0.take = a0_take

    xnT_all_ps = [psum[:, k, 0:4 * NQ].rearrange("p (b c n) -> p b c n", b=2, c=2) for k in range(4)]
    logits_ps = psum[0:NQ, 4, 0:B * E0].rearrange("p (b e) -> p b e", b=B)
    ranks_ps = psum[0:NQ, 5, 0:B * E0].rearrange("p (b e) -> p b e", b=B)
    totals_ps = psum[:, 6, 0:B * E0].rearrange("p (b e) -> p b e", b=B)
    xsT_ps = psum[:, 0, 0:2 * P].rearrange("p (c n) -> p c n", c=2)
    b1_ps = psum[:, 1, 0:E0 * HC]
    hid_ps = [psum[:, 2 + k, :].rearrange("p (m n) -> p m n", m=4) for k in range(2)]
    ys_ps = psum[:, 6, 0:D]

    def pool_consts_moe(pool):
        nc.gpsimd.memset(earlier[:, :], 1.0).then_inc(consts_ready, 1)
        nc.gpsimd.memset(ones_sq[:, :], 1.0).then_inc(consts_ready, 1)
        nc.gpsimd.memset(below8[:, :, :], 1.0).then_inc(consts_ready, 1)
        nc.gpsimd.iota(iota16[:, :], [[1, 16]], base=0, channel_multiplier=0, allow_small_or_imprecise_dtypes=True
                       ).then_inc(consts_ready, 1)
        nc.gpsimd.memset(zeros[:, :], 0.0).then_inc(consts_ready, 1)
        pool.wait_ge(consts_ready, N_CONSTS + 5)
        nc.gpsimd.affine_select(out=earlier[:, :], in_=earlier[:, :], compare_op=ALU.is_gt, fill=0.0, base=0,
                                pattern=[[1, NQ]], channel_multiplier=-1).then_inc(consts_ready, 1)
        nc.gpsimd.affine_select(out=below8[:, :, :], in_=below8[:, :, :], compare_op=ALU.is_gt, fill=0.0, base=0,
                                pattern=[[1, 8], [-1, 8]], channel_multiplier=0).then_inc(consts_ready, 1)
    N_MOE_CONSTS = 7

    def sp_load_moe(sp):
        sp.dma_start(wg0[:, :, :], a["L0_ffn_Wg"].rearrange("(c p) e -> p c e", p=P)).then_inc(gate_loaded, 16)
        sp.dma_start(bg0[:, :], a["L0_ffn_bg"].rearrange("(o e) -> o e", o=1).broadcast_to([NQ, E0])
                     ).then_inc(gate_loaded, 16)
        sp.wait_ge(consts_ready, N_CONSTS + N_MOE_CONSTS)
        sp.dma_start(xs_dram.rearrange("(i p) d -> p i d", p=P), zeros[:, :].unsqueeze(1).broadcast_to([P, NBLK + 2, D])
                     ).then_inc(xs_cleared, 16)
        sp.dma_start(ys_dram.rearrange("(i p) d -> p i d", p=P), zeros[:, :].unsqueeze(1).broadcast_to([P, NBLK, D])
                     ).then_inc(xs_cleared, 16)

    def normalise0(b):
        nc.vector.tensor_scalar(xn_all[:, b, :], x[:, b + 1, :], mv[:, b, 0:1], rstd[:, b:b + 1], ALU.subtract,
                                ALU.mult).then_inc(xn_ready, 1)

    def dve_before_last0(dve):
        dve.wait_ge(A0.stats_ready, B)
        for b in range(B - 1):
            nc.vector.bn_aggr(mv[:, b, :], stats[:, b + 1, :]).then_inc(ln_stats, 1)
    A0.before_last = dve_before_last0

    def act_std_before_last0(act):
        act.wait_ge(ln_stats, 2 * B - 1)
        nc.scalar.activation(std[:, 0:B - 1], mv[:, 0:B - 1, 1], ACT.Sqrt, bias=eps_col[0:NQ, :]).then_inc(ln_std, 1)
    A0.std_before_last = act_std_before_last0

    def dve_while_projecting0(dve):
        dve.wait_ge(ln_std, 2)
        step(dve, nc.vector.reciprocal(rstd[:, 0:B - 1], std[:, 0:B - 1]))
        dve.wait_ge(A0.attended, B + 1)
        for b in range(B - 1):
            normalise0(b)
    A0.while_projecting = dve_while_projecting0

    def dve_gate(dve):
        dve.wait_ge(A0.stats_ready, B + 1)
        nc.vector.bn_aggr(mv[:, B - 1, :], stats[:, B, :]).then_inc(ln_stats, 1)
        dve.wait_ge(ln_std, 3)
        step(dve, nc.vector.reciprocal(rstd[:, B - 1:B], std[:, B - 1:B]))
        normalise0(B - 1)
        dve.wait_ge(consts_ready, N_CONSTS + N_MOE_CONSTS)
        back = route_a[0:NQ, 64:64 + E0]
        mark(nc.vector.tensor_scalar(back, iota16[0:NQ, 0:E0], -1.0, float(E0), ALU.mult, ALU.add))
        mark(nc.vector.tensor_scalar(block_starts[:, :], iota16[:, 0:MAXB], float(P), None, ALU.mult))
        dve.wait_ge(gate_loaded, 32)
        dve.wait_ge(gate_logits, B)
        step(dve, nc.vector.tensor_tensor(logits[:, :, :], logits_ps, bg0[:, :].unsqueeze(1).broadcast_to([NQ, B, E0]),
                                          ALU.add))
        step(dve, nc.vector.tensor_reduce(top_logit[:, :], logits[:, :, :], AX.X, ALU.max))
        top = top_logit[:, :].unsqueeze(2).broadcast_to([NQ, B, E0])
        grid = route_a[0:NQ, 0:B * E0].rearrange("q (b e) -> q b e", b=B)
        step(dve, nc.vector.tensor_tensor(choice[:, :, :], logits[:, :, :], top, ALU.is_equal))
        each = back.unsqueeze(1).broadcast_to([NQ, B, E0])
        step(dve, nc.vector.tensor_tensor(grid, choice[:, :, :], each, ALU.mult))
        step(dve, nc.vector.tensor_reduce(slot_f[:, :], grid, AX.X, ALU.max))
        nc.vector.tensor_tensor(choice[:, :, :], each, slot_f[:, :].unsqueeze(2).broadcast_to([NQ, B, E0]),
                                ALU.is_equal).then_inc(choice_ready, 1)
        nc.vector.tensor_tensor(logits[:, :, :], logits[:, :, :], top, ALU.subtract).then_inc(g_centred, 1)
        dve.wait_ge(g_exp, 1)
        step(dve, nc.vector.tensor_reduce(top_weight[:, :], logits[:, :, :], AX.X, ALU.add))
        step(dve, nc.vector.reciprocal(top_weight[:, :], top_weight[:, :]))
        dve.wait_ge(ranks_ready, 1)
        step(dve, nc.vector.tensor_copy(counts[:, :, :], totals_ps))
        tokens, blocks, first, end = (per_expert[:, k, :] for k in range(4))
        step(dve, nc.vector.tensor_reduce(tokens, counts[:, :, :].rearrange("p b e -> p e b"), AX.X, ALU.add))
        over = route_a[:, 0:E0 * MAXB].rearrange("p (e j) -> p e j", e=E0)
        step(dve, nc.vector.tensor_tensor(over, tokens.unsqueeze(2).broadcast_to([P, E0, MAXB]),
                                     block_starts[:, :].unsqueeze(1).broadcast_to([P, E0, MAXB]), ALU.is_gt))
        step(dve, nc.vector.tensor_reduce(blocks, over, AX.X, ALU.add))
        step(dve, nc.vector.tensor_scalar(blocks, blocks, 1.0, None, ALU.max))
        pairs = route_a[:, 0:64].rearrange("p (i j) -> p i j", i=8)
        step(dve, nc.vector.tensor_tensor(pairs, below8[:, :, :], blocks.unsqueeze(1).broadcast_to([P, E0, E0]), ALU.mult))
        step(dve, nc.vector.tensor_reduce(first, pairs, AX.X, ALU.add))
        step(dve, nc.vector.tensor_tensor(end, first, blocks, ALU.add))
        nc.vector.tensor_copy(per_expert_i[:, :, :], per_expert[:, 1:4, :]).then_inc(slots_ready, 1)
        before = route_a[:, :].rearrange("p (b e k) -> p b e k", b=B, e=E0)
        step(dve, nc.vector.tensor_tensor(
            before, counts[:, :, :].rearrange("p k e -> p e k").unsqueeze(1).broadcast_to([P, B, E0, B]),
            below8[:, :, :].unsqueeze(2).broadcast_to([P, B, E0, B]), ALU.mult))
        step(dve, nc.vector.tensor_reduce(route_b[:, :, :], before, AX.X, ALU.add))
        step(dve, nc.vector.scalar_tensor_tensor(route_b[:, :, :], first.unsqueeze(1).broadcast_to([P, B, E0]), float(P),
                                            route_b[:, :, :], ALU.mult, ALU.add))
        step(dve, nc.vector.tensor_tensor(route_b[0:NQ], ranks_ps, route_b[0:NQ], ALU.add))
        step(dve, nc.vector.tensor_tensor(route_b[0:NQ], route_b[0:NQ], choice[:, :, :], ALU.mult))
        step(dve, nc.vector.tensor_reduce(slot_f[:, :], route_b[0:NQ], AX.X, ALU.add))
        nc.vector.tensor_copy(slot[:, :], slot_f[:, :]).then_inc(slots_ready, 1)

    def act_gate(act):
        act.wait_ge(ln_stats, 2 * B)
        nc.scalar.activation(std[:, B - 1:B], mv[:, B - 1:B, 1], ACT.Sqrt, bias=eps_col[0:NQ, :]).then_inc(ln_std, 1)
        for k in range(B // 2):
            act.wait_ge(xnT_in_psum, B + 2 * k + 2)
            nc.scalar.activation(xnT0[:, :, 2 * k * NQ:2 * (k + 1) * NQ].rearrange("p c (b n) -> p b c n", b=2),
                                 xnT_all_ps[k], ACT.Copy).then_inc(xnT_ready, 2)
        act.wait_ge(g_centred, 1)
        nc.scalar.activation(logits[:, :, :], logits[:, :, :], ACT.Exp).then_inc(g_exp, 1)

    def pe_gate(pe):
        pe.wait_ge(gate_loaded, 32)
        pe.wait_ge(A0.added, B + 1)
        for b in range(B):
            pe.wait_ge(xn_ready, B + b + 1)
            for c in range(2):
                last = nc.tensor.transpose(xnT_all_ps[b // 2][:, b % 2, c, :], xn_all[:, b, c * P:(c + 1) * P],
                                           ident[0:NQ, 0:NQ])
            last.then_inc(xnT_in_psum, 1)
        for b in range(B):
            pe.wait_ge(xnT_ready, B + 2 * (b // 2) + 2)
            for c in range(2):
                last = nc.tensor.matmul(logits_ps[:, b, :], xnT0[:, c, b * NQ:(b + 1) * NQ], wg0[:, c, :],
                                        start=(c == 0), stop=(c == 1))
            last.then_inc(gate_logits, 1)
        pe.wait_ge(choice_ready, 1)
        nc.tensor.matmul(ranks_ps, earlier[:, :], choice[:, :, :], start=True, stop=True)
        nc.tensor.matmul(totals_ps, ones_sq[:, :], choice[:, :, :], start=True, stop=True).then_inc(ranks_ready, 1)

    def pool_dispatch(pool):
        pool.wait_ge(slots_ready, 2)
        pool.wait_ge(xn_ready, 2 * B)
        pool.wait_ge(xs_cleared, 32)
        for b in range(B):
            nc.gpsimd.indirect_dma_start(
                out=xs_dram, out_offset=bass.IndirectOffsetOnAxis(ap=slot[:, b:b + 1], axis=0),
                in_=xn_all[:, b, :], in_offset=None).then_inc(xs_scattered, 16)

    def split_ctx1(pool, n, p):
        pool.wait_ge(ctxT_ready, n)
        nc.gpsimd.tensor_tensor(ctxT_low[p][:, :, :], ctxT_full[:, :, :], ctxT_high[p][:, :, :].bitcast(F32), ALU.subtract
                                ).then_inc(ctxT_split, 1)

    def pool_project1(pool):
        pool.wait_ge(ys_stored, 16 * all_blocks(pool) + 16)
        nc.gpsimd.tensor_tensor(pool_turn[:, :], ones_row[0:1, 0:1], ones_row[0:1, 0:1], ALU.mult)

        def gather(b):
            nc.gpsimd.indirect_dma_start(
                out=y_tok[:, b % 2, :], out_offset=None, in_=ys_dram,
                in_offset=bass.IndirectOffsetOnAxis(ap=slot[:, b:b + 1], axis=0)).then_inc(y_gathered[b % 2], 16)
        gather(0)
        gather(1)
        for b in range(B):
            split_ctx1(pool, CTX0 + b + 2, (b + 1) % 2)
            if b + 2 < B:
                pool.wait_ge(x2_added, b + 1)
                gather(b + 2)

    def all_blocks(e):
        return e.value_load(per_expert_i[0:1, 2, E0 - 1:E0], min_val=E0, max_val=NBLK)

    def each_block(e, run):
        def within(n):
            return nc.s_assert_within(n, 0, NBLK - 1, skip_runtime_bounds_check_because=
                                      "all experts take NBLK blocks at most")

        e.wait_ge(slots_ready, 1)
        with e.Fori(0, E0 // 2) as i:
            for p in range(2):
                blocks = e.value_load(per_expert_i[0:1, 0, bass.ds(2 * i + p, 1)], min_val=1, max_val=MAXB)
                first = e.value_load(per_expert_i[0:1, 1, bass.ds(2 * i + p, 1)], min_val=0, max_val=NBLK - 1)
                run(first, i, p, True)
                with e.If(blocks > 1):
                    run(within(first + 1), i, p, False)
                    with e.If(blocks > 2):
                        with e.Fori(2, MAXB) as k:
                            with e.If(blocks > k):
                                run(within(first + k), i, p, False)

    def sp_experts(sp):
        sp.dma_start(b1_rows[:, :], a["L0_ffn_b1"].rearrange("e (m q) -> (e m) q", q=P)).then_inc(biases_loaded, 16)
        sp.dma_start(b2_row[:, :], a["L0_ffn_b2"].rearrange("(o e) d -> o (e d)", o=1)).then_inc(biases_loaded, 16)
        def load(e, p):
            sp.dma_start(w1_e[p], a["L0_ffn_W1"].rearrange("e (c q) h -> q (e c) h", q=P)[:, bass.ds(2 * e, 2), :]
                         ).then_inc(w1_loaded[p], 16)
            sp.dma_start(w2_e[p], a["L0_ffn_W2"].rearrange("e (m q) d -> q (e m) d", q=P)[:, bass.ds(HC * e, HC), :]
                         ).then_inc(w2_loaded[p], 16)

        def block(n, i, p, first):
            if first:
                with sp.If(i > 0 if p == 0 else i < E0 // 2 - 1):
                    sp.wait_ge(expert_begun, 2 * i + p + 1)
                    load(nc.s_assert_within(2 * i + p + 1, 1, E0 - 1, skip_runtime_bounds_check_because=
                                            "after the last expert there is none to load"), 1 - p)
            sp.wait_ge(ys_ready, n + 2)
            sp.dma_start(ys_dram[bass.ds(n * P, P), :], ys_rows).then_inc(ys_stored, 16)

        load(0, 0)
        load(1, 1)
        each_block(sp, block)

    def transpose_ctx1(pe, p, loaded):
        pe.wait_ge(ctx_loaded[p], 32 * (B // 2 + 1 - p) + loaded)
        for c in range(2):
            for t in range(3):
                last = nc.tensor.transpose(ctxT_ps[:, c, t * P:t * P + rows[t]],
                                           ctx_nat[p][0:rows[t], t, c * DCC:(c + 1) * DCC],
                                           ident[0:rows[t], 0:rows[t]])
        last.then_inc(ctxT_in_psum, 1)

    def pe_experts(pe):
        def take_rows(n):
            pe.wait_ge(xs_loaded, 16 * n + 16)
            for c in range(2):
                last = nc.tensor.transpose(xsT_ps[:, c, :], xs_rows[:, c * P:(c + 1) * P], ident[:, :])
            last.then_inc(rows_used, 1)

        def block(n, i, p, first):
            pe.wait_ge(xsT_ready, n + 1)
            if first:
                pe.wait_ge(w1_loaded[p], 16 * i + 16)
            for m in range(HC):
                for c in range(2):
                    last = nc.tensor.matmul(hid_ps[m // 4][:, m % 4, :], w1_e[p][:, c, m * P:(m + 1) * P],
                                            xsT[:, c, :], start=(c == 0), stop=(c == 1))
                if first and m == 0:
                    last.then_inc(expert_begun, 1)
                if m % 4 == 3:
                    last.then_inc(hidden_in_psum, 1)
            take_rows(n + 1)
            if first:
                pe.wait_ge(w2_loaded[p], 16 * i + 16)
            pe.wait_ge(ys_ready, n + 1)
            for m in range(HC):
                if m % 4 == 0:
                    pe.wait_ge(hidden_ready, 2 * n + 1 + m // 4)
                nc.tensor.matmul(ys_ps, hT[:, m, :], w2_e[p][:, m, :], start=(m == 0), stop=False)
            last = nc.tensor.matmul(ys_ps, ones_row[0:1, :], b2_row[0:1, bass.ds((2 * i + p) * D, D)], start=False,
                                    stop=True)
            last.then_inc(ys_in_psum, 1)

        pe.wait_ge(slots_ready, 2)
        transpose_ctx1(pe, 0, 32)
        pe.wait_ge(ctxT_split, 1)
        pe.sem_inc(ys_ready, 1)
        pe.wait_ge(biases_loaded, 32)
        nc.tensor.transpose(b1_ps, b1_rows[:, :], ident[0:E0 * HC, 0:E0 * HC]).then_inc(b1_in_psum, 1)
        take_rows(0)
        each_block(pe, block)

    def take_ctx1(act, n, p, first=False):
        act.wait_ge(ctxT_in_psum, n)
        if not first:
            act.wait_ge(ctxT_split, n - 1 - CTX0)
        nc.scalar.activation(ctxT_full[:, :, :], ctxT_ps, ACT.Copy)
        nc.scalar.activation(ctxT_high[p][:, :, :], ctxT_ps, ACT.Copy).then_inc(ctxT_ready, 1)

    def act_experts(act):
        def load_rows(n):
            act.dma_start(xs_rows, xs_dram[bass.ds(n * P, P), :]).then_inc(xs_loaded, 16)

        def block(n, i, p, first):
            if first:
                act.wait_ge(b1_ready, 2 * i + p + 2)
            for half in range(2):
                act.wait_ge(hidden_in_psum, 2 * n + half + 1)
                for m in range(4 * half, 4 * half + 4):
                    last = nc.scalar.activation(hT[:, m, :], hid_ps[half][:, m % 4, :], ACT.Silu,
                                                bias=b1_col[p][:, m:m + 1])
                last.then_inc(hidden_ready, 1)
            act.wait_ge(rows_used, n + 2)
            load_rows(n + 2)

        take_ctx1(act, CTX0 + 1, 0, True)
        act.wait_ge(xs_scattered, 16 * B)
        load_rows(0)
        act.wait_ge(rows_used, 1)
        load_rows(1)
        each_block(act, block)

    def dve_experts(dve):
        def take_rows(n):
            dve.wait_ge(rows_used, n + 1)
            nc.vector.tensor_copy(xsT, xsT_ps).then_inc(xsT_ready, 1)

        def block(n, i, p, first):
            take_rows(n + 1)
            if first:
                nc.vector.tensor_copy(b1_col[1 - p], b1_all[:, bass.ds(2 * i + p + 1, 1), :]).then_inc(b1_ready, 1)
            dve.wait_ge(ys_in_psum, n + 1)
            dve.wait_ge(ys_stored, 16 * n + 16)
            nc.vector.tensor_copy(ys_rows, ys_ps).then_inc(ys_ready, 1)

        dve.wait_ge(b1_in_psum, 1)
        nc.vector.tensor_copy(b1_all[:, 0:E0, :], b1_ps.rearrange("p (e m) -> p e m", e=E0))
        nc.vector.memset(b1_all[:, E0, :], 0.0).then_inc(b1_ready, 1)
        dve.wait_ge(b1_ready, 1)
        nc.vector.tensor_copy(b1_col[0], b1_all[:, 0, :]).then_inc(b1_ready, 1)
        dve.sem_inc(ys_stored, 16)
        take_rows(0)
        each_block(dve, block)
        nc.vector.memset(turn[:, 0:1], 0.0).then_inc(experts_taken, 1)

    A1.wo, A1.bo = wo1, None

    def sp_load1(sp):
        for dst, src in (
            (wo1[:, :, :], a["L1_xattn_Wo"].rearrange("(c p) n -> p c n", p=P)),
            (g_norm[:, :], a["L1_xattn_g_norm"].rearrange("(o d) -> o d", o=1).broadcast_to([NQ, D])),
            (g_out[:, :], a["L1_xattn_g_out"].rearrange("(o d) -> o d", o=1).broadcast_to([NQ, D])),
            (mask_u8[:, 0:B, :], a["mask_BxS2_bf1"].rearrange("(o b) n -> o b n", o=1).broadcast_to([NQ, B, NKV])),
            (mask_u8[:, B, :], a["mask_BxS2_bf1"][0:1, :].broadcast_to([NQ, NKV])),
            (null_row[:, :], a["L1_xattn_null_kv"][0:1, :].broadcast_to([P, HD1])),
        ):
            sp.dma_start(dst, src).then_inc(const1_loaded, 16)
        for half in range(2):
            rows64 = slice(half * HD1, (half + 1) * HD1)
            for col, src in (
                (null_col, a["L1_xattn_null_kv"][0, :]),
                (q_scale_col, a["L1_xattn_q_scale"]),
                (k_scale_col, a["L1_xattn_k_scale"]),
            ):
                sp.dma_start(col[rows64, :], src.rearrange("(d o) -> d o", o=1), allow_slow_non_contiguous=True
                             ).then_inc(const1_loaded, 16)

    N_CONST1 = 12

    def sp_load1_weights(sp):
        sp.wait_ge(A0.added, B + 1)
        for p in range(2):
            sp_ctx(sp, p, p)
        wkv = a["L1_xattn_Wkv"].rearrange("(c p) n -> p c n", p=DCC)
        sp.dma_start(wk1, wkv[:, :, 0:512]).then_inc(w1x_loaded, 16)
        sp.dma_start(wv1, wkv[:, :, 512:1024]).then_inc(w1x_loaded, 16)
        sp.dma_start(wq1, a["L1_xattn_Wq"].rearrange("(c p) n -> p c n", p=P)).then_inc(w1x_loaded, 16)

    def sp_project1(sp):
        def load(b, p):
            src = a["ctx_768"][b]
            sp.dma_start(ctx_nat[p][:, 0:FULL, :], src[0:FULL * P, :].rearrange("(t p) d -> p t d", p=P)
                         ).then_inc(ctx_loaded[p], 16)
            sp.dma_start(ctx_nat[p][0:TAIL, FULL, :], src[FULL * P:NKV, :]).then_inc(ctx_loaded[p], 16)
        sp.wait_ge(ys_stored, 16 * all_blocks(sp) + 16)
        for h in range(8):
            sp.dma_start(v_all[TAIL:TAIL + 1, :, FULL, h * HD1:(h + 1) * HD1],
                         a["L1_xattn_null_kv"][1:2, :].unsqueeze(1).broadcast_to([1, B, HD1])).then_inc(null_v_stored, 16)
        with sp.Fori(1, B // 2) as i:
            for p in range(2):
                sp.wait_ge(ctxT_in_psum, CTX0 + 2 * i + p - 1)
                sp_ctx(sp, 2 * i + p, p)
        sp.wait_ge(ctxT_in_psum, CTX0 + B - 1)
        sp_ctx(sp, 0, 0)

    def pool_consts1(pool):
        nc.gpsimd.memset(halfmask[:, :], -SCALE1).then_inc(consts_ready, 1)
        nc.gpsimd.memset(key_ss[:, :, :], 1.0).then_inc(consts_ready, 1)
        pool.wait_ge(consts_ready, N_CONSTS + N_MOE_CONSTS + 2)
        nc.gpsimd.affine_select(out=halfmask[:, :], in_=halfmask[:, :], compare_op=ALU.is_ge, fill=0.0, base=0,
                                pattern=[[-HD1, 2]], channel_multiplier=1).then_inc(consts_ready, 1)
        pool.wait_ge(consts_ready, N_CONSTS + N_MOE_CONSTS + 3)
        nc.gpsimd.affine_select(out=halfmask[:, :], in_=halfmask[:, :], compare_op=ALU.is_ge, fill=0.0, base=HD1 - 1,
                                pattern=[[HD1, 2]], channel_multiplier=-1).then_inc(consts_ready, 1)
        pool.wait_ge(consts_ready, N_CONSTS + N_MOE_CONSTS + 4)
        pool.wait_ge(const1_loaded, 16 * N_CONST1)
        nc.gpsimd.memset(flt_max[:, :], FLT_MAX).then_inc(mask_null, 1)
        nc.gpsimd.tensor_scalar(halfmask[:, :], halfmask[:, :], q_scale_col[:, 0:1], k_scale_col[:, 0:1], ALU.mult,
                                ALU.mult).then_inc(consts_ready, 1)

    def pool_clear1(pool):
        nc.gpsimd.memset(A1.kT[:, :, B * A1.nk:(B + 1) * A1.nk], 0.0).then_inc(kq1_cleared, 1)
        nc.gpsimd.memset(A1.qT[:, :, B * NQ:(B + 1) * NQ], 0.0).then_inc(kq1_cleared, 1)

    def pool_mask_clear(pool):
        pool.wait_ge(ctxT_in_psum, CTX0 + B + 1)
        for p in range(2):
            nc.gpsimd.memset(mask_bias[p][:, NKV:NKV + 1], 0.0).then_inc(mask_null, 1)

    def act_mask_bias(act, b, p):
        nc.scalar.activation(mask_bias[p][:, 0:NKV], mask_u8[:, b, :], ACT.Identity, bias=flt_max[:, 0:1],
                             scale=-FLT_MAX).then_inc(mask_ready, 1)
    A1.mask_bias = act_mask_bias

    def act_split_weights1(act):
        act.wait_ge(w1x_loaded, 48)
        nc.scalar.activation(wk1_high, wk1, ACT.Copy).then_inc(w1x_high, 1)
        nc.scalar.activation(wv1_high, wv1, ACT.Copy).then_inc(w1x_high, 1)

    def pool_split_weights1(pool):
        for k, (w, high, low) in enumerate(((wk1, wk1_high, wk1_low), (wv1, wv1_high, wv1_low))):
            pool.wait_ge(w1x_high, k + 1)
            nc.gpsimd.tensor_tensor(low, w, high.bitcast(F32), ALU.subtract).then_inc(w1x_split, 1)

    def dve_project1(dve):
        total = all_blocks(dve)
        dve.wait_ge(ys_stored, 16 * total + 16)
        dve.wait_ge(xs_loaded, 16 * total + 32)
        dve.wait_ge(null_norm, 2)
        mark(nc.vector.tensor_scalar(null_ss[:, :], null_ss[:, :], 1e-12, None, ALU.max))
        marked(dve)
        mark(nc.vector.reciprocal(null_ss[:, :], null_ss[:, :]))
        marked(dve)
        mark(nc.vector.tensor_tensor(null_col[:, :], null_col[:, :], null_ss[:, :], ALU.mult))
        marked(dve)
        nc.vector.tensor_copy(
            A1.kT[:, :, 0:B * A1.nk].rearrange("p c (b n) -> p c b n", n=A1.nk)[:, :, :, NKV],
            null_col[:, :].unsqueeze(2).broadcast_to([P, 4, B])).then_inc(null_k_stored, 1)
        dve.wait_ge(const1_loaded, 16 * N_CONST1)

        def invert(ss, norm, b, ready):
            dve.wait_ge(norm, b + 1)
            nc.vector.tensor_scalar(ss, ss, 1e-12, None, ALU.max).then_inc(ready, 1)
            dve.wait_ge(ready, 2 * b + 1)
            nc.vector.reciprocal(ss, ss).then_inc(ready, 1)
            dve.wait_ge(ready, 2 * b + 2)

        heads = lambda v: v.rearrange("p (h e) -> p h e", e=HD1)
        with dve.Fori(0, B // 2) as i:
            for p in range(2):
                b = 2 * i + p
                count = [0]

                def chain(ins, wait=True):
                    count[0] += 1
                    ins.then_inc(x2_step, 1)
                    if wait:
                        dve.wait_ge(x2_step, X2_STEPS * b + count[0])

                def spread():
                    chain(nc.vector.memset(turn[:, 0:1], 0.0), wait=False)
                    nc.vector.bn_aggr(mv[:, 0, :], stats[:, 0, :]).then_inc(ln_stats, 1)

                dve.wait_ge(y_gathered[p], 16 * i + 16)
                chain(nc.vector.scalar_tensor_tensor(y_row, y_tok[:, p, :], top_weight[:, bass.ds(b, 1)], x[:, b + 1, :],
                                                     ALU.mult, ALU.add))
                chain(nc.vector.bn_stats(stats[:, 0, :], y_row), wait=False)
                nc.vector.tensor_copy(x[:, b + 1, :], y_row).then_inc(x2_added, 1)
                dve.wait_ge(x2_step, X2_STEPS * b + count[0])
                spread()
                dve.wait_ge(ln_std, 3 + 2 * b + 1)
                chain(nc.vector.reciprocal(rstd[:, 0:1], std[:, 0:1]))
                chain(nc.vector.tensor_scalar(y_row, y_row, mv[:, 0, 0:1], rstd[:, 0:1], ALU.subtract, ALU.mult))
                chain(nc.vector.tensor_reduce(row_max[:, 0:1], y_row, AX.X, ALU.max))
                chain(nc.vector.reciprocal(row_max[:, 0:1], row_max[:, 0:1]))
                chain(nc.vector.tensor_scalar(y_row, y_row, row_max[:, 0:1], None, ALU.mult))
                chain(nc.vector.bn_stats(stats[:, 0, :], y_row))
                spread()
                dve.wait_ge(ln_std, 3 + 2 * b + 2)
                chain(nc.vector.reciprocal(rstd[:, 0:1], std[:, 0:1]))
                chain(nc.vector.tensor_scalar(y_row, y_row, mv[:, 0, 0:1], rstd[:, 0:1], ALU.subtract, ALU.mult))
                dve.wait_ge(xnT_in_psum, 2 * B + b)
                nc.vector.tensor_tensor(xn[:, :], y_row, g_norm[:, :], ALU.mult).then_inc(xn_ready, 1)
                dve.wait_ge(xnT_in_psum, 2 * B + b + 1)
                nc.vector.tensor_copy(xnT[:, :, :], xnT1_ps).then_inc(xnT_ready, 1)
                dve.wait_ge(k1_squared, 2 * b + 1)
                nc.vector.tensor_reduce(key_ss[:, 0:FULL, :], k_tok_full.rearrange("p t (h e) -> p t h e", e=HD1),
                                        AX.X, ALU.add).then_inc(k1_ss, 1)
                dve.wait_ge(k1_squared, 2 * b + 2)
                nc.vector.tensor_reduce(key_ss[0:TAIL, FULL, :], heads(k_tok[FULL][0:TAIL, :]), AX.X, ALU.add
                                        ).then_inc(k1_ss, 1)
                invert(key_ss[:, :, :], k1_norm, b, k1_inv)
                each = key_ss[:, :, :].unsqueeze(3).broadcast_to([P, 3, 8, HD1])
                for t in range(3):
                    nc.vector.tensor_tensor(heads(k_tok[t][0:rows[t], :]), heads(k1_ps[0:rows[t], t, :]),
                                            each[0:rows[t], t], ALU.mult).then_inc(k1_scaled, 1)
                dve.wait_ge(q1_squared, b + 1)
                nc.vector.tensor_reduce(q_ss[:, :], heads(o_tok[:, :]), AX.X, ALU.add).then_inc(q1_ss, 1)
                invert(q_ss[:, :], q1_norm, b, q1_inv)
                nc.vector.tensor_tensor(heads(o_tok[:, :]), heads(q1_ps[0:NQ, :]),
                                        q_ss[:, :].unsqueeze(2).broadcast_to([NQ, 8, HD1]), ALU.mult
                                        ).then_inc(q1_scaled, 1)
    X2_STEPS = 12

    def pe_project1(pe):
        def times(p, ps, t, high, low):
            for c in range(2):
                cols = slice(t * P, t * P + rows[t])
                nc.tensor.matmul(ps, ctxT_high[p][:, c, cols], high[:, c, :], start=(c == 0), stop=False)
                nc.tensor.matmul(ps, ctxT_high[p][:, c, cols], low[:, c, :], start=False, stop=False)
                last = nc.tensor.matmul(ps, ctxT_low[p][:, c, cols], high[:, c, :], start=False, stop=(c == 1))
            return last

        pe.wait_ge(w1x_split, 2)
        with pe.Fori(0, B // 2) as i:
            for p in range(2):
                b = 2 * i + p
                pe.wait_ge(ctxT_split, b + 1)
                for t in range(3):
                    pe.wait_ge(kT1_stored, 3 * b + t + 1)
                    last = times(p, k1_ps[0:rows[t], t, :], t, wk1_high, wk1_low)
                last.then_inc(k1_in_psum, 1)
                def values(t):
                    times(p, v1_ps[t][0:rows[t], :], t, wv1_high, wv1_low).then_inc(v1_in_psum, 1)
                pe.wait_ge(experts_taken, 1)
                transpose_ctx1(pe, 1 - p, 32 * i + 32 * (p + 1))
                values(0)
                pe.wait_ge(xn_ready, 2 * B + b + 1)
                pe.wait_ge(qT1_stored, b + 1)
                for c in range(2):
                    last = nc.tensor.transpose(xnT1_ps[:, c, :], xn[:, c * P:(c + 1) * P], ident[0:NQ, 0:NQ])
                last.then_inc(xnT_in_psum, 1)
                pe.wait_ge(xnT_ready, 2 * B + b + 1)
                for c in range(2):
                    last = nc.tensor.matmul(q1_ps[0:NQ, :], xnT[:, c, :], wq1[:, c, :], start=(c == 0), stop=(c == 1))
                last.then_inc(q1_in_psum, 1)
                values(1)
                pe.wait_ge(v1_stored, 3 * b + 1)
                values(2)
                for t in range(3):
                    pe.wait_ge(k1_scaled, 3 * b + t + 1)
                    for c in range(4):
                        last = nc.tensor.transpose(k1_ps[:, t, c * P:c * P + rows[t]],
                                                   k_tok[t][0:rows[t], c * P:(c + 1) * P], ident[0:rows[t], 0:rows[t]])
                    last.then_inc(kT1_in_psum, 1)
                pe.wait_ge(q1_scaled, b + 1)
                for c in range(4):
                    last = nc.tensor.transpose(q1_ps[:, c * NQ:(c + 1) * NQ], o_tok[:, c * P:(c + 1) * P],
                                               ident[0:NQ, 0:NQ])
                last.then_inc(qT1_in_psum, 1)

    def act_project1(act):
        def keep_v(b, t):
            act.wait_ge(v1_in_psum, 3 * b + t + 1)
            nc.scalar.activation(v_all[0:rows[t], b, t, :], v1_ps[t][0:rows[t], :], ACT.Copy).then_inc(v1_stored, 1)

        act.wait_ge(const1_loaded, 16 * N_CONST1)
        act.sem_inc(kT1_stored, 3)
        act.sem_inc(qT1_stored, 1)
        nc.scalar.activation(null_row[:, :], null_row[:, :], ACT.Square, accum_out=null_ss[:, :]).then_inc(null_norm, 1)
        act.wait_ge(null_norm, 1)
        nc.scalar.activation(null_ss[:, :], null_ss[:, :], ACT.Sqrt).then_inc(null_norm, 1)
        with act.Fori(0, B // 2) as i:
            for p in range(2):
                b = 2 * i + p
                for k in range(2):
                    act.wait_ge(ln_stats, 2 * B + 2 * b + k + 1)
                    nc.scalar.activation(std[:, 0:1], mv[:, 0, 1:2], ACT.Sqrt, bias=eps_col[0:NQ, :]).then_inc(ln_std, 1)
                act.wait_ge(k1_in_psum, b + 1)
                nc.scalar.activation(k_tok_full, k1_ps[:, 0:FULL, :], ACT.Square).then_inc(k1_squared, 1)
                nc.scalar.activation(k_tok[FULL][0:TAIL, :], k1_ps[0:TAIL, FULL, :], ACT.Square).then_inc(k1_squared, 1)
                take_ctx1(act, CTX0 + b + 2, 1 - p)
                keep_v(b, 0)
                act.wait_ge(k1_ss, 2 * b + 2)
                nc.scalar.activation(key_ss[:, :, :], key_ss[:, :, :], ACT.Sqrt).then_inc(k1_norm, 1)
                act.wait_ge(q1_in_psum, b + 1)
                nc.scalar.activation(o_tok[:, :], q1_ps[0:NQ, :], ACT.Square).then_inc(q1_squared, 1)
                keep_v(b, 1)
                act.wait_ge(q1_ss, b + 1)
                nc.scalar.activation(q_ss[:, :], q_ss[:, :], ACT.Sqrt).then_inc(q1_norm, 1)
                keep_v(b, 2)
                for t in range(3):
                    act.wait_ge(kT1_in_psum, 3 * b + t + 1)
                    nc.scalar.activation(A1.kT[:, :, bass.ds(b * A1.nk + t * P, rows[t])],
                                         k1_ps[:, t, :].rearrange("p (c n) -> p c n", c=4)[:, :, 0:rows[t]], ACT.Copy
                                         ).then_inc(kT1_stored, 1)
                act.wait_ge(qT1_in_psum, b + 1)
                nc.scalar.activation(A1.qT[:, :, bass.ds(b * NQ, NQ)],
                                     q1_ps[:, 0:4 * NQ].rearrange("p (c n) -> p c n", c=4), ACT.Copy).then_inc(qT1_stored, 1)

    def a1_prepare(dve):
        dve.wait_ge(mask_null, 3)
    A1.prepare = a1_prepare
    A1.clipped = A1.max_ready

    def a1_masked_max(dve, j, n, b):
        k = j % NPB
        p = (j // A1.ppb) % 2
        dve.wait_ge(A1.scores_ready, n + 1)
        dve.wait_ge(A1.transposed, n + 1)
        if j % A1.ppb == 0:
            dve.wait_ge(mask_ready, b + 1)
        nc.vector.memset(turn[:, k:k + 1], 0.0)
        for hh in range(2):
            last = nc.vector.tensor_tensor_reduce(
                out=probs[:, k, hh, 0:A1.nk], in0=score_ps[j % 2][0:NQ, hh, 0:A1.nk], in1=mask_bias[p],
                op0=ALU.add, op1=ALU.min, scale=1.0, scalar=FLT_MAX, accum_out=negmax[:, k, hh:hh + 1])
        last.then_inc(A1.max_ready, 1)
    A1.masked_max = a1_masked_max

    def a1_take(dve, b):
        dve.wait_ge(A1.projected, b + 1)
        nc.vector.tensor_reduce(top_out[:, :], y_ps[0:NQ, 0:D], AX.X, ALU.max).then_inc(take_step, 1)
        dve.wait_ge(take_step, 2 * b + 1)
        nc.vector.reciprocal(top_out[:, :], top_out[:, :]).then_inc(take_step, 1)
        dve.wait_ge(take_step, 2 * b + 2)
        nc.vector.tensor_scalar(z_all[:, b, :], y_ps[0:NQ, 0:D], top_out[:, 0:1], None, ALU.mult).then_inc(A1.added, 1)
        dve.wait_ge(A1.added, b + 1)
        nc.vector.bn_stats(stats[:, b, :], z_all[:, b, :]).then_inc(A1.stats_ready, 1)
    A1.take = a1_take

    HALVES = [range(0, B // 2), range(B // 2, B)]
    N_STD1 = 3 + 2 * B

    def centre1(b):
        mark(nc.vector.scalar_tensor_tensor(z_all[:, b + 1, :], z_all[:, b + 1, :], mv[:, b, 0:1], g_out[:, :],
                                            ALU.subtract, ALU.mult))

    def add1(b):
        mark(nc.vector.scalar_tensor_tensor(x[:, b + 1, :], z_all[:, b + 1, :], rstd[:, b:b + 1], x[:, b + 1, :],
                                            ALU.mult, ALU.add))

    def x_stats1(b):
        mark(nc.vector.bn_stats(stats[:, b + 1, :], x[:, b + 1, :]))

    def x_aggregate1(half):
        for b in half:
            nc.vector.bn_aggr(mv[:, b, :], stats[:, b + 1, :]).then_inc(ln_stats, 1)

    def dve_before_last1(dve):
        dve.wait_ge(A1.stats_ready, B)
        for b in range(B - 1):
            nc.vector.bn_aggr(mv[:, b, :], stats[:, b + 1, :]).then_inc(ln_stats, 1)
        dve.wait_ge(ln_stats, 5 * B - 1)
        for b in HALVES[0]:
            centre1(b)
    A1.before_last = dve_before_last1

    def dve_while_projecting1(dve):
        for b in range(B // 2, B - 1):
            centre1(b)
        dve.wait_ge(ln_std, N_STD1 + 1)
        mark(nc.vector.reciprocal(rstd[:, 0:B - 1], std[:, 0:B - 1]))
        marked(dve)
        for b in range(B - 1):
            add1(b)
    A1.while_projecting = dve_while_projecting1

    def act_std_before_last1(act):
        act.wait_ge(ln_stats, 5 * B - 1)
        nc.scalar.activation(std[:, 0:B - 1], mv[:, 0:B - 1, 1], ACT.Sqrt, bias=eps_col[0:NQ, :]).then_inc(ln_std, 1)
    A1.std_before_last = act_std_before_last1

    def dve_add1(dve):
        dve.wait_ge(A1.stats_ready, B + 1)
        nc.vector.bn_aggr(mv[:, B - 1, :], stats[:, B, :]).then_inc(ln_stats, 1)
        marked(dve)
        for b in HALVES[0]:
            x_stats1(b)
        dve.wait_ge(ln_stats, 5 * B)
        centre1(B - 1)
        marked(dve)
        dve.wait_ge(ln_std, N_STD1 + 2)
        x_aggregate1(HALVES[0])
        step(dve, nc.vector.reciprocal(rstd[:, B - 1:B], std[:, B - 1:B]))
        add1(B - 1)
        marked(dve)
        for b in HALVES[1]:
            x_stats1(b)
        marked(dve)
        x_aggregate1(HALVES[1])
        for k, half in enumerate(HALVES):
            dve.wait_ge(ln_std, N_STD1 + 3 + k)
            cols = slice(half[0], half[-1] + 1)
            step(dve, nc.vector.reciprocal(rstd[:, cols], std[:, cols]))
            for b in half:
                nc.vector.tensor_scalar(z_all[:, b + 1, :], x[:, b + 1, :], mv[:, b, 0:1], rstd[:, b:b + 1], ALU.subtract,
                                        ALU.mult).then_inc(xn_ready, 1)

    def act_add1(act):
        act.wait_ge(ln_stats, 5 * B)
        nc.scalar.activation(std[:, B - 1:B], mv[:, B - 1:B, 1], ACT.Sqrt, bias=eps_col[0:NQ, :]).then_inc(ln_std, 1)
        for k in range(2):
            cols = slice(k * B // 2, (k + 1) * B // 2)
            act.wait_ge(ln_stats, 5 * B + (k + 1) * B // 2)
            nc.scalar.activation(std[:, cols], mv[:, cols, 1], ACT.Sqrt, bias=eps_col[0:NQ, :]).then_inc(ln_std, 1)


    gu_ps = [psum[:, k, 0:HT] for k in range(4)]
    yT_ps = [psum[:, 4 + k, 0:HT] for k in range(4)]
    coefT_ps = [psum[0:E1, 5, 0:5 * NQ], psum[0:E1, 6, 0:(B - 5) * NQ]]
    r_logits_ps = psum[0:NQ, 4, :].rearrange("q (b e) -> q b e", b=B)
    r_wT_ps = psum[:, 6, 0:2 * E1].rearrange("p (c e) -> p c e", c=2)
    r_count_ps = psum[0:E1, 7, 0:1]
    r_before_ps = psum[0:E1, 7, 8:9]
    r_total_ps = psum[0:E1, 7, 16:17]
    r_list_ps = psum[0:1, 7, 64:64 + E1]
    sh_y_ps = [psum[0:NQ, k, :].rearrange("q (b d) -> q b d", b=2) for k in range(4)]

    def pool_consts_ffn1(pool):
        nc.gpsimd.iota(iota64[:, :], [[1, E1]], base=0, channel_multiplier=0, allow_small_or_imprecise_dtypes=True
                       ).then_inc(consts_ready, 1)
        nc.gpsimd.iota(e_col[:, :], [[1, 1]], base=0, channel_multiplier=1, allow_small_or_imprecise_dtypes=True
                       ).then_inc(consts_ready, 1)

    def sp_load_ffn1(sp):
        for p in range(2):
            sp.wait_ge(A1.vs_loaded[p], 32 * (B // 2))
        sp.dma_start(router_rows, a["L1_ffn_router_w"]).then_inc(router_loaded, 16)
        sp.dma_start(e_bias[:, :], a["L1_ffn_e_bias"].rearrange("(o e) -> o e", o=1).broadcast_to([NQ, E1])
                     ).then_inc(router_loaded, 16)
        for dst, name in ((swg, "SWg"), (swu, "SWu"), (swd, "SWd")):
            sp.dma_start(dst, a["L1_ffn_" + name].rearrange("(c p) n -> p c n", p=P)).then_inc(sh_loaded, 16)

    def sp_experts1(sp):
        def load(i, p):
            n = 2 * i + p
            e = sp.value_load(expert_list[0:1, bass.ds(n, 1)], min_val=0, max_val=E1 - 1)
            sp.wait_ge(we_split, 4 * i + p + 3)
            for at, name in ((0, "Wg"), (2 * H1, "Wu")):
                sp.dma_start(we[p][:, at:at + 2 * H1].rearrange("q (c h) -> q c h", c=2),
                             a["L1_ffn_" + name].rearrange("e (c q) h -> q (e c) h", q=P)[
                                 :, bass.ds(2 * e, 2), :]).then_inc(we_loaded[p], 16)
            sp.dma_start(we[p][:, WGU:WALL], a["L1_ffn_Wd"].rearrange("e q d -> (e q) d")[
                bass.ds(e * H1, H1), :]).then_inc(we_loaded[p], 16)

        def load_coef(i, p):
            e = sp.value_load(expert_list[0:1, bass.ds(2 * i + p, 1)], min_val=0, max_val=E1 - 1)
            sp.wait_ge(coef_used, 4 * i + 2 * p + 2)
            sp.dma_start(coef_rows[p], coefT_dram[bass.ds(e, 1), :].broadcast_to([P, B * NQ])
                         ).then_inc(coef_loaded[p], 16)

        sp.wait_ge(route_step, 4)
        total = sp.value_load(n_used[0:1, 0:1], min_val=0, max_val=E1)
        load(0, 0)
        with sp.Fori(0, E1 // (2 * PAIRS)) as o:
            with sp.If(2 * PAIRS * o < total):
                with sp.Fori(0, PAIRS) as k:
                    i = o * PAIRS + k
                    with sp.If(2 * i < total):
                        load(i, 1)
                        sp.wait_ge(coefT_stored, 16)
                        for p in range(2):
                            load_coef(i, p)
                        load(i + 1, 0)

    def pe_gate1(pe):
        pe.wait_ge(router_loaded, 32)
        pe.wait_ge(A1.added, B + 1)
        for c in range(2):
            last = nc.tensor.transpose(r_wT_ps[:, c, :], router_rows[:, c * P:(c + 1) * P], ident[0:E1, 0:E1])
        last.then_inc(r_wT_in_psum, 1)
        pe.wait_ge(r_wT_ready, 1)
        for b in range(B):
            pe.wait_ge(xn_ready, 3 * B + b + 1)
            for c in range(2):
                last = nc.tensor.transpose(xnT_all_ps[b // 2][:, b % 2, c, :], z_all[:, b + 1, c * P:(c + 1) * P],
                                           ident[0:NQ, 0:NQ])
            last.then_inc(xnT_in_psum, 1)
        for b in range(B):
            pe.wait_ge(xnT_ready, 3 * B + 2 * (b // 2) + 2)
            for c in range(2):
                last = nc.tensor.matmul(r_logits_ps[:, b, :], xnT_all[:, c, b * NQ:(b + 1) * NQ], routerT[:, c, :],
                                        start=(c == 0), stop=(c == 1))
            last.then_inc(gate_logits, 1)

    def pe_shared(pe):
        pe.wait_ge(sh_loaded, 48)
        pe.wait_ge(xnT_ready, 4 * B)
        for m in range(2):
            for half in range(2):
                for k, w in enumerate((swg, swu)):
                    if m == 1:
                        pe.wait_ge((sh_g_taken, sh_u_taken)[k], half + 1)
                    for c in range(2):
                        last = nc.tensor.matmul(gu_ps[2 * half + k], w[:, c, m * P:(m + 1) * P],
                                                xnT_all[:, c, half * HT:(half + 1) * HT], start=(c == 0), stop=(c == 1))
                    last.then_inc(sh_in_psum, 1)
        pe.wait_ge(route_step, 1)
        nc.tensor.matmul(r_count_ps, taken[:, :], ones_sq[0:NQ, 0:1], start=True, stop=True).then_inc(route_sums, 1)
        pe.wait_ge(route_step, 2)
        nc.tensor.matmul(r_before_ps, earlier[0:E1, 0:E1], used[:, 0:1], start=True, stop=True)
        nc.tensor.matmul(r_total_ps, ones_sq[0:E1, 0:E1], used[:, 0:1], start=True, stop=True).then_inc(route_sums, 1)
        pe.wait_ge(sh_h_ready, 4)
        for b in range(B):
            for m in range(2):
                last = nc.tensor.matmul(sh_y_ps[b // 2][:, b % 2, :], sh_hT[:, m, b * NQ:(b + 1) * NQ], swd[:, m, :],
                                        start=(m == 0), stop=(m == 1))
            if b % 2 == 1:
                last.then_inc(sh_y_in_psum, 1)
            if b == 0:
                pe.wait_ge(route_step, 3)
                nc.tensor.matmul(r_list_ps, e_col[:, 0:1], place[:, :], start=True, stop=True).then_inc(route_sums, 1)
            if b == 5:
                pe.wait_ge(route_step, 5)
                for bb in range(B):
                    at = bb % 5 * NQ
                    last = nc.tensor.transpose(coefT_ps[bb // 5][:, at:at + NQ], coef[:, bb, :], ident[0:NQ, 0:NQ])
                last.then_inc(route_sums, 1)

    def act_shared(act):
        act.wait_ge(r_wT_in_psum, 1)
        nc.scalar.activation(routerT, r_wT_ps, ACT.Copy).then_inc(r_wT_ready, 1)
        for k in range(B // 2):
            act.wait_ge(xnT_in_psum, 3 * B + 2 * k + 2)
            nc.scalar.activation(xnT_all[:, :, 2 * k * NQ:2 * (k + 1) * NQ].rearrange("p c (b n) -> p b c n", b=2),
                                 xnT_all_ps[k], ACT.Copy).then_inc(xnT_ready, 2)
        act.wait_ge(xnT_ready, 4 * B)
        nc.scalar.activation(xT_high, xnT_all, ACT.Copy).then_inc(x_high_ready, 1)
        act.wait_ge(gate_logits, 2 * B)
        nc.scalar.activation(scores1, r_logits_ps, ACT.Sigmoid).then_inc(r_scores, 1)
        for m in range(2):
            for half in range(2):
                n = 2 * m + half
                if m == 1:
                    act.wait_ge(sh_h_ready, half + 1)
                act.wait_ge(sh_in_psum, 2 * n + 1)
                nc.scalar.activation(sh_g[half], gu_ps[2 * half], ACT.Silu).then_inc(sh_g_taken, 1)
                act.wait_ge(sh_in_psum, 2 * n + 2)
                nc.scalar.activation(sh_u[half], gu_ps[2 * half + 1], ACT.Copy).then_inc(sh_u_taken, 1)
        act.wait_ge(sh_h_ready, 4)
        act.wait_ge(route_sums, 4)
        for k, cols in enumerate((slice(0, 5 * NQ), slice(5 * NQ, B * NQ))):
            nc.scalar.activation(coefT[:, cols], coefT_ps[k], ACT.Copy).then_inc(coefT_taken, 1)
        act.wait_ge(coefT_taken, 2)
        act.dma_start(coefT_dram, coefT).then_inc(coefT_stored, 16)

    def pool_shared(pool):
        pool.wait_ge(x_high_ready, 1)
        nc.gpsimd.tensor_tensor(xT_low, xnT_all, xT_high.bitcast(F32), ALU.subtract).then_inc(x_low_ready, 1)
        for m in range(2):
            for half in range(2):
                n = 2 * m + half
                pool.wait_ge(sh_g_taken, n + 1)
                pool.wait_ge(sh_u_taken, n + 1)
                nc.gpsimd.tensor_tensor(sh_hT[:, m, half * HT:(half + 1) * HT], sh_g[half], sh_u[half], ALU.mult
                                        ).then_inc(sh_h_ready, 1)

    def dve_route1(dve):
        step(dve, nc.vector.memset(expert_list[:, E1:], 0))
        dve.wait_ge(r_scores, 1)
        dve.wait_ge(router_loaded, 32)
        dve.wait_ge(consts_ready, N_CONSTS + N_MOE_CONSTS + 5 + 2)
        step(dve, nc.vector.tensor_tensor(sfc, scores1, e_bias[:, :].unsqueeze(1).broadcast_to([NQ, B, E1]), ALU.add))
        eights = sfc.rearrange("q b (g k) -> q (b g) k", k=G1)
        grid = lambda k, n: group2[:, k, 0:B * G1 * n].rearrange("q (g n) -> q g n", n=n)
        high, low = grid(0, 4), grid(1, 4)
        nc.vector.tensor_tensor(high, eights[:, :, 0:4], eights[:, :, 4:8], ALU.max)
        step(dve, nc.vector.tensor_tensor(low, eights[:, :, 0:4], eights[:, :, 4:8], ALU.min))
        for n, to in ((2, 2), (1, 0)):
            top, second = grid(to, n), grid(to + 1, n)
            below = work1.rearrange("q b e -> q (b e)")[:, 0:B * G1 * n].rearrange("q (g n) -> q g n", n=n)
            nc.vector.tensor_tensor(top, high[:, :, 0:n], high[:, :, n:2 * n], ALU.max)
            nc.vector.tensor_tensor(below, high[:, :, 0:n], high[:, :, n:2 * n], ALU.min)
            step(dve, nc.vector.tensor_tensor(second, low[:, :, 0:n], low[:, :, n:2 * n], ALU.max))
            step(dve, nc.vector.tensor_tensor(second, second, below, ALU.max))
            high, low = top, second
        step(dve, nc.vector.tensor_tensor(group_sum[:, :, :].rearrange("q b (g o) -> q (b g) o", o=1), high, low, ALU.add))
        ij = lambda t: t.rearrange("q b (i j) -> q b i j", j=G1)
        mine = group_sum[:, :, :].unsqueeze(3).broadcast_to([NQ, B, G1, G1])
        other = group_sum[:, :, :].unsqueeze(2).broadcast_to([NQ, B, G1, G1])
        nc.vector.tensor_tensor(ij(work1), other, mine, ALU.is_gt)
        step(dve, nc.vector.tensor_tensor(ij(work2), other, mine, ALU.is_equal))
        step(dve, nc.vector.tensor_tensor(ij(work2), ij(work2),
                                     below8[0:NQ, :, :].unsqueeze(1).broadcast_to([NQ, B, G1, G1]), ALU.mult))
        step(dve, nc.vector.tensor_tensor(work1, work1, work2, ALU.add))
        step(dve, nc.vector.tensor_reduce(group_kept[:, :, :], ij(work1), AX.X, ALU.add))
        step(dve, nc.vector.tensor_scalar(group_kept[:, :, :], group_kept[:, :, :], float(TOPG), None, ALU.is_lt))
        step(dve, nc.vector.tensor_tensor(sfc.rearrange("q b (g k) -> q b g k", k=G1),
                                     sfc.rearrange("q b (g k) -> q b g k", k=G1),
                                     group_kept[:, :, :].unsqueeze(3).broadcast_to([NQ, B, G1, G1]), ALU.mult))
        for b in range(B):
            last = nc.vector.max(top8[:, b, :], sfc[:, b, :])
        step(dve, last)
        for b in range(B):
            last = nc.vector.match_replace(out=picked[:, b, :], in_to_replace=top8[:, b, :], in_values=sfc[:, b, :],
                                           imm_value=-FLT_MAX)
        step(dve, last)
        step(dve, nc.vector.tensor_scalar(picked, picked, -FLT_MAX, None, ALU.is_equal))
        step(dve, nc.vector.tensor_reduce(taken[:, :], picked.rearrange("q b e -> q e b"), AX.X, ALU.add))
        dve.sem_inc(route_step, 1)
        dve.wait_ge(route_sums, 1)
        nc.vector.tensor_scalar(used[:, 0:1], r_count_ps, 0.0, None, ALU.is_gt).then_inc(route_step, 1)
        dve.wait_ge(route_sums, 2)
        step(dve, nc.vector.tensor_scalar(used[:, 2:3], r_total_ps, e_col[:, 0:1], r_before_ps, ALU.add, ALU.subtract))
        step(dve, nc.vector.tensor_tensor(used[:, 1:2], r_before_ps, used[:, 2:3], ALU.subtract))
        step(dve, nc.vector.scalar_tensor_tensor(used[:, 1:2], used[:, 1:2], used[:, 0:1], used[:, 2:3], ALU.mult, ALU.add))
        nc.vector.tensor_copy(n_used[:, :], r_total_ps[0:1, :])
        nc.vector.tensor_scalar(place[:, :], iota64[:, :], used[:, 1:2], None, ALU.is_equal).then_inc(route_step, 1)
        dve.wait_ge(route_sums, 3)
        nc.vector.tensor_copy(expert_list[:, 0:E1], r_list_ps).then_inc(route_step, 1)
        step(dve, nc.vector.tensor_tensor(work1, scores1, picked, ALU.mult))
        step(dve, nc.vector.tensor_reduce(weight_sum[:, :], work1, AX.X, ALU.add))
        step(dve, nc.vector.tensor_scalar(weight_sum[:, :], weight_sum[:, :], 1e-20, None, ALU.add))
        step(dve, nc.vector.reciprocal(weight_sum[:, :], weight_sum[:, :]))
        nc.vector.scalar_tensor_tensor(coef, work1, SCALE2, weight_sum[:, :].unsqueeze(2).broadcast_to([NQ, B, E1]),
                                       ALU.mult, ALU.mult).then_inc(route_step, 1)

    def pe_experts1(pe):
        pe.wait_ge(route_step, 4)
        pe.wait_ge(sh_added, 4)
        pe.wait_ge(x_low_ready, 1)
        pe.wait_ge(coefT_taken, 2)
        for k in range(4):
            nc.tensor.matmul(yT_ps[k], zeros[:, 0:P], xnT_all[:, 0, k // 2 * HT:(k // 2 + 1) * HT], start=True, stop=False)
        pe.sem_inc(gu_in_psum, 8)
        pe.sem_inc(y1_in_psum, 8)

        def gate_up(i, p):
            n = 2 * i + p
            pe.wait_ge(we_split, 4 * i + p + 1 + 4)
            for half in range(2):
                tok = slice(half * HT, (half + 1) * HT)
                pe.wait_ge(h1_full, 2 * n + half + 1)
                for k in range(2):
                    for c in range(2):
                        col = slice((2 * k + c) * H1, (2 * k + c + 1) * H1)
                        ps = gu_ps[2 * half + k]
                        nc.tensor.matmul(ps, we_high[p][:, col], xT_high[:, c, tok], start=(c == 0), stop=False)
                        nc.tensor.matmul(ps, we_high[p][:, col], xT_low[:, c, tok], start=False, stop=False)
                        last = nc.tensor.matmul(ps, we_low[p][:, col], xT_high[:, c, tok], start=False, stop=(c == 1))
                    last.then_inc(gu_in_psum, 1)

        def down(i, p):
            n = 2 * i + p
            pe.wait_ge(we_split, 4 * i + 2 + p + 1 + 4)
            for half in range(2):
                pe.wait_ge(h1_ready, 2 * n + half + 1 + 2)
                tok = slice(half * HT, (half + 1) * HT)
                for c in range(2):
                    col = slice(WGU + c * P, WGU + (c + 1) * P)
                    ps = yT_ps[2 * half + c]
                    nc.tensor.matmul(ps, we_low[p][:, col], h1_high[p][:, tok], start=False, stop=False)
                    nc.tensor.matmul(ps, we_high[p][:, col], h1_high[p][:, tok], start=False, stop=False)
                    last = nc.tensor.matmul(ps, we_high[p][:, col], h1_low[p][:, tok], start=False, stop=False)
            last.then_inc(y1_in_psum, 4)

        total = pe.value_load(n_used[0:1, 0:1], min_val=0, max_val=E1)
        with pe.Fori(0, E1 // (2 * PAIRS)) as o:
            with pe.If(2 * PAIRS * o < total):
                with pe.Fori(0, PAIRS) as k:
                    i = o * PAIRS + k
                    with pe.If(2 * i < total):
                        for p in range(2):
                            gate_up(i, p)
                        for p in range(2):
                            down(i, p)
        for k in range(4):
            nc.tensor.matmul(yT_ps[k][:, 0:1], zeros[:, 0:P], zeros[:, 0:1], start=False, stop=True
                             ).then_inc(experts_done, 1)
        for b in range(B):
            if b % (B // 2) == 0:
                pe.wait_ge(yT_taken, 2 * (b // (B // 2)) + 2)
            for c in range(2):
                last = nc.tensor.transpose(sh_y_ps[b // 2][:, b % 2, c * P:(c + 1) * P], sh_hT[:, c, b * NQ:(b + 1) * NQ],
                                           ident[:, :])
            if b % 2 == 1:
                last.then_inc(out_in_psum, 1)

    def act_experts1(act):
        def split_gate_up(i, p):
            act.wait_ge(we_loaded[p], 48 * i + 48)
            act.wait_ge(gu_in_psum, 4 * (2 * i + p) + 4)
            nc.scalar.activation(we_high[p][:, 0:WGU], we[p][:, 0:WGU], ACT.Copy).then_inc(we_high_ready, 1)

        def split_down(i, p):
            act.wait_ge(y1_in_psum, 4 * (2 * i + p) + 4)
            nc.scalar.activation(we_high[p][:, WGU:WALL], we[p][:, WGU:WALL], ACT.Copy).then_inc(we_high_ready, 1)

        def hidden(i, p):
            n = 2 * i + p
            for half in range(2):
                act.wait_ge(gu_in_psum, 4 * n + 2 * half + 1 + 8)
                act.wait_ge(h1_full, 2 * n + half + 1)
                nc.scalar.activation(g_act[half], gu_ps[2 * half], ACT.Silu).then_inc(silu_done, 1)
            for half in range(2):
                act.wait_ge(h1_full, 2 * n + half + 1 + 2)
                tok = slice(half * HT, (half + 1) * HT)
                nc.scalar.activation(h1_high[p][:, tok], h1T[:, tok], ACT.Copy).then_inc(h1_high_ready, 1)

        act.wait_ge(route_step, 4)
        split_gate_up(0, 0)
        total = act.value_load(n_used[0:1, 0:1], min_val=0, max_val=E1)
        with act.Fori(0, E1 // (2 * PAIRS)) as o:
            with act.If(2 * PAIRS * o < total):
                with act.Fori(0, PAIRS) as k:
                    i = o * PAIRS + k
                    with act.If(2 * i < total):
                        split_gate_up(i, 1)
                        for p in range(2):
                            split_down(i, p)
                        hidden(i, 0)
                        split_gate_up(i + 1, 0)
                        hidden(i, 1)
        for half in range(2):
            for c in range(2):
                act.wait_ge(experts_done, 2 * half + c + 1)
                nc.scalar.activation(sh_hT[:, c, half * HT:(half + 1) * HT], yT_ps[2 * half + c], ACT.Copy
                                     ).then_inc(yT_taken, 1)

    def pool_experts1(pool):
        def split(i, p, part, cols):
            pool.wait_ge(we_high_ready, 4 * i + 2 * part + p + 1)
            nc.gpsimd.tensor_tensor(we_low[p][:, cols], we[p][:, cols], we_high[p][:, cols].bitcast(F32), ALU.subtract
                                    ).then_inc(we_split, 1)

        def hidden(i, p):
            n = 2 * i + p
            for half in range(2):
                tok = slice(half * HT, (half + 1) * HT)
                pool.wait_ge(h1_high_ready, 2 * n + half + 1)
                pool.wait_ge(y1_in_psum, 4 * n + 4)
                nc.gpsimd.tensor_tensor(h1_low[p][:, tok], h1T[:, tok], h1_high[p][:, tok].bitcast(F32), ALU.subtract
                                        ).then_inc(h1_ready, 1)

        pool.wait_ge(route_step, 4)
        pool.sem_inc(we_split, 4)
        pool.sem_inc(h1_ready, 2)
        split(0, 0, 0, slice(0, WGU))
        total = pool.value_load(n_used[0:1, 0:1], min_val=0, max_val=E1)
        with pool.Fori(0, E1 // (2 * PAIRS)) as o:
            with pool.If(2 * PAIRS * o < total):
                with pool.Fori(0, PAIRS) as k:
                    i = o * PAIRS + k
                    with pool.If(2 * i < total):
                        split(i, 1, 0, slice(0, WGU))
                        for p in range(2):
                            split(i, p, 1, slice(WGU, WALL))
                        hidden(i, 0)
                        split(i + 1, 0, 0, slice(0, WGU))
                        hidden(i, 1)

    def dve_experts1(dve):
        def hidden(i, p):
            n = 2 * i + p
            for half in range(2):
                dve.wait_ge(coef_loaded[p], 16 * i + 16)
                dve.wait_ge(silu_done, 2 * n + half + 1)
                nc.vector.tensor_tensor(g_act[half], g_act[half], coef_rows[p][:, half * HT:(half + 1) * HT], ALU.mult
                                        ).then_inc(coef_used, 1)
                dve.wait_ge(coef_used, 2 * n + half + 1 + 4)
                dve.wait_ge(gu_in_psum, 4 * n + 2 * half + 2 + 8)
                dve.wait_ge(h1_ready, 2 * n + half + 1)
                nc.vector.tensor_tensor(h1T[:, half * HT:(half + 1) * HT], g_act[half], gu_ps[2 * half + 1], ALU.mult
                                        ).then_inc(h1_full, 1)

        for k in range(4):
            dve.wait_ge(sh_y_in_psum, k + 1)
            two = x[:, 2 * k + 1:2 * k + 3, :]
            nc.vector.tensor_tensor(two, two, sh_y_ps[k], ALU.add).then_inc(sh_added, 1)
        dve.wait_ge(sh_added, 4)
        dve.wait_ge(route_step, 4)
        dve.sem_inc(h1_full, 2)
        dve.sem_inc(coef_used, 4)
        total = dve.value_load(n_used[0:1, 0:1], min_val=0, max_val=E1)
        with dve.Fori(0, E1 // (2 * PAIRS)) as o:
            with dve.If(2 * PAIRS * o < total):
                with dve.Fori(0, PAIRS) as k:
                    i = o * PAIRS + k
                    with dve.If(2 * i < total):
                        for p in range(2):
                            hidden(i, p)
        for k in range(4):
            dve.wait_ge(out_in_psum, k + 1)
            two = x[:, 2 * k + 1:2 * k + 3, :]
            nc.vector.tensor_tensor(two, two, sh_y_ps[k], ALU.add).then_inc(x_final, 1)

    with nc.Block() as block:
        @block.sync
        def _(sp):
            sp_load0(sp)
            sp_project0(sp)
            sp_load1(sp)

            def v0_ready(e):
                e.wait_ge(v_stored, 2 * B)
                e.wait_ge(consts_ready, N_CONSTS)
            sp_attend(sp, A0, v0_ready)
            sp_load_moe(sp)
            sp_load1_weights(sp)
            sp_experts(sp)
            sp_project1(sp)

            def v1_ready(e):
                e.wait_ge(v1_stored, 3 * B)
                e.wait_ge(null_v_stored, 16 * 8)
                e.wait_ge(ctxT_split, B + 1)
            sp_attend(sp, A1, v1_ready)
            sp_load_ffn1(sp)
            sp_experts1(sp)
            for k in range(2):
                sp.wait_ge(x_final, 2 * k + 2)
                half = slice(k * B // 2, (k + 1) * B // 2)
                sp.dma_start(a["out"][half].rearrange("b q d -> q b d"), x[:, 1 + half.start:1 + half.stop, :]
                             ).then_inc(out_stored, 16)
            sp.wait_ge(out_stored, 32)

        @block.gpsimd
        def _(pool):
            pool_consts(pool)

            def q0_ready(e):
                e.wait_ge(q_stored, 2 * B)
                e.wait_ge(consts_ready, N_CONSTS)
            pool_consts_moe(pool)
            pool_consts1(pool)
            pool_consts_ffn1(pool)
            pool_attend(pool, A0, q0_ready, headmask[:, :])
            pool_dispatch(pool)
            split_ctx1(pool, CTX0 + 1, 0)
            pool_split_weights1(pool)
            pool_project1(pool)
            pool_clear1(pool)
            pool_mask_clear(pool)

            def q1_ready(e):
                e.wait_ge(qT1_stored, B + 1)
                e.wait_ge(kT1_in_psum, 3 * B)
                e.wait_ge(kq1_cleared, 2)
            pool_attend(pool, A1, q1_ready, halfmask[:, :])
            pool_shared(pool)
            pool_experts1(pool)

        @block.vector
        def _(dve):
            dve_project0(dve)
            dve_attend(dve, A0)
            dve_gate(dve)
            dve_experts(dve)
            dve_project1(dve)
            dve_attend(dve, A1)
            dve_add1(dve)
            dve_route1(dve)
            dve_experts1(dve)

        @block.scalar
        def _(act):
            act_project0(act)
            act_attend(act, A0)
            act_gate(act)
            act_split_weights1(act)
            act_experts(act)
            act_project1(act)
            act_attend(act, A1)
            act_add1(act)
            act_shared(act)
            act_experts1(act)

        @block.tensor
        def _(pe):
            pe_project0(pe)

            def p0_ready(e):
                e.wait_ge(q_stored, 2 * B)
                e.wait_ge(k_stored, 2 * B)
                e.wait_ge(v_stored, 2 * B)
                e.wait_ge(A0.out_cleared, 1)
                e.wait_ge(wo0_loaded, 32)
            pe_attend(pe, A0, p0_ready)
            pe_gate(pe)
            pe_experts(pe)
            pe_project1(pe)

            def p1_ready(e):
                e.wait_ge(qT1_stored, B + 1)
                e.wait_ge(kT1_stored, 3 * B + 3)
                e.wait_ge(v1_stored, 3 * B)
                e.wait_ge(null_k_stored, 1)
                e.wait_ge(ctxT_split, B + 1)
                e.wait_ge(kq1_cleared, 2)
            pe_attend(pe, A1, p1_ready)
            pe_gate1(pe)
            pe_shared(pe)
            pe_experts1(pe)


_INS = ["x", "ctx_768", "mask_BxS2_bf1", "L0_xattn_Wq", "L0_xattn_bq", "L0_xattn_Wk", "L0_xattn_bk", "L0_xattn_Wv",
        "L0_xattn_bv", "L0_xattn_Wo", "L0_xattn_bo", "L0_ffn_Wg", "L0_ffn_bg", "L0_ffn_W1", "L0_ffn_b1", "L0_ffn_W2",
        "L0_ffn_b2", "L1_xattn_g_norm", "L1_xattn_Wq", "L1_xattn_Wkv", "L1_xattn_null_kv", "L1_xattn_q_scale",
        "L1_xattn_k_scale", "L1_xattn_Wo", "L1_xattn_g_out", "L1_ffn_router_w", "L1_ffn_e_bias", "L1_ffn_Wg",
        "L1_ffn_Wu", "L1_ffn_Wd", "L1_ffn_SWg", "L1_ffn_SWu", "L1_ffn_SWd"]


def kernel(**inputs):
    import concourse.bacc as _bacc
    from concourse.bass_utils import run_bass_kernel_spmd as _run

    nc = _bacc.Bacc("TRN2", target_bir_lowering=False, num_devices=1)
    arrays, aps = {}, {}
    for name in _INS:
        array = np.ascontiguousarray(inputs[name])
        if array.dtype == np.bool_:
            array = array.view(np.uint8)
        arrays[f"in_{name}_dram"] = array
        aps[name] = nc.dram_tensor(f"in_{name}_dram", array.shape, mybir.dt.from_np(array.dtype),
                                   kind="ExternalInput").ap()
    aps["out"] = nc.dram_tensor("out_0_dram", (B, NQ, D), F32, kind="ExternalOutput").ap()
    build(nc, aps)
    r = _run(nc, [arrays], core_ids=[0])
    return r.results[0]["out_0_dram"]
```
